# Optimizing a Trainium2 kernel written in Bass

```python
import numpy as np
import jax
import jax.numpy as jnp

def _softmax(x, axis=-1):
    return jax.nn.softmax(x, axis=axis)

def _gelu(x):
    return jax.nn.gelu(x, approximate=True)

def _silu(x):
    return jax.nn.silu(x)

def _sigmoid(x):
    return jax.nn.sigmoid(x)

def _layernorm(x, axis=-1, eps=1e-05):
    m = jnp.mean(x, axis=axis, keepdims=True)
    v = jnp.var(x, axis=axis, keepdims=True)
    return (x - m) / jnp.sqrt(v + eps)

def _scatter_add(tgt, idx, src, axis=0):
    return tgt.at[idx].add(src)

def _segment_sum(src, seg, n):
    return jax.ops.segment_sum(src, seg, n)
kernel_name = 'mk_seq_preln_d1_jaxref_r2_cf2009'

def setup_inputs(seed: int=0):
    np.random.seed(seed)
    _w = jnp.asarray

    def _L0_attn_setup():
        import jax, jax.numpy as jnp
        import numpy as np
        import math
        NEG_INF = -1e+38

        def wkv_scan(w, u, k, v):
            B, T, C = k.shape

            def step(carry, kv_t):
                a, b, pp = carry
                kt, vt = kv_t
                ww = u + kt
                q = jnp.maximum(pp, ww)
                e1 = jnp.exp(pp - q)
                e2 = jnp.exp(ww - q)
                y = (e1 * a + e2 * vt) / (e1 * b + e2)
                ww2 = pp + w
                q2 = jnp.maximum(ww2, kt)
                e1b = jnp.exp(ww2 - q2)
                e2b = jnp.exp(kt - q2)
                return ((e1b * a + e2b * vt, e1b * b + e2b, q2), y)
            init = (jnp.zeros((B, C), k.dtype), jnp.zeros((B, C), k.dtype), jnp.full((B, C), NEG_INF, k.dtype))
            kT = jnp.swapaxes(k, 0, 1)
            vT = jnp.swapaxes(v, 0, 1)
            _, ys = jax.lax.scan(step, init, (kT, vT))
            return jnp.swapaxes(ys, 0, 1)
        key = jax.random.key(seed)
        B, T, C = (16, 512, 512)
        k1, k2, k3, k4 = jax.random.split(key, 4)
        x = jax.random.normal(k1, (B, T, C), dtype=jnp.float32)
        scale = 0.02
        Wk = jax.random.normal(k2, (C, C), dtype=jnp.float32) * scale
        Wr = jax.random.normal(k3, (C, C), dtype=jnp.float32) * scale
        Wo = jax.random.normal(k4, (C, C), dtype=jnp.float32) * scale
        h = np.arange(C, dtype=np.float64)
        decay_speed = -5.0 + 8.0 * (h / (C - 1)) ** (0.7 + 1.3 * 1)
        zigzag = ((np.arange(C) + 1) % 3 - 1) * 0.5
        time_first = np.ones(C) * math.log(0.3) + zigzag
        return {'x': x, 'Wk': Wk, 'Wr': Wr, 'Wo': Wo, 'time_decay': jnp.asarray(decay_speed, dtype=jnp.float32), 'time_first': jnp.asarray(time_first, dtype=jnp.float32)}
    _L0_attn_in = _L0_attn_setup()

    def _L0_ffn_setup():
        import jax, jax.numpy as jnp
        import numpy as np
        D = 512
        H = 16
        HD = D // H
        L = 64
        E = 8
        B, T = (4, 1024)
        EPS = 1e-06

        def _glorot(k, shape):
            fan_in, fan_out = (shape[-2], shape[-1])
            lim = np.sqrt(6.0 / (fan_in + fan_out)).astype(np.float32)
            return jax.random.uniform(k, shape, jnp.float32, -lim, lim)

        def _rmsnorm(x, gamma):
            return gamma * x * jax.lax.rsqrt(jnp.mean(x * x, axis=-1, keepdims=True) + EPS)
        key = jax.random.key(seed)
        ks = jax.random.split(key, 8)
        return {'x': jax.random.normal(ks[0], (B, T, D), jnp.float32), 'gamma1': jnp.ones((D,), jnp.float32), 'Wq': _glorot(ks[1], (D, D)), 'bq': jnp.zeros((D,), jnp.float32), 'Wdown': _glorot(ks[2], (D, L)), 'bdown': jnp.zeros((L,), jnp.float32), 'Wup': _glorot(ks[3], (L, 2 * D)), 'bup': jnp.zeros((2 * D,), jnp.float32), 'Wo': _glorot(ks[4], (D, D)), 'bo': jnp.zeros((D,), jnp.float32), 'gamma2': jnp.ones((D,), jnp.float32), 'Wg': _glorot(ks[5], (D, E)), 'bg': jnp.zeros((E,), jnp.float32), 'We': _glorot(ks[6], (E, D, D))}
    _L0_ffn_in = _L0_ffn_setup()
    _d = {'L0_attn_x': _L0_attn_in['x'], 'L0_attn_Wk': _L0_attn_in['Wk'], 'L0_attn_Wr': _L0_attn_in['Wr'], 'L0_attn_Wo': _L0_attn_in['Wo'], 'L0_attn_time_decay': _L0_attn_in['time_decay'], 'L0_attn_time_first': _L0_attn_in['time_first'], 'L0_ffn_gamma1': _L0_ffn_in['gamma1'], 'L0_ffn_Wq': _L0_ffn_in['Wq'], 'L0_ffn_bq': _L0_ffn_in['bq'], 'L0_ffn_Wdown': _L0_ffn_in['Wdown'], 'L0_ffn_bdown': _L0_ffn_in['bdown'], 'L0_ffn_Wup': _L0_ffn_in['Wup'], 'L0_ffn_bup': _L0_ffn_in['bup'], 'L0_ffn_Wo': _L0_ffn_in['Wo'], 'L0_ffn_bo': _L0_ffn_in['bo'], 'L0_ffn_gamma2': _L0_ffn_in['gamma2'], 'L0_ffn_Wg': _L0_ffn_in['Wg'], 'L0_ffn_bg': _L0_ffn_in['bg'], 'L0_ffn_We': _L0_ffn_in['We']}
    _x0 = _d['L0_attn_x']
    _d['L0_attn_x'] = jax.random.normal(jax.random.fold_in(jax.random.key(seed), 1), (2, 4096, 512), dtype=_x0.dtype)
    del _x0
    return _d

def reference(L0_attn_x, L0_attn_Wk, L0_attn_Wr, L0_attn_Wo, L0_attn_time_decay, L0_attn_time_first, L0_ffn_gamma1, L0_ffn_Wq, L0_ffn_bq, L0_ffn_Wdown, L0_ffn_bdown, L0_ffn_Wup, L0_ffn_bup, L0_ffn_Wo, L0_ffn_bo, L0_ffn_gamma2, L0_ffn_Wg, L0_ffn_bg, L0_ffn_We):

    def _L0_attn_ref(x, Wk, Wr, Wo, time_decay, time_first):
        import jax, jax.numpy as jnp
        import numpy as np
        import math
        NEG_INF = -1e+38

        def wkv_scan(w, u, k, v):
            B, T, C = k.shape

            def step(carry, kv_t):
                a, b, pp = carry
                kt, vt = kv_t
                ww = u + kt
                q = jnp.maximum(pp, ww)
                e1 = jnp.exp(pp - q)
                e2 = jnp.exp(ww - q)
                y = (e1 * a + e2 * vt) / (e1 * b + e2)
                ww2 = pp + w
                q2 = jnp.maximum(ww2, kt)
                e1b = jnp.exp(ww2 - q2)
                e2b = jnp.exp(kt - q2)
                return ((e1b * a + e2b * vt, e1b * b + e2b, q2), y)
            init = (jnp.zeros((B, C), k.dtype), jnp.zeros((B, C), k.dtype), jnp.full((B, C), NEG_INF, k.dtype))
            kT = jnp.swapaxes(k, 0, 1)
            vT = jnp.swapaxes(v, 0, 1)
            _, ys = jax.lax.scan(step, init, (kT, vT))
            return jnp.swapaxes(ys, 0, 1)
        k = jnp.einsum('btc,hc->bth', x, Wk)
        r = jnp.einsum('btc,hc->bth', x, Wr)
        v = r
        w = -jnp.exp(time_decay)
        y = wkv_scan(w, time_first, k, v)
        out = jax.nn.sigmoid(r) * y
        return jnp.einsum('bth,ch->btc', out, Wo)

    def _L0_ffn_ref(x, gamma1, Wq, bq, Wdown, bdown, Wup, bup, Wo, bo, gamma2, Wg, bg, We):
        import jax, jax.numpy as jnp
        import numpy as np
        D = 512
        H = 16
        HD = D // H
        L = 64
        E = 8
        B, T = (4, 1024)
        EPS = 1e-06

        def _glorot(k, shape):
            fan_in, fan_out = (shape[-2], shape[-1])
            lim = np.sqrt(6.0 / (fan_in + fan_out)).astype(np.float32)
            return jax.random.uniform(k, shape, jnp.float32, -lim, lim)

        def _rmsnorm(x, gamma):
            return gamma * x * jax.lax.rsqrt(jnp.mean(x * x, axis=-1, keepdims=True) + EPS)
        b, t = (x.shape[0], x.shape[1])
        h = _rmsnorm(x, gamma1)
        q = (h @ Wq + bq).reshape(b, t, H, HD)
        kv = ((h @ Wdown + bdown) @ Wup + bup).reshape(b, t, H, 2 * HD)
        k, v = jnp.split(kv, 2, axis=-1)
        att = jnp.einsum('bthd,btgd->bthg', q, k) / np.sqrt(HD).astype(np.float32)
        att = jax.nn.softmax(att, axis=-1)
        out = jnp.einsum('bthg,btgd->bthd', att, v).reshape(b, t, D)
        x = x + (out @ Wo + bo)
        h2 = _rmsnorm(x, gamma2)
        gate = jax.nn.softmax(h2 @ Wg + bg, axis=-1)
        combined = jnp.einsum('btd,edf,bte->btf', h2, We, gate)
        return x + combined
    x = L0_attn_x
    x = x + _L0_attn_ref(_layernorm(x, axis=-1), L0_attn_Wk, L0_attn_Wr, L0_attn_Wo, L0_attn_time_decay, L0_attn_time_first)
    x = x + _L0_ffn_ref(_layernorm(x, axis=-1), L0_ffn_gamma1, L0_ffn_Wq, L0_ffn_bq, L0_ffn_Wdown, L0_ffn_bdown, L0_ffn_Wup, L0_ffn_bup, L0_ffn_Wo, L0_ffn_bo, L0_ffn_gamma2, L0_ffn_Wg, L0_ffn_bg, L0_ffn_We)
    return x

_drawn_inputs = setup_inputs


def setup_inputs(seed=0):
    import zlib

    import numpy as np

    out = dict(_drawn_inputs(seed))
    spreads = {'L0_ffn_gamma1': (1.0, 0.6),
     'L0_ffn_bq': (0.0, 0.8),
     'L0_ffn_bdown': (0.0, 0.8),
     'L0_ffn_bup': (0.0, 0.446),
     'L0_ffn_bo': (0.0, 0.1),
     'L0_ffn_gamma2': (1.0, 0.2),
     'L0_ffn_bg': (0.0, 0.636)}
    factors = {'L0_attn_Wk': 3.459, 'L0_attn_time_first': 200.0}
    for name, (base, spread) in spreads.items():
        noise = np.random.default_rng([zlib.crc32(name.encode()), seed]).standard_normal(out[name].shape)
        drawn = base * np.exp(spread * noise) if base else spread * noise
        out[name] = jnp.asarray(drawn.astype(out[name].dtype))
    for name, factor in factors.items():
        out[name] = (out[name] * factor).astype(out[name].dtype)
    return out
```

```python
from contextlib import ExitStack

import numpy as np

import concourse.bass as bass
from concourse import mybir

P = 128
B, L, C = 2, 4096, 512
T = 256
SUB = T // P
NT = B * L // T
CB = C // P
H, HD = 16, 32
LAT = 64
E = 8
G = 32
NJ = T // G
HF = CB // 2
XS = 2048.0
NEG_INF = -1e38
ZMAX = 87.0
LN_EPS, RMS_EPS = 1e-5, 1e-6
SCAN_ROWS = 3 * HD + NJ

ALU = mybir.AluOpType
ACT = mybir.ActivationFunctionType
AX = mybir.AxisListType.X
F32, F16, I32 = mybir.dt.float32, mybir.dt.float16, mybir.dt.int32
RMAX = bass.bass_isa.ReduceOp.max


class Tile:

    def __init__(self, n, par, chunk):
        self.n, self.par, self.chunk = n, par, chunk

    def back(self, d):
        if isinstance(self.n, int) and self.n < d:
            return None
        return Tile(self.n - d, (self.par - d) % 2, None)


class Steps:

    def __init__(self, sem, unit=1, **counts):
        self.sem, self.unit, self.first, self.total = sem, unit, {}, 0
        for step, count in counts.items():
            self.first[step] = (self.total, count)
            self.total += count

    def done(self, tile, step, k=-1):
        first, count = self.first[step]
        assert k < count
        k = k % count
        return self.sem, tile.n * (self.total * self.unit) + (first + k + 1) * self.unit


BIG = ["k", "r", "o1", "q", "o2"] + [f"e{e}" for e in range(E)]
SMALL = ["d", "g", "u"]
NAMES = BIG + SMALL
IX = {name: n for n, name in enumerate(NAMES)}
NW = len(NAMES)
TURNED = ("k", "r", "o1")

ATT_USES = ([("T", 0), ("T", 1), ("D", 0), ("Q", 0), ("Q", 1), ("K", 0), ("K", 1), ("V", 0), ("V", 1),
             ] + [("M", k) for k in range(8)] + [("S", 0)]
            + [x for k in range(7) for x in (("S", k + 1), ("PV", k))] + [("PV", 7)]
            + [("O", 0), ("O", 1), ("T2", 0), ("T2", 1), ("G", 0)])
ATT_RING = 4
ATT_BANK = {use: n % ATT_RING for n, use in enumerate(ATT_USES)}


def att_before(use):
    n = ATT_USES.index(use)
    for m in range(n - 1, -1, -1):
        if ATT_BANK[ATT_USES[m]] == ATT_BANK[use]:
            return ATT_USES[m], False
    for m in range(len(ATT_USES) - 1, -1, -1):
        if ATT_BANK[ATT_USES[m]] == ATT_BANK[use]:
            return ATT_USES[m], True


ORDER = [
    ("att_norm", 0), ("moe", 0), ("moe", 1), ("mix_norm", 0),
    ("att_turn", 0), ("moe", 2), ("att_latent", 0), ("mix_turn", 0), ("att_up", 0), ("mix_kv", 0),
    ("mix_decay", 0), ("moe", 3), ("moe", 4), ("att_max", 0), ("moe", 5), ("mix_state", 0),
    ("moe", 6), ("moe", 7), ("att_probs", 0), ("moe", 8), ("mix_out", 0), ("mix_decay", 1),
    ("att_back", 0), ("moe", 9), ("moe", 10), ("mix_state", 1), ("moe", 11), ("att_project", 0),
    ("moe", 12), ("moe", 13), ("mix_out", 1), ("att_norm2", 0), ("moe", 14), ("moe", 15),
    ("moe_store", 0), ("att_turn2", 0), ("att_gate", 0), ("mix_project", 0),
]


def build(nc, x, wk, wr, wo1, decay, first, gamma1, wq, bq, wdown, bdown, wup, bup, wo2, bo, gamma2,
          wg, bg, we, ident_in, kmask_in, qmask_in, out):
    with ExitStack() as ctx:
        def sb(name, shape, dt=F32):
            return ctx.enter_context(nc.sbuf_tensor(name, shape, dt))

        def sem(name):
            return ctx.enter_context(nc.semaphore(name))

        ctx.enter_context(nc.allow_non_contiguous_dma(reason="short columns of constants"))
        bank = [ctx.enter_context(nc.psum_tensor(f"bank{n}", [P, 512], F32)) for n in range(8)]
        moe_bank, mix_bank, att_bank = bank[0:2], bank[2:4], bank[4:8]

        w16 = {name: sb(f"w_{name}", [P, 2, CB, C], F16) for name in BIG}
        w16["d"] = sb("w_d", [P, 2, CB, 2 * LAT], F16)
        w16["g"] = sb("w_g", [P, 2, CB, E], F16)
        w16["u"] = sb("w_u", [P, 2, 2 * C], F16)

        ident = sb("ident", [P, P])
        wcol, ucol = sb("wcol", [P, CB]), sb("ucol", [P, CB])
        gam = sb("gam", [P, 2, CB])
        bqcol, bkcol, bvcol, bdcol = sb("bqcol", [P, CB]), sb("bkcol", [P, CB]), sb("bvcol", [P, CB]), sb("bdcol", [P, 1])
        bqs, bks, bds = sb("bqs", [P, CB]), sb("bks", [P, CB]), sb("bds", [P, 1])
        bo_row, bg_row = sb("bo_row", [P, C]), sb("bg_row", [P, SUB, E])
        mx = sb("mx", [P, NW + 3, CB])
        bound, pw2, inv = sb("bound", [P, NW + 8]), sb("pw2", [P, NW + 4]), sb("inv", [P, NW + 4])
        scl = sb("scl", [P, NW, CB])
        col = sb("col", [P, 24])
        ee = sb("ee", [P, SUB, E])
        half, eps_ln, eps_rms, idle = sb("half", [P, SUB]), sb("eps_ln", [P, SUB]), sb("eps_rms", [P, SUB]), sb("idle", [P, 1])
        ones4 = sb("ones4", [P, CB])
        names = ["k", "v", "o", "o_hi", "c", "q", "kk", "vv", "soft", "ot_hi", "x2", "g", "t0", "t1", "t2", "t3", "t4"]
        colof = {name: col[:, n:n + 1] for n, name in enumerate(names)}

        xk = sb("xk", [P, 1024])
        xk_rows = xk[:, :].rearrange("p (s c) -> p s c", s=SUB)
        k32 = xk[:, :].rearrange("p (b t) -> p b t", b=CB)
        v32 = sb("v32", [P, CB, T])
        xo16 = sb("xo16", [P, 2, CB, T], F16)
        wkv = sb("wkv", [P, 3, HF, T + 1])
        e1, e2, ev, zz = (sb(n, [P, HF, T]) for n in ("e1", "e2", "ev", "zz"))
        carry = [sb(f"carry{b}", [P, 3, CB]) for b in range(B)]
        st1, mv1 = sb("st1", [P, SUB, 6]), sb("mv1", [P, SUB, 2])
        ve1, rs1 = sb("ve1", [P, SUB]), sb("rs1", [P, SUB])
        x1 = [sb(f"x1_{n}", [P, SUB, C]) for n in range(2)]

        x2 = sb("x2", [P, SUB, C])
        hrow = sb("hrow", [P, SUB * C])
        h_rows = hrow[:, :].rearrange("p (s c) -> p s c", s=SUB)
        on = hrow[:, :].rearrange("p (g d) -> p g d", d=HD)
        ht = sb("ht", [P, 1024])
        ht16 = ht[:, :].bitcast(F16).rearrange("p (l b t) -> p l b t", l=2, b=CB)
        ot32 = ht[:, :].rearrange("p (b t) -> p b t", b=CB)
        c32, c16 = sb("c32", [P, T]), sb("c16", [P, T], F16)
        t32 = sb("t32", [P, 2, T])
        qo16 = sb("qo16", [P, 2, CB, T], F16)
        k16 = sb("k16", [P, 2, CB, T], F16)
        va32 = ht[:, :].rearrange("p (b t) -> p b t", b=CB)
        vp = sb("vp", [P, G, HD + 1])
        qs, ks = sb("qs", [P, H, T], F16), sb("ks", [P, H, T], F16)
        pr = sb("pr", [P, 2, 4 * P])
        mcol, m16 = sb("mcol", [P, G]), sb("m16", [P, 2, G], F16)
        rden = sb("rden", [P, G])
        st2, mv2 = sb("st2", [P, SUB, 6]), sb("mv2", [P, SUB, 2])
        sm = sb("sm", [P, 8, SUB])
        msq = sb("msq", [P, SUB])
        gl, gmx, gsum = sb("gl", [P, SUB, E]), sb("gmx", [P, SUB]), sb("gsum", [P, SUB])
        gates = sb("gates", [P, SUB, E])

        h2t = sb("h2t", [P, 2, CB, T], F16)
        acc = sb("acc", [P, SUB, C])

        stage = [b[:, :, :].rearrange("p h t -> p (h t)").bitcast(F32).rearrange("p (b c) -> p b c", b=CB)
                 for b in (qs, ks)]
        d32 = hrow[:, 0:512].rearrange("p (b c) -> p b c", b=CB)
        g32 = hrow[:, 512:512 + CB * E].rearrange("p (b c) -> p b c", b=CB)
        u32 = x2[:, :, :].rearrange("p s c -> p (s c)")

        const_in, smalls_in = sem("const_in"), sem("smalls_in")
        max_in = [sem("max_in0"), sem("max_in1")]
        split_in = [sem("split_in0"), sem("split_in1")]
        masks_in = sem("masks_in")
        set_dve, set_act, set_pool, set_pe = sem("set_dve"), sem("set_act"), sem("set_pool"), sem("set_pe")

        x_in = Steps(sem("x_in"), 16, x=1)
        res_in = Steps(sem("res_in"), 16, x=1)
        stack_in = Steps(sem("stack_in"), 16, qk=24)
        m_in = Steps(sem("m_in"), 16, m=2)
        stored = Steps(sem("stored"), 16, out=1)
        mix_pe = Steps(sem("mix_pe"), T=2, K=2, V=2, O=2)
        mix_act = Steps(sem("mix_act"), x_hi=2, k=2, v=2, e1_0=2, e2_0=1, r_0=1, th_0=1, o_hi_0=1,
                        e1_1=2, e2_1=1, r_1=1, th_1=1, o_hi_1=1)
        wkv_steps = ("carry", 1), ("pp", 2), ("z", 2), ("zc", 1), ("ev", 1), ("a", 2), ("b", 2), ("keep", 1), ("bv", 1), \
            ("num", 1), ("den", 1), ("rec", 1), ("frac", 1), ("y", 1), ("gated", 1), ("o_lo", 1)
        mix_dve = Steps(sem("mix_dve"), stats=2, idle=1, aggr=2, norm=2, x_lo=2,
                        **{f"{s}_{h}": c for h in (0, 1) for s, c in wkv_steps}, x1=2)
        mix_pool = Steps(sem("mix_pool"), eps=1, rstd=1, d1_0=1, d2_0=1, d1_1=1, d2_1=1)
        att_pe = Steps(sem("att_pe"), **{f"{n}{k}": 1 for n, k in ATT_USES})
        att_act = Steps(sem("att_act"), h_hi=2, c=2, q=8, k=8, v=4, ex=8, ot_hi=1, sq=2,
                        h2_hi=2, ge=1)
        att_dve = Steps(sem("att_dve"), stats=2, idle=1, aggr=2, xn=2, h=2, h_lo=2, c_lo=1, q_lo=4, k_lo=4,
                        vt=1, smax=8, m_hi=1, m_lo=1, norm=16, ot=1, ot_lo=1, x2=2, h2=2, h2_lo=2,
                        gl=1, gmax=1, gsub=1, gsum=1, grec=1, gmul=1, gates=1)
        att_pool = Steps(sem("att_pool"), small=7, xb=2, rms=2, acc=2)
        moe_pe = Steps(sem("moe_pe"), u=2 * E)
        moe_dve = Steps(sem("moe_dve"), u=2 * E)

        def mix_reader(use, k):
            return {"T": (mix_dve, "x_lo", k), "K": (mix_act, "k", k), "V": (mix_act, "v", k),
                    "O": (mix_dve, "x1", k)}[use]

        def att_reader(use, k):
            return {"T": (att_dve, "h_lo", k), "D": (att_act, "c", 0), "Q": (att_act, "q", 4 * k + 2),
                    "K": (att_act, "k", 4 * k + 2), "V": (att_act, "v", 2 * k + 1),
                    "M": (att_dve, "smax", k), "S": (att_act, "ex", k), "PV": (att_dve, "norm", 2 * k + 1),
                    "O": (att_dve, "x2", k), "T2": (att_dve, "h2_lo", k),
                    "G": (att_dve, "gl", 0)}[use]

        def pipeline(eng, steps):
            def iteration(i, par, chunk):
                flat = isinstance(i, int)
                tiles = {}
                if not flat or i < NT:
                    tiles["mix"] = Tile(i, par, chunk)
                if not flat or 1 <= i <= NT:
                    tiles["att"] = Tile(i - 1, 1 - par, None)
                if not flat or 2 <= i:
                    tiles["moe"] = Tile(i - 2, par, chunk - 1)
                for name, k in ORDER:
                    stage_name = name.split("_")[0]
                    if name in steps and stage_name in tiles:
                        steps[name](tiles[stage_name], k)

            for i in range(4):
                iteration(i, i % 2, i // 2)
            with eng.Fori(0, (NT - 4) // 2) as pair:
                for par in range(2):
                    iteration(pair * 2 + (4 + par), par, pair + 2)
            for i in range(NT, NT + 2):
                iteration(i, i % 2, i // 2)

        weight_dram = {"k": wk, "r": wr, "o1": wo1, "q": wq, "o2": wo2}
        weight_dram |= {f"e{e}": we[e] for e in range(E)}
        block = ctx.enter_context(nc.Block())

        def rows(dram, tile):
            view = dram[tile.par].rearrange("(n s p) c -> n p s c", s=SUB, p=P)
            if isinstance(tile.chunk, int):
                return view[tile.chunk]
            return view[bass.ds(tile.chunk, 1)].rearrange("n p s c -> (n p) s c")

        @block.sync
        def _(sp):
            sp.dma_start(ident[:, :], ident_in).then_inc(const_in, 16)
            for tile_, dram in ((wcol, decay), (ucol, first), (gam[:, 0, :], gamma1), (gam[:, 1, :], gamma2), (bqcol, bq)):
                sp.dma_start(tile_[:, :], dram.rearrange("(b p) -> p b", p=P)).then_inc(const_in, 16)
            bup_v = bup.rearrange("(b f k d) -> k f d b", f=4, k=2, d=HD)
            for f in range(4):
                sp.dma_start(bkcol[f * HD:(f + 1) * HD, :], bup_v[0, f]).then_inc(const_in, 16)
                sp.dma_start(bvcol[f * HD:(f + 1) * HD, :], bup_v[1, f]).then_inc(const_in, 16)
            for n in range(2):
                sp.dma_start(bdcol[n * LAT:(n + 1) * LAT, :], bdown.rearrange("(p a) -> p a", a=1)).then_inc(const_in, 16)
            sp.dma_start(bo_row[:, :], bo.partition_broadcast(P)).then_inc(const_in, 16)
            for s in range(SUB):
                sp.dma_start(bg_row[:, s, :], bg.partition_broadcast(P)).then_inc(const_in, 16)
            for n in range(2):
                sp.dma_start(d32[:, :, n * LAT:(n + 1) * LAT], wdown.rearrange("(b p) c -> p b c", p=P)).then_inc(smalls_in, 16)
                for k in range(2):
                    sp.dma_start(u32[n * LAT:(n + 1) * LAT, k * C:(k + 1) * C].rearrange("p (g d) -> p g d", g=H),
                                 wup.rearrange("l (g k d) -> k l g d", g=H, k=2)[k]).then_inc(smalls_in, 16)
            sp.dma_start(g32, wg.rearrange("(b p) c -> p b c", p=P)).then_inc(smalls_in, 16)
            for n, name in enumerate(BIG):
                if n >= 2:
                    sp.wait_ge(set_dve, MAX_DONE + n - 2 + 1)
                sp.dma_start(stage[n % 2], weight_dram[name].rearrange("(b p) c -> p b c", p=P)).then_inc(max_in[n % 2], 16)
            for n, name in enumerate(BIG):
                if n < 2:
                    sp.wait_ge(set_dve, MAX_DONE + len(BIG))
                else:
                    sp.wait_ge(set_dve, split_done(n - 2))
                sp.dma_start(stage[n % 2], weight_dram[name].rearrange("(b p) c -> p b c", p=P)).then_inc(split_in[n % 2], 16)
            sp.wait_ge(set_dve, split_done(len(BIG) - 1))
            sp.dma_start(ks[3 * HD:SCAN_ROWS + 2, :, :], kmask_in.rearrange("a (h t) -> a h t", h=H)).then_inc(masks_in, 16)
            sp.dma_start(qs[3 * HD:SCAN_ROWS, :, :], qmask_in.rearrange("a (h t) -> a h t", h=H)).then_inc(masks_in, 16)

            def mix_norm(t, _):
                if t.back(1):
                    sp.wait_ge(*mix_dve.done(t.back(1), "z_1"))
                    sp.wait_ge(*mix_pool.done(t.back(1), "d2_1"))
                sp.dma_start(xk_rows, rows(x, t)).then_inc(x_in.sem, 16)

            def mix_kv(t, _):
                if t.back(2):
                    sp.wait_ge(*att_pool.done(t.back(2), "acc"))
                sp.dma_start(x1[t.par][:, :, :], rows(x, t)).then_inc(res_in.sem, 16)

            def att_up(t, _):
                for src, dst, parts, last in ((qo16, qs, (0, 0, 1), "q_lo"), (k16, ks, (0, 1, 0), "k_lo")):
                    sp.wait_ge(*att_dve.done(t, last))
                    for f in range(4):
                        for n, part in enumerate(parts):
                            sp.dma_start(dst[n * HD:(n + 1) * HD, f * CB:(f + 1) * CB, :],
                                         src[f * HD:(f + 1) * HD, part]).then_inc(stack_in.sem, 16)

            def att_max(t, _):
                sp.wait_ge(*att_dve.done(t, "m_lo"))
                for l in range(2):
                    sp.dma_start(qs[SCAN_ROWS + l:SCAN_ROWS + l + 1, :, :].rearrange("a h (j g) -> a (h j) g", j=NJ), m16[:, l, :])\
                        .then_inc(m_in.sem, 16)

            def moe_store(t, _):
                sp.wait_ge(*moe_dve.done(t, "u"))
                sp.dma_start(rows(out, t), acc[:, :, :]).then_inc(stored.sem, 16)

            pipeline(sp, {"mix_norm": mix_norm, "mix_kv": mix_kv, "att_up": att_up, "att_max": att_max,
                          "moe_store": moe_store})
            sp.wait_ge(*stored.done(Tile(NT - 1, 1, 0), "out"))

        @block.gpsimd
        def _(pool):
            pool.memset(half[:, :], -0.5).then_inc(set_pool, 1)
            pool.memset(eps_ln[:, :], LN_EPS).then_inc(set_pool, 1)
            pool.memset(eps_rms[:, :], RMS_EPS).then_inc(set_pool, 1)
            pool.wait_ge(set_dve, MAXES)
            pool.partition_all_reduce(bound[:, 0:NW + 3], bound[:, 0:NW + 3], P, RMAX).then_inc(set_pool, 1)

            def mix_norm(t, _):
                pool.wait_ge(*mix_dve.done(t, "aggr"))
                nc.gpsimd.tensor_tensor(ve1[:, :], mv1[:, :, 1], eps_ln[:, :], ALU.add).then_inc(mix_pool.sem, 1)
                pool.wait_ge(*mix_pool.done(t, "eps"))
                nc.gpsimd.tensor_tensor(rs1[:, :], ve1[:, :], half[:, :], ALU.pow).then_inc(mix_pool.sem, 1)

            def mix_decay(t, h):
                pool.wait_ge(*mix_dve.done(t, f"pp_{h}"))
                nc.gpsimd.tensor_tensor(e1[:, :, :], wkv[:, 0, :, 0:T], wkv[:, 0, :, 1:T + 1], ALU.subtract).then_inc(mix_pool.sem, 1)
                nc.gpsimd.tensor_tensor(e2[:, :, :], k32[:, HF * h:HF * h + HF, :], wkv[:, 0, :, 1:T + 1], ALU.subtract)\
                    .then_inc(mix_pool.sem, 1)

            def att_norm(t, _):
                pool.wait_ge(*att_dve.done(t, "aggr"))
                nc.gpsimd.tensor_tensor(sm[:, 0, :], mv2[:, :, 1], eps_ln[:, :], ALU.add).then_inc(att_pool.sem, 1)
                pool.wait_ge(*att_pool.done(t, "small", 0))
                nc.gpsimd.tensor_tensor(sm[:, 1, :], sm[:, 0, :], half[:, :], ALU.pow).then_inc(att_pool.sem, 1)
                pool.wait_ge(*att_pool.done(t, "small", 1))
                nc.gpsimd.tensor_tensor(sm[:, 2, :], mv2[:, :, 1], sm[:, 1, :], ALU.mult).then_inc(att_pool.sem, 1)
                pool.wait_ge(*att_pool.done(t, "small", 2))
                nc.gpsimd.tensor_tensor(sm[:, 3, :], sm[:, 2, :], sm[:, 1, :], ALU.mult).then_inc(att_pool.sem, 1)
                pool.wait_ge(*att_pool.done(t, "small", 3))
                nc.gpsimd.tensor_tensor(sm[:, 4, :], sm[:, 3, :], eps_rms[:, :], ALU.add).then_inc(att_pool.sem, 1)
                pool.wait_ge(*att_pool.done(t, "small", 4))
                nc.gpsimd.tensor_tensor(sm[:, 5, :], sm[:, 4, :], half[:, :], ALU.pow).then_inc(att_pool.sem, 1)
                pool.wait_ge(*att_pool.done(t, "small", 5))
                nc.gpsimd.tensor_tensor(sm[:, 6, :], sm[:, 5, :], sm[:, 1, :], ALU.mult).then_inc(att_pool.sem, 1)
                for s in range(SUB):
                    pool.wait_ge(*att_dve.done(t, "xn", s))
                    nc.gpsimd.tensor_tensor(x2[:, s, :], x2[:, s, :], bo_row[:, :], ALU.add).then_inc(att_pool.sem, 1)

            def att_norm2(t, _):
                pool.wait_ge(*att_act.done(t, "sq"))
                nc.gpsimd.tensor_tensor(sm[:, 7, :], msq[:, :], eps_rms[:, :], ALU.add).then_inc(att_pool.sem, 1)
                pool.wait_ge(*att_pool.done(t, "rms", 0))
                nc.gpsimd.tensor_tensor(sm[:, 0, :], sm[:, 7, :], half[:, :], ALU.pow).then_inc(att_pool.sem, 1)

            def att_gate(t, _):
                if t.back(1):
                    pool.wait_ge(*stored.done(t.back(1), "out"))
                for s in range(SUB):
                    nc.gpsimd.tensor_tensor(acc[:, s, :], x1[t.par][:, s, :], x2[:, s, :], ALU.add).then_inc(att_pool.sem, 1)

            pipeline(pool, {"mix_norm": mix_norm, "mix_decay": mix_decay, "att_norm": att_norm,
                            "att_norm2": att_norm2, "att_gate": att_gate})

        @block.scalar
        def _(act):
            act.wait_ge(const_in, 16 * CONSTS)
            nc.scalar.activation(wcol[:, :], wcol[:, :], ACT.Exp).then_inc(set_act, 1)
            act.wait_ge(set_dve, SCALES)
            for n, name in enumerate(BIG):
                act.wait_ge(split_in[n % 2], 16 * (n // 2 + 1))
                for b in range(CB):
                    if name in TURNED:
                        use = n * CB + b
                        act.wait_ge(set_pe, use + 1)
                        src = bank[use % 2][:, :]
                    else:
                        src = stage[n % 2][:, b, :]
                    nc.scalar.activation(w16[name][:, 0, b, :], src, ACT.Copy, scale=scl[:, n, b:b + 1]).then_inc(set_act, 1)
            for name, src in (("d", d32), ("g", g32)):
                for b in range(CB):
                    nc.scalar.activation(w16[name][:, 0, b, :], src[:, b, :], ACT.Copy, scale=scl[:, IX[name], b:b + 1]).then_inc(set_act, 1)
            nc.scalar.activation(w16["u"][:, 0, :], u32, ACT.Copy, scale=scl[:, IX["u"], 0:1]).then_inc(set_act, 1)
            act.wait_ge(set_dve, SET_DVE)

            def mix_turn(t, _):
                for b in range(2):
                    act.wait_ge(*mix_pe.done(t, "T", b))
                    if b == 0 and t.back(1):
                        act.wait_ge(*mix_pe.done(t.back(1), "O"))
                    nc.scalar.activation(xo16[:, 0, 2 * b:2 * b + 2, :], mix_bank[b][:, :], ACT.Copy, scale=XS)\
                        .then_inc(mix_act.sem, 1)

            def mix_kv(t, _):
                for b in range(2):
                    act.wait_ge(*mix_pe.done(t, "K", b))
                    nc.scalar.activation(k32[:, 2 * b:2 * b + 2, :], mix_bank[b][:, :], ACT.Copy, scale=colof["k"])\
                        .then_inc(mix_act.sem, 1)
                for b in range(2):
                    act.wait_ge(*mix_pe.done(t, "V", b))
                    nc.scalar.activation(v32[:, 2 * b:2 * b + 2, :], mix_bank[b][:, :], ACT.Copy, scale=colof["v"])\
                        .then_inc(mix_act.sem, 1)

            def mix_decay(t, h):
                act.wait_ge(*mix_pool.done(t, f"d1_{h}"))
                for c in range(HF):
                    nc.scalar.activation(e1[:, c, :], e1[:, c, :], ACT.Exp, bias=wcol[:, HF * h + c:HF * h + c + 1])\
                        .then_inc(mix_act.sem, 1)
                act.wait_ge(*mix_pool.done(t, f"d2_{h}"))
                nc.scalar.activation(e2[:, :, :], e2[:, :, :], ACT.Exp).then_inc(mix_act.sem, 1)

            def mix_state(t, h):
                act.wait_ge(*mix_dve.done(t, f"zc_{h}"))
                nc.scalar.activation(zz[:, :, :], zz[:, :, :], ACT.Exp).then_inc(mix_act.sem, 1)
                act.wait_ge(*mix_dve.done(t, f"b_{h}"))
                nc.scalar.activation(e1[:, :, :], v32[:, HF * h:HF * h + HF, :], ACT.Tanh, scale=0.5).then_inc(mix_act.sem, 1)

            def mix_out(t, h):
                act.wait_ge(*mix_dve.done(t, f"gated_{h}"))
                nc.scalar.activation(xo16[:, 0, HF * h:HF * h + HF, :], e2[:, :, :], ACT.Copy, scale=colof["o_hi"])\
                    .then_inc(mix_act.sem, 1)

            def att_turn(t, _):
                for b in range(2):
                    act.wait_ge(*att_pe.done(t, f"T{b}"))
                    nc.scalar.activation(ht16[:, 0, 2 * b:2 * b + 2, :], att_bank[ATT_BANK["T", b]][:, :], ACT.Copy, scale=XS)\
                        .then_inc(att_act.sem, 1)

            def att_latent(t, _):
                act.wait_ge(*att_pe.done(t, "D0"))
                nc.scalar.activation(c32[:, :], att_bank[ATT_BANK["D", 0]][:, 0:T], ACT.Identity, bias=bds[:, 0:1], scale=colof["c"])\
                    .then_inc(att_act.sem, 1)
                act.wait_ge(*att_act.done(t, "c", 0))
                nc.scalar.activation(c16[:, :], c32[:, :], ACT.Copy).then_inc(att_act.sem, 1)
                heads(t, "Q", "q", qo16, colof["q"], bqs, "q_lo", None)

            def heads(t, use, step, dst, scale, bias, lo, before):
                for b in range(CB):
                    act.wait_ge(*att_pe.done(t, f"{use}{b // 2}"))
                    if b >= 2:
                        act.wait_ge(*att_dve.done(t, lo, b - 2))
                    elif before:
                        act.wait_ge(*att_dve.done(t, before, b + 2))
                    nc.scalar.activation(t32[:, b % 2, :], att_bank[ATT_BANK[use, b // 2]][:, (b % 2) * T:(b % 2) * T + T],
                                         ACT.Identity, bias=bias[:, b:b + 1], scale=scale).then_inc(att_act.sem, 1)
                    act.wait_ge(*att_act.done(t, step, 2 * b))
                    nc.scalar.activation(dst[:, 0, b, :], t32[:, b % 2, :], ACT.Copy).then_inc(att_act.sem, 1)

            def att_up(t, _):
                heads(t, "K", "k", k16, colof["kk"], bks, "k_lo", "q_lo")
                for b in range(CB):
                    act.wait_ge(*att_pe.done(t, f"V{b // 2}"))
                    nc.scalar.activation(va32[:, b, :], att_bank[ATT_BANK["V", b // 2]][:, (b % 2) * T:(b % 2) * T + T],
                                         ACT.Identity, bias=bvcol[:, b:b + 1], scale=colof["vv"]).then_inc(att_act.sem, 1)

            def att_probs(t, _):
                for k in range(8):
                    act.wait_ge(*att_pe.done(t, f"S{k}"))
                    if k >= 2:
                        act.wait_ge(*att_pe.done(t, f"PV{k - 2}"))
                    nc.scalar.activation(pr[:, k % 2, :], att_bank[ATT_BANK["S", k]][:, :], ACT.Exp, scale=colof["soft"])\
                        .then_inc(att_act.sem, 1)

            def att_back(t, _):
                act.wait_ge(*att_dve.done(t, "ot"))
                nc.scalar.activation(qo16[:, 0, :, :], ot32, ACT.Copy, scale=colof["ot_hi"]).then_inc(att_act.sem, 1)

            def att_norm2(t, _):
                for s in range(SUB):
                    act.wait_ge(*att_dve.done(t, "x2", s))
                    nc.scalar.activation(h_rows[:, s, :], x2[:, s, :], ACT.Square, scale=float(C) ** -0.5,
                                         accum_out=msq[:, s:s + 1]).then_inc(att_act.sem, 1)

            def att_turn2(t, _):
                if t.back(1):
                    act.wait_ge(*moe_pe.done(t.back(1), "u"))
                for b in range(2):
                    act.wait_ge(*att_pe.done(t, f"T2{b}"))
                    nc.scalar.activation(h2t[:, 0, 2 * b:2 * b + 2, :], att_bank[ATT_BANK["T2", b]][:, :], ACT.Copy, scale=XS)\
                        .then_inc(att_act.sem, 1)

            def att_gate(t, _):
                act.wait_ge(*att_dve.done(t, "gsub"))
                nc.scalar.activation(gl[:, :, :], gl[:, :, :], ACT.Exp).then_inc(att_act.sem, 1)

            pipeline(act, {"mix_turn": mix_turn, "mix_kv": mix_kv, "mix_decay": mix_decay, "mix_state": mix_state,
                           "mix_out": mix_out, "att_turn": att_turn, "att_latent": att_latent, "att_up": att_up,
                           "att_probs": att_probs, "att_back": att_back,
                           "att_norm2": att_norm2, "att_turn2": att_turn2, "att_gate": att_gate})

        @block.vector
        def _(dve):
            count = [0]

            def link(ins):
                count[0] += 1
                ins.then_inc(set_dve, 1)
                dve.wait_ge(set_dve, count[0])

            def mark(ins):
                count[0] += 1
                ins.then_inc(set_dve, 1)

            V = nc.vector
            mark(V.memset(mx[:, :, :], 0.0))
            mark(V.memset(ones4[:, :], 1.0))
            mark(V.memset(vp[:, :, HD], 1.0))
            mark(V.memset(carry[0][:, 0, :], NEG_INF))
            mark(V.memset(carry[1][:, 0, :], NEG_INF))
            mark(V.memset(carry[0][:, 1:3, :], 0.0))
            link(V.memset(carry[1][:, 1:3, :], 0.0))
            assert count[0] == MAX_DONE
            for n, name in enumerate(BIG):
                dve.wait_ge(max_in[n % 2], 16 * (n // 2 + 1))
                mark(V.tensor_reduce(mx[:, n, :], stage[n % 2], AX, ALU.max, apply_absolute_value=True))
            dve.wait_ge(smalls_in, 16 * 7)
            mark(V.tensor_reduce(mx[:, IX["d"], :], d32, AX, ALU.max, apply_absolute_value=True))
            mark(V.tensor_reduce(mx[:, IX["g"], :], g32, AX, ALU.max, apply_absolute_value=True))
            mark(V.tensor_reduce(mx[:, IX["u"], 0:1], u32, AX, ALU.max, apply_absolute_value=True))
            dve.wait_ge(const_in, 16 * CONSTS)
            mark(V.tensor_reduce(mx[:, NW, 0:1], bqcol[:, :], AX, ALU.max, apply_absolute_value=True))
            mark(V.tensor_reduce(mx[:, NW + 1, 0:1], bdcol[:, :], AX, ALU.max, apply_absolute_value=True))
            mark(V.tensor_reduce(mx[:, NW + 2, 0:1], bkcol[:, :], AX, ALU.max, apply_absolute_value=True))
            link(V.tensor_reduce(mx[:, NW + 2, 1:2], bvcol[:, :], AX, ALU.max, apply_absolute_value=True))
            gamma_of = {"q": 0, "d": 0, "g": 1} | {f"e{e}": 1 for e in range(E)}
            for name, which in gamma_of.items():
                mark(V.tensor_tensor(mx[:, IX[name], :], mx[:, IX[name], :], gam[:, which, :], ALU.mult))
            dve.wait_ge(set_dve, count[0])
            mark(V.tensor_reduce(bound[:, 0:NW + 3], mx[:, :, :], AX, ALU.max, apply_absolute_value=True))
            assert count[0] == MAXES
            dve.wait_ge(set_pool, 4)
            bb = {"o": NW + 3, "c": NW + 4, "q": NW + 5, "kv": NW + 6}

            def bcol(n):
                return bound[:, n:n + 1]

            link(V.tensor_scalar(bcol(bb["o"]), bcol(IX["r"]), float(C), None, ALU.mult))
            link(V.scalar_tensor_tensor(out=bcol(bb["c"]), in0=bcol(IX["d"]), scalar=float(C), in1=bcol(NW + 1), op0=ALU.mult, op1=ALU.add))
            link(V.scalar_tensor_tensor(out=bcol(bb["q"]), in0=bcol(IX["q"]), scalar=float(C), in1=bcol(NW), op0=ALU.mult, op1=ALU.add))
            link(V.tensor_tensor(bcol(bb["kv"]), bcol(bb["c"]), bcol(IX["u"]), ALU.mult))
            link(V.scalar_tensor_tensor(out=bcol(bb["kv"]), in0=bcol(bb["kv"]), scalar=float(LAT), in1=bcol(NW + 2), op0=ALU.mult, op1=ALU.add))
            link(V.tensor_scalar(bound[:, bb["q"]:bb["kv"] + 1], bound[:, bb["q"]:bb["kv"] + 1], 16.0, None, ALU.max))
            mark(V.tensor_scalar(pw2[:, 0:NW], bound[:, 0:NW], 1e-30, None, ALU.max))
            link(V.tensor_scalar(pw2[:, NW:NW + 4], bound[:, NW + 3:NW + 7], 1e-30, None, ALU.max))
            link(V.tensor_scalar(pw2[:, :].bitcast(I32), pw2[:, :].bitcast(I32), 0x7F800000, None, ALU.bitwise_and))
            link(V.reciprocal(inv[:, :], pw2[:, :]))
            O_, C_, Q_, K_ = NW, NW + 1, NW + 2, NW + 3

            def p(n):
                n = IX[n] if isinstance(n, str) else n
                return pw2[:, n:n + 1]

            def i_(n):
                return inv[:, n:n + 1]

            for n in range(NW):
                mark(V.tensor_scalar(scl[:, n, :], ones4[:, :], i_(n), 2.0 ** 14, ALU.mult, ALU.mult))
            dve.wait_ge(set_dve, count[0])
            for name, which in gamma_of.items():
                mark(V.tensor_tensor(scl[:, IX[name], :], scl[:, IX[name], :], gam[:, which, :], ALU.mult))

            def product(dst, a, b, factor):
                mark(V.tensor_scalar(dst, a, b, factor, ALU.mult, ALU.mult))

            def times(dst, a, factor):
                mark(V.tensor_scalar(dst, a, factor, None, ALU.mult))

            times(colof["k"], p("k"), 2.0 ** -25)
            times(colof["v"], p("r"), 2.0 ** -25)
            product(colof["o"], p(O_), p("o1"), 2.0 ** -28)
            times(colof["o_hi"], i_(O_), 2.0 ** 13)
            product(colof["c"], i_(C_), p("d"), 2.0 ** -11)
            product(colof["q"], i_(Q_), p("q"), 2.0 ** -14)
            product(colof["t0"], p(C_), p("u"), 2.0 ** -17)
            product(colof["vv"], p(C_), p("u"), 2.0 ** -28)
            product(colof["soft"], p(Q_), p(K_), 2.0 ** -22 * float(HD) ** -0.5)
            times(colof["ot_hi"], i_(K_), 2.0 ** 14)
            product(colof["x2"], p(K_), p("o2"), 2.0 ** -28)
            times(colof["g"], p("g"), 2.0 ** -25)
            for s in range(SUB):
                times(ee[:, s, :], pw2[:, IX["e0"]:IX["e0"] + E], 2.0 ** -25)
            times(colof["t1"], i_(Q_), 2.0 ** 11)
            times(colof["t2"], i_(K_), 2.0 ** 11)
            times(colof["t3"], i_(C_), 2.0 ** 14)
            dve.wait_ge(set_dve, count[0])
            mark(V.tensor_tensor(colof["kk"], colof["t0"], i_(K_), ALU.mult))
            mark(V.tensor_scalar(bqs[:, :], bqcol[:, :], colof["t1"], None, ALU.mult))
            mark(V.tensor_scalar(bks[:, :], bkcol[:, :], colof["t2"], None, ALU.mult))
            mark(V.tensor_scalar(bds[:, :], bdcol[:, :], colof["t3"], None, ALU.mult))
            dve.wait_ge(set_act, 1)
            link(V.tensor_scalar(wcol[:, :], wcol[:, :], -1.0, None, ALU.mult))
            assert count[0] == SCALES, count[0]
            for n, name in enumerate(BIG):
                for b in range(CB):
                    src = bank[(n * CB + b) % 2][:, :] if name in TURNED else stage[n % 2][:, b, :]
                    dve.wait_ge(set_act, 1 + n * CB + b + 1)
                    mark(V.scalar_tensor_tensor(out=w16[name][:, 1, b, :], in0=src, scalar=scl[:, n, b:b + 1],
                                                in1=w16[name][:, 0, b, :], op0=ALU.mult, op1=ALU.subtract))
                assert count[0] == split_done(n)
            done = 1 + len(BIG) * CB
            for name, src in (("d", d32), ("g", g32)):
                for b in range(CB):
                    done += 1
                    dve.wait_ge(set_act, done)
                    mark(V.scalar_tensor_tensor(out=w16[name][:, 1, b, :], in0=src[:, b, :], scalar=scl[:, IX[name], b:b + 1],
                                                in1=w16[name][:, 0, b, :], op0=ALU.mult, op1=ALU.subtract))
            dve.wait_ge(set_act, done + 1)
            link(V.scalar_tensor_tensor(out=w16["u"][:, 1, :], in0=u32, scalar=scl[:, IX["u"], 0:1],
                                        in1=w16["u"][:, 0, :], op0=ALU.mult, op1=ALU.subtract))
            assert count[0] == SET_DVE, count[0]

            def lo(out_, in_, scale, hi):
                return V.scalar_tensor_tensor(out=out_, in0=in_, scalar=scale, in1=hi, op0=ALU.mult, op1=ALU.subtract)

            def mix_norm(t, _):
                dve.wait_ge(*x_in.done(t, "x"))
                for s in range(SUB):
                    V.bn_stats(st1[:, s, :], xk_rows[:, s, :]).then_inc(mix_dve.sem, 1)
                dve.wait_ge(*mix_dve.done(t, "stats"))
                V.memset(idle[:, :], 0.0).then_inc(mix_dve.sem, 1)
                for s in range(SUB):
                    V.bn_aggr(mv1[:, s, :], st1[:, s, :]).then_inc(mix_dve.sem, 1)
                dve.wait_ge(*mix_pool.done(t, "rstd"))
                for s in range(SUB):
                    V.tensor_scalar(xk_rows[:, s, :], xk_rows[:, s, :], mv1[:, s, 0:1], rs1[:, s:s + 1],
                                    ALU.subtract, ALU.mult).then_inc(mix_dve.sem, 1)

            def mix_turn(t, _):
                for b in range(2):
                    dve.wait_ge(*mix_act.done(t, "x_hi", b))
                    lo(xo16[:, 1, 2 * b:2 * b + 2, :], mix_bank[b][:, :], XS, xo16[:, 0, 2 * b:2 * b + 2, :]).then_inc(mix_dve.sem, 1)

            def mix_decay(t, h):
                V.tensor_copy(wkv[:, :, :, 0], carry[t.par][:, :, HF * h:HF * h + HF]).then_inc(mix_dve.sem, 1)
                dve.wait_ge(*mix_act.done(t, "k", h))
                dve.wait_ge(*mix_dve.done(t, f"carry_{h}"))
                for c in range(HF):
                    V.tensor_tensor_scan(wkv[:, 0, c, 1:T + 1], wcol[:, HF * h + c:HF * h + c + 1].to_broadcast([P, T]),
                                         k32[:, HF * h + c, :], wkv[:, 0, c, 0:1], ALU.add, ALU.max).then_inc(mix_dve.sem, 1)
                dve.wait_ge(*mix_dve.done(t, f"pp_{h}"))
                for c in range(HF):
                    V.scalar_tensor_tensor(out=zz[:, c, :], in0=k32[:, HF * h + c, :], scalar=ucol[:, HF * h + c:HF * h + c + 1],
                                           in1=wkv[:, 0, c, 0:T], op0=ALU.add, op1=ALU.subtract).then_inc(mix_dve.sem, 1)
                dve.wait_ge(*mix_dve.done(t, f"z_{h}"))
                V.tensor_scalar(zz[:, :, :], zz[:, :, :], ZMAX, None, ALU.min).then_inc(mix_dve.sem, 1)

            def mix_state(t, h):
                vh = v32[:, HF * h:HF * h + HF, :]
                prev_a, prev_b = wkv[:, 1, :, 0:T], wkv[:, 2, :, 0:T]
                dve.wait_ge(*mix_act.done(t, f"e2_{h}"))
                V.tensor_tensor(ev[:, :, :], e2[:, :, :], vh, ALU.mult).then_inc(mix_dve.sem, 1)
                dve.wait_ge(*mix_dve.done(t, f"ev_{h}"))
                for n, src in ((1, ev), (2, e2)):
                    for c in range(HF):
                        V.tensor_tensor_scan(wkv[:, n, c, 1:T + 1], e1[:, c, :], src[:, c, :], wkv[:, n, c, 0:1],
                                             ALU.mult, ALU.add).then_inc(mix_dve.sem, 1)
                dve.wait_ge(*mix_dve.done(t, f"b_{h}"))
                V.tensor_copy(carry[t.par][:, :, HF * h:HF * h + HF], wkv[:, :, :, T]).then_inc(mix_dve.sem, 1)
                V.tensor_tensor(e2[:, :, :], prev_b, vh, ALU.mult).then_inc(mix_dve.sem, 1)
                dve.wait_ge(*mix_dve.done(t, f"bv_{h}"))
                V.tensor_tensor(e2[:, :, :], prev_a, e2[:, :, :], ALU.subtract).then_inc(mix_dve.sem, 1)
                dve.wait_ge(*mix_act.done(t, f"r_{h}"))
                V.tensor_tensor(zz[:, :, :], prev_b, zz[:, :, :], ALU.add).then_inc(mix_dve.sem, 1)

            def mix_out(t, h):
                vh = v32[:, HF * h:HF * h + HF, :]
                dve.wait_ge(*mix_dve.done(t, f"den_{h}"))
                V.reciprocal(zz[:, :, :], zz[:, :, :]).then_inc(mix_dve.sem, 1)
                dve.wait_ge(*mix_dve.done(t, f"rec_{h}"))
                V.tensor_tensor(e2[:, :, :], e2[:, :, :], zz[:, :, :], ALU.mult).then_inc(mix_dve.sem, 1)
                dve.wait_ge(*mix_dve.done(t, f"frac_{h}"))
                V.tensor_tensor(e2[:, :, :], e2[:, :, :], vh, ALU.add).then_inc(mix_dve.sem, 1)
                dve.wait_ge(*mix_dve.done(t, f"y_{h}"))
                dve.wait_ge(*mix_act.done(t, f"th_{h}"))
                V.scalar_tensor_tensor(out=e2[:, :, :], in0=e1[:, :, :], scalar=1.0, in1=e2[:, :, :],
                                       op0=ALU.add, op1=ALU.mult).then_inc(mix_dve.sem, 1)
                dve.wait_ge(*mix_act.done(t, f"o_hi_{h}"))
                lo(xo16[:, 1, HF * h:HF * h + HF, :], e2[:, :, :], colof["o_hi"], xo16[:, 0, HF * h:HF * h + HF, :])\
                    .then_inc(mix_dve.sem, 1)

            def mix_project(t, _):
                dve.wait_ge(*res_in.done(t, "x"))
                for s in range(SUB):
                    dve.wait_ge(*mix_pe.done(t, "O", s))
                    V.scalar_tensor_tensor(out=x1[t.par][:, s, :], in0=mix_bank[s][:, :], scalar=colof["o"],
                                           in1=x1[t.par][:, s, :], op0=ALU.mult, op1=ALU.add).then_inc(mix_dve.sem, 1)

            def att_norm(t, _):
                xa = x1[t.par]
                for s in range(SUB):
                    dve.wait_ge(*mix_dve.done(t, "x1", s))
                    V.bn_stats(st2[:, s, :], xa[:, s, :]).then_inc(att_dve.sem, 1)
                dve.wait_ge(*att_dve.done(t, "stats"))
                V.memset(idle[:, :], 0.0).then_inc(att_dve.sem, 1)
                for s in range(SUB):
                    V.bn_aggr(mv2[:, s, :], st2[:, s, :]).then_inc(att_dve.sem, 1)
                dve.wait_ge(*att_pool.done(t, "small"))
                for s in range(SUB):
                    V.tensor_scalar(x2[:, s, :], xa[:, s, :], mv2[:, s, 0:1], sm[:, 1, s:s + 1],
                                    ALU.subtract, ALU.mult).then_inc(att_dve.sem, 1)
                for s in range(SUB):
                    V.tensor_scalar(h_rows[:, s, :], xa[:, s, :], mv2[:, s, 0:1], sm[:, 6, s:s + 1],
                                    ALU.subtract, ALU.mult).then_inc(att_dve.sem, 1)

            def att_turn(t, _):
                for b in range(2):
                    dve.wait_ge(*att_act.done(t, "h_hi", b))
                    lo(ht16[:, 1, 2 * b:2 * b + 2, :], att_bank[ATT_BANK["T", b]][:, :], XS, ht16[:, 0, 2 * b:2 * b + 2, :])\
                        .then_inc(att_dve.sem, 1)

            def att_latent(t, _):
                dve.wait_ge(*att_act.done(t, "c"))
                V.tensor_tensor(c16[LAT:2 * LAT, :], c32[LAT:2 * LAT, :], c16[LAT:2 * LAT, :], ALU.subtract).then_inc(att_dve.sem, 1)
                for b in range(CB):
                    dve.wait_ge(*att_act.done(t, "q", 2 * b + 1))
                    V.tensor_tensor(qo16[:, 1, b, :], t32[:, b % 2, :], qo16[:, 0, b, :], ALU.subtract).then_inc(att_dve.sem, 1)

            def att_up(t, _):
                for b in range(CB):
                    dve.wait_ge(*att_act.done(t, "k", 2 * b + 1))
                    V.tensor_tensor(k16[:, 1, b, :], t32[:, b % 2, :], k16[:, 0, b, :], ALU.subtract).then_inc(att_dve.sem, 1)

            def att_max(t, _):
                dve.wait_ge(*att_act.done(t, "v"))
                V.transpose(vp[:, :, 0:HD], va32[:, :, :].rearrange("p b (j g) -> p g (b j)", g=G)).then_inc(att_dve.sem, 1)
                for k in range(8):
                    dve.wait_ge(*att_pe.done(t, f"M{k}"))
                    V.tensor_reduce(mcol[:, 4 * k:4 * k + 4], att_bank[ATT_BANK["M", k]][:, :].rearrange("p (g x) -> p g x", g=4),
                                    AX, ALU.max).then_inc(att_dve.sem, 1)
                dve.wait_ge(*att_dve.done(t, "smax"))
                V.tensor_scalar(m16[:, 0, :], mcol[:, :], -2.0 ** -14, None, ALU.mult).then_inc(att_dve.sem, 1)
                dve.wait_ge(*att_dve.done(t, "m_hi"))
                lo(m16[:, 1, :], mcol[:, :], -2.0 ** -14, m16[:, 0, :]).then_inc(att_dve.sem, 1)

            def att_probs(t, _):
                for k in range(8):
                    pv = att_bank[ATT_BANK["PV", k]][:, 0:4 * (HD + 1)].rearrange("p (g d) -> p g d", g=4)
                    dve.wait_ge(*att_pe.done(t, f"PV{k}"))
                    V.reciprocal(rden[:, 4 * k:4 * k + 4], pv[:, :, HD]).then_inc(att_dve.sem, 1)
                    dve.wait_ge(*att_dve.done(t, "norm", 2 * k))
                    V.tensor_tensor(on[:, 4 * k:4 * k + 4, :], pv[:, :, 0:HD],
                                    rden[:, 4 * k:4 * k + 4].unsqueeze(2).to_broadcast([P, 4, HD]), ALU.mult).then_inc(att_dve.sem, 1)

            def att_back(t, _):
                dve.wait_ge(*att_dve.done(t, "norm"))
                V.transpose(ot32.rearrange("p b (j g) -> p g (b j)", g=G), on[:, :, :]).then_inc(att_dve.sem, 1)
                dve.wait_ge(*att_act.done(t, "ot_hi"))
                lo(qo16[:, 1, :, :].rearrange("p b t -> p (b t)"), ot32.rearrange("p b t -> p (b t)"), colof["ot_hi"],
                   qo16[:, 0, :, :].rearrange("p b t -> p (b t)")).then_inc(att_dve.sem, 1)

            def att_project(t, _):
                for s in range(SUB):
                    dve.wait_ge(*att_pe.done(t, f"O{s}"))
                    dve.wait_ge(*att_pool.done(t, "xb", s))
                    V.scalar_tensor_tensor(out=x2[:, s, :], in0=att_bank[ATT_BANK["O", s]][:, :], scalar=colof["x2"],
                                           in1=x2[:, s, :], op0=ALU.mult, op1=ALU.add).then_inc(att_dve.sem, 1)

            def att_norm2(t, _):
                dve.wait_ge(*att_pool.done(t, "rms"))
                for s in range(SUB):
                    V.tensor_scalar(h_rows[:, s, :], x2[:, s, :], sm[:, 0, s:s + 1], None, ALU.mult).then_inc(att_dve.sem, 1)

            def att_turn2(t, _):
                for b in range(2):
                    dve.wait_ge(*att_act.done(t, "h2_hi", b))
                    lo(h2t[:, 1, 2 * b:2 * b + 2, :], att_bank[ATT_BANK["T2", b]][:, :], XS, h2t[:, 0, 2 * b:2 * b + 2, :])\
                        .then_inc(att_dve.sem, 1)

            def att_gate(t, _):
                def bcast(a):
                    return a[:, :].unsqueeze(2).to_broadcast([P, SUB, E])

                dve.wait_ge(*att_pe.done(t, "G0"))
                V.scalar_tensor_tensor(out=gl[:, :, :].rearrange("p s e -> p (s e)"), in0=att_bank[ATT_BANK["G", 0]][:, 0:SUB * E],
                                       scalar=colof["g"], in1=bg_row[:, :, :].rearrange("p s e -> p (s e)"),
                                       op0=ALU.mult, op1=ALU.add).then_inc(att_dve.sem, 1)
                dve.wait_ge(*att_dve.done(t, "gl"))
                V.tensor_reduce(gmx[:, :], gl[:, :, :], AX, ALU.max).then_inc(att_dve.sem, 1)
                dve.wait_ge(*att_dve.done(t, "gmax"))
                V.tensor_tensor(gl[:, :, :], gl[:, :, :], bcast(gmx), ALU.subtract).then_inc(att_dve.sem, 1)
                dve.wait_ge(*att_act.done(t, "ge"))
                V.tensor_reduce(gsum[:, :], gl[:, :, :], AX, ALU.add).then_inc(att_dve.sem, 1)
                dve.wait_ge(*att_dve.done(t, "gsum"))
                V.reciprocal(gmx[:, :], gsum[:, :]).then_inc(att_dve.sem, 1)
                dve.wait_ge(*att_dve.done(t, "grec"))
                V.tensor_tensor(gl[:, :, :], gl[:, :, :], bcast(gmx), ALU.mult).then_inc(att_dve.sem, 1)
                dve.wait_ge(*att_dve.done(t, "gmul"))
                V.tensor_tensor(gates[:, :, :], gl[:, :, :], ee[:, :, :], ALU.mult).then_inc(att_dve.sem, 1)

            def moe(t, u):
                e, s = u // SUB, u % SUB
                if u == 0:
                    dve.wait_ge(*att_pool.done(t, "acc"))
                    dve.wait_ge(*att_dve.done(t, "gates"))
                if u >= SUB:
                    dve.wait_ge(*moe_dve.done(t, "u", u - SUB))
                dve.wait_ge(*moe_pe.done(t, "u", u))
                V.scalar_tensor_tensor(out=acc[:, s, :], in0=moe_bank[u % 2][:, :], scalar=gates[:, s, e:e + 1],
                                       in1=acc[:, s, :], op0=ALU.mult, op1=ALU.add).then_inc(moe_dve.sem, 1)

            pipeline(dve, {"mix_norm": mix_norm, "mix_turn": mix_turn, "mix_decay": mix_decay, "mix_state": mix_state,
                           "mix_out": mix_out, "mix_project": mix_project, "att_norm": att_norm, "att_turn": att_turn,
                           "att_latent": att_latent, "att_up": att_up, "att_max": att_max, "att_probs": att_probs,
                           "att_back": att_back, "att_project": att_project, "att_norm2": att_norm2,
                           "att_turn2": att_turn2, "att_gate": att_gate, "moe": moe})

        @block.tensor
        def _(pe):
            PASSES = ((0, 0), (1, 0), (0, 1))

            def product(dst, blocks):
                last = len(blocks) * len(PASSES) - 1
                n = 0
                for left, right in blocks:
                    for a, b in PASSES:
                        ins = nc.tensor.matmul(dst, left(a), right(b), start=(n == 0), stop=(n == last))
                        n += 1
                return ins

            pe.wait_ge(const_in, 16 * CONSTS)
            for n, name in enumerate(BIG):
                if name not in TURNED:
                    continue
                pe.wait_ge(split_in[n % 2], 16 * (n // 2 + 1))
                for b in range(CB):
                    use = n * CB + b
                    if use >= 2:
                        pe.wait_ge(set_dve, SCALES + use - 1)
                    for r in range(CB):
                        ins = nc.tensor.transpose(bank[use % 2][:, r * P:(r + 1) * P], stage[n % 2][:, r, b * P:(b + 1) * P], ident[:, :])
                    ins.then_inc(set_pe, 1)
            pe.wait_ge(set_dve, SET_DVE)
            pe.wait_ge(masks_in, 32)

            def turn(rows_, banks, steps, sem_, waits):
                for b in range(2):
                    waits(b)
                    for c in range(2):
                        for s in range(SUB):
                            ins = nc.tensor.transpose(banks[b][:, c * T + s * P:c * T + (s + 1) * P],
                                                      rows_[:, s, (2 * b + c) * P:(2 * b + c + 1) * P], ident[:, :])
                    ins.then_inc(sem_, 1)

            def mix_free(t, use, k):
                before = {"T": ("O", True), "K": ("T", False), "V": ("K", False), "O": ("V", False)}[use]
                steps, step, n = mix_reader(before[0], k)
                if not before[1]:
                    pe.wait_ge(*steps.done(t, step, n))
                elif t.back(1):
                    pe.wait_ge(*steps.done(t.back(1), step, n))

            def att_free(t, use, k):
                (before, n), earlier = att_before((use, k))
                steps, step, m = att_reader(before, n)
                if not earlier:
                    pe.wait_ge(*steps.done(t, step, m))
                elif t.back(1):
                    pe.wait_ge(*steps.done(t.back(1), step, m))

            def channel(dst, name, blk, src, width=P):
                return product(dst, [(lambda a, kb=kb: w16[name][:, a, kb, blk * width:(blk + 1) * width],
                                      lambda b, kb=kb: src[:, b, kb, :]) for kb in range(CB)])

            def token(dst, name, s, src):
                return product(dst, [(lambda a, kb=kb: src[:, a, kb, s * P:(s + 1) * P],
                                      lambda b, kb=kb: w16[name][:, b, kb, :]) for kb in range(CB)])

            def mix_turn(t, _):
                pe.wait_ge(*mix_dve.done(t, "norm"))
                turn(xk_rows, mix_bank, mix_pe, mix_pe.sem, lambda b: mix_free(t, "T", b))

            def mix_kv(t, _):
                pe.wait_ge(*mix_dve.done(t, "x_lo"))
                for use, name in (("K", "k"), ("V", "r")):
                    for b in range(2):
                        mix_free(t, use, b)
                        for c in range(2):
                            ins = channel(mix_bank[b][:, c * T:(c + 1) * T], name, 2 * b + c, xo16)
                        ins.then_inc(mix_pe.sem, 1)

            def mix_project(t, _):
                pe.wait_ge(*mix_dve.done(t, "o_lo_1"))
                for s in range(SUB):
                    mix_free(t, "O", s)
                    token(mix_bank[s][:, :], "o1", s, xo16).then_inc(mix_pe.sem, 1)

            def att_turn(t, _):
                pe.wait_ge(*att_dve.done(t, "h"))
                turn(h_rows, [att_bank[ATT_BANK["T", b]] for b in range(2)], att_pe, att_pe.sem, lambda b: att_free(t, "T", b))

            def att_latent(t, _):
                pe.wait_ge(*att_dve.done(t, "h_lo"))
                att_free(t, "D", 0)
                channel(att_bank[ATT_BANK["D", 0]][:, 0:T], "d", 0, ht16).then_inc(att_pe.sem, 1)
                for b in range(2):
                    att_free(t, "Q", b)
                    for c in range(2):
                        ins = channel(att_bank[ATT_BANK["Q", b]][:, c * T:(c + 1) * T], "q", 2 * b + c, ht16)
                    ins.then_inc(att_pe.sem, 1)

            def att_up(t, _):
                pe.wait_ge(*att_dve.done(t, "c_lo"))
                for n, use in enumerate("KV"):
                    for b in range(2):
                        att_free(t, use, b)
                        for c in range(2):
                            blk = n * CB + 2 * b + c
                            for a in range(2):
                                ins = nc.tensor.matmul(att_bank[ATT_BANK[use, b]][:, c * T:(c + 1) * T],
                                                       w16["u"][:, a, blk * P:(blk + 1) * P], c16[:, :], start=(a == 0), stop=(a == 1))
                        ins.then_inc(att_pe.sem, 1)

            def group(stacked, n_rows, g):
                return stacked[0:n_rows, :, :].rearrange("p h (j g) -> p g (h j)", j=NJ)[:, g]

            def att_max(t, _):
                pe.wait_ge(*stack_in.done(t, "qk"))
                for k in range(8):
                    att_free(t, "M", k)
                    for n in range(4):
                        ins = nc.tensor.matmul(att_bank[ATT_BANK["M", k]][:, n * P:(n + 1) * P],
                                               group(qs, SCAN_ROWS, 4 * k + n), group(ks, SCAN_ROWS, 4 * k + n), start=True, stop=True)
                    ins.then_inc(att_pe.sem, 1)

            def att_probs(t, _):
                def scores(k):
                    att_free(t, "S", k)
                    for n in range(4):
                        ins = nc.tensor.matmul(att_bank[ATT_BANK["S", k]][:, n * P:(n + 1) * P],
                                               group(ks, SCAN_ROWS + 2, 4 * k + n), group(qs, SCAN_ROWS + 2, 4 * k + n), start=True, stop=True)
                    ins.then_inc(att_pe.sem, 1)

                def weigh(k):
                    att_free(t, "PV", k)
                    pe.wait_ge(*att_act.done(t, "ex", k))
                    for n in range(4):
                        ins = nc.tensor.matmul(att_bank[ATT_BANK["PV", k]][:, n * (HD + 1):(n + 1) * (HD + 1)],
                                               pr[:, k % 2, n * P:(n + 1) * P], vp[:, 4 * k + n, :], start=True, stop=True)
                    ins.then_inc(att_pe.sem, 1)

                pe.wait_ge(*m_in.done(t, "m"))
                pe.wait_ge(*att_dve.done(t, "vt"))
                scores(0)
                for k in range(7):
                    scores(k + 1)
                    weigh(k)
                weigh(7)

            def att_project(t, _):
                pe.wait_ge(*att_dve.done(t, "ot_lo"))
                for s in range(SUB):
                    att_free(t, "O", s)
                    token(att_bank[ATT_BANK["O", s]][:, :], "o2", s, qo16).then_inc(att_pe.sem, 1)

            def att_turn2(t, _):
                pe.wait_ge(*att_dve.done(t, "h2"))
                turn(h_rows, [att_bank[ATT_BANK["T2", b]] for b in range(2)], att_pe, att_pe.sem, lambda b: att_free(t, "T2", b))

            def att_gate(t, _):
                pe.wait_ge(*att_dve.done(t, "h2_lo"))
                att_free(t, "G", 0)
                for s in range(SUB):
                    ins = token(att_bank[ATT_BANK["G", 0]][:, s * E:(s + 1) * E], "g", s, h2t)
                ins.then_inc(att_pe.sem, 1)

            def moe(t, u):
                if u >= 2:
                    pe.wait_ge(*moe_dve.done(t, "u", u - 2))
                elif t.back(1):
                    pe.wait_ge(*moe_dve.done(t.back(1), "u", 2 * E - 2 + u))
                token(moe_bank[u % 2][:, :], f"e{u // SUB}", u % SUB, h2t).then_inc(moe_pe.sem, 1)

            pipeline(pe, {"mix_turn": mix_turn, "mix_kv": mix_kv, "mix_project": mix_project, "att_turn": att_turn,
                          "att_latent": att_latent, "att_up": att_up, "att_max": att_max, "att_probs": att_probs,
                          "att_project": att_project, "att_turn2": att_turn2,
                          "att_gate": att_gate, "moe": moe})


CONSTS = 1 + 5 + 8 + 2 + 1 + SUB
MAX_DONE = 7
MAXES = MAX_DONE + len(BIG) + 7 + (3 + E) + 1
SCALES = MAXES + 10 + NW + (3 + E) + 12 + SUB + 3 + 4 + 1
SET_DVE = SCALES + len(BIG) * CB + 2 * CB + 1


def split_done(n):
    return SCALES + (n + 1) * CB


def masks():
    j = np.arange(T) // G
    same = (j[None, :] == np.arange(NJ)[:, None]).astype(np.float16)
    km = np.repeat((same * np.float16(2.0 ** 15))[:, None, :], H, axis=1).reshape(NJ, H * T)
    qm = np.repeat(((1 - same) * np.float16(-65504.0))[:, None, :], H, axis=1).reshape(NJ, H * T)
    km = np.concatenate([km, np.full((2, H * T), 2.0 ** 14, np.float16)])
    return np.ascontiguousarray(km), np.ascontiguousarray(qm)


_INS = ["attn_x", "attn_Wk", "attn_Wr", "attn_Wo", "attn_time_decay", "attn_time_first", "ffn_gamma1",
        "ffn_Wq", "ffn_bq", "ffn_Wdown", "ffn_bdown", "ffn_Wup", "ffn_bup", "ffn_Wo", "ffn_bo",
        "ffn_gamma2", "ffn_Wg", "ffn_bg", "ffn_We"]


def kernel(**inputs):
    import concourse.bacc as bacc
    from concourse.bass_utils import run_bass_kernel_spmd

    nc = bacc.Bacc("TRN2", target_bir_lowering=False, num_devices=1)
    arrays = {f"in_{n}": np.ascontiguousarray(inputs[f"L0_{n}"]) for n in _INS}
    arrays["in_ident"] = np.eye(P, dtype=np.float32)
    arrays["in_kmask"], arrays["in_qmask"] = masks()
    args = [nc.dram_tensor(n, a.shape, mybir.dt.from_np(a.dtype), kind="ExternalInput").ap() for n, a in arrays.items()]
    out = nc.dram_tensor("result", (B, L, C), F32, kind="ExternalOutput").ap()
    build(nc, *args, out)
    r = run_bass_kernel_spmd(nc, [arrays], core_ids=[0])
    return r.results[0]["result"]
```

```python
from contextlib import ExitStack

import numpy as np

import concourse.bass as bass
from concourse import mybir

P = 128
B, L, C = 2, 4096, 512
T = 256
SUB = T // P
NT = B * L // T
CB = C // P
H, HD = 16, 32
LAT = 64
E = 8
G = 32
NJ = T // G
HF = CB // 2
XS = 2048.0
NEG_INF = -1e38
ZMAX = 87.0
LN_EPS, RMS_EPS = 1e-5, 1e-6
SCAN_ROWS = 3 * HD + NJ

ALU = mybir.AluOpType
ACT = mybir.ActivationFunctionType
AX = mybir.AxisListType.X
F32, F16, I32 = mybir.dt.float32, mybir.dt.float16, mybir.dt.int32
RMAX = bass.bass_isa.ReduceOp.max


class Tile:

    def __init__(self, n, par, chunk):
        self.n, self.par, self.chunk = n, par, chunk

    def back(self, d):
        if isinstance(self.n, int) and self.n < d:
            return None
        return Tile(self.n - d, (self.par - d) % 2, None)


class Steps:

    def __init__(self, sem, unit=1, **counts):
        self.sem, self.unit, self.first, self.total = sem, unit, {}, 0
        for step, count in counts.items():
            self.first[step] = (self.total, count)
            self.total += count

    def done(self, tile, step, k=-1):
        first, count = self.first[step]
        assert k < count
        k = k % count
        return self.sem, tile.n * (self.total * self.unit) + (first + k + 1) * self.unit


BIG = ["k", "r", "o1", "q", "o2"] + [f"e{e}" for e in range(E)]
SMALL = ["d", "g", "u"]
NAMES = BIG + SMALL
IX = {name: n for n, name in enumerate(NAMES)}
NW = len(NAMES)
TURNED = ("k", "r", "o1")

ATT_USES = ([("T", 0), ("T", 1), ("D", 0), ("Q", 0), ("Q", 1), ("K", 0), ("K", 1), ("V", 0), ("V", 1),
             ] + [("M", k) for k in range(8)] + [("S", 0)]
            + [x for k in range(7) for x in (("S", k + 1), ("PV", k))] + [("PV", 7)]
            + [("O", 0), ("O", 1), ("T2", 0), ("T2", 1), ("G", 0)])
ATT_RING = 4
ATT_BANK = {use: n % ATT_RING for n, use in enumerate(ATT_USES)}


def att_before(use):
    n = ATT_USES.index(use)
    for m in range(n - 1, -1, -1):
        if ATT_BANK[ATT_USES[m]] == ATT_BANK[use]:
            return ATT_USES[m], False
    for m in range(len(ATT_USES) - 1, -1, -1):
        if ATT_BANK[ATT_USES[m]] == ATT_BANK[use]:
            return ATT_USES[m], True


ORDER = [
    ("att_stats", 0), ("mix_turn", 0), ("att_norm", 0), ("moe_acc", 0), ("moe_gate", 0), ("moe", 0),
    ("att_turn", 0), ("att_rest", 0), ("moe", 1), ("att_latent", 0), ("att_q", 0), ("att_up", 0),
    ("mix_k", 0), ("mix_v", 0), ("mix_decay", 0), ("att_stack", 0), ("moe", 2), ("att_vt", 0), ("mix_exp", 0),
    ("mix_sum", 0), ("moe", 3), ("mix_rec", 0), ("mix_rec", 1), ("moe", 4), ("mix_scan", 0), ("att_max", 0),
    ("moe", 5), ("att_max", 1), ("att_m", 0), ("mix_num", 0), ("moe", 6), ("mix_gate", 0), ("moe", 7),
    ("mix_split", 0), ("mix_decay", 1), ("att_scores", 0), ("att_scores", 1), ("mix_exp", 1), ("moe", 8),
    ("mix_sum", 1), ("att_probs", 0), ("att_scores", 2), ("att_probs", 1), ("att_scores", 3), ("mix_rec", 2),
    ("moe", 9), ("att_probs", 2), ("att_scores", 4), ("att_probs", 3), ("att_scores", 5), ("pre_load", 0),
    ("mix_rec", 3), ("moe", 10), ("att_probs", 4), ("att_scores", 6), ("att_probs", 5), ("att_scores", 7),
    ("mix_scan", 1), ("moe", 11), ("att_probs", 6), ("att_probs", 7), ("att_back", 0), ("moe", 12),
    ("mix_num", 1), ("moe", 13), ("pre_stats", 0), ("att_project", 0), ("mix_gate", 1), ("att_square", 0),
    ("moe", 14), ("att_norm2", 0), ("mix_split", 1), ("pre_norm", 0), ("moe", 15), ("moe_store", 0),
    ("att_turn2", 0), ("mix_project", 0), ("att_gate", 0),
]


def build(nc, x, wk, wr, wo1, decay, first, gamma1, wq, bq, wdown, bdown, wup, bup, wo2, bo, gamma2,
          wg, bg, we, ident_in, kmask_in, qmask_in, out):
    with ExitStack() as ctx:
        def sb(name, shape, dt=F32):
            return ctx.enter_context(nc.sbuf_tensor(name, shape, dt))

        def sem(name):
            return ctx.enter_context(nc.semaphore(name))

        ctx.enter_context(nc.allow_non_contiguous_dma(reason="short columns of constants"))
        bank = [ctx.enter_context(nc.psum_tensor(f"bank{n}", [P, 512], F32)) for n in range(8)]
        moe_bank, mix_bank, att_bank = bank[0:2], bank[2:4], bank[4:8]

        w16 = {name: sb(f"w_{name}", [P, 2, CB, C], F16) for name in BIG}
        w16["d"] = sb("w_d", [P, 2, CB, 2 * LAT], F16)
        w16["g"] = sb("w_g", [P, 2, CB, E], F16)
        w16["u"] = sb("w_u", [P, 2, 2 * C], F16)

        ident = sb("ident", [P, P])
        wcol, ucol = sb("wcol", [P, CB]), sb("ucol", [P, CB])
        gam = sb("gam", [P, 2, CB])
        bqcol, bkcol, bvcol, bdcol = sb("bqcol", [P, CB]), sb("bkcol", [P, CB]), sb("bvcol", [P, CB]), sb("bdcol", [P, 1])
        bqs, bks, bds = sb("bqs", [P, CB]), sb("bks", [P, CB]), sb("bds", [P, 1])
        bo_row, bg_row = sb("bo_row", [P, C]), sb("bg_row", [P, SUB, E])
        mx = sb("mx", [P, NW + 3, CB])
        bound, pw2, inv = sb("bound", [P, NW + 8]), sb("pw2", [P, NW + 4]), sb("inv", [P, NW + 4])
        scl = sb("scl", [P, NW, CB])
        col = sb("col", [P, 24])
        ee = sb("ee", [P, SUB, E])
        half4 = sb("half4", [P, 2, SUB])
        half = half4[:, 0, :]
        eps_ln, eps_rms, idle = sb("eps_ln", [P, SUB]), sb("eps_rms", [P, SUB]), sb("idle", [P, 1])
        ones4 = sb("ones4", [P, CB])
        names = ["k", "v", "o", "o_hi", "c", "q", "kk", "vv", "soft", "ot_hi", "x2", "g", "t0", "t1", "t2", "t3", "t4"]
        colof = {name: col[:, n:n + 1] for n, name in enumerate(names)}

        xk = sb("xk", [P, 1024])
        xk_rows = xk[:, :].rearrange("p (s c) -> p s c", s=SUB)
        k32 = xk[:, :].rearrange("p (b t) -> p b t", b=CB)
        v32 = sb("v32", [P, CB, T])
        xo16 = sb("xo16", [P, 2, CB, T], F16)
        wkv = sb("wkv", [P, 3, HF, T + 1])
        e1, e2, ev, zz = (sb(n, [P, HF, T]) for n in ("e1", "e2", "ev", "zz"))
        carry = [sb(f"carry{b}", [P, 3, CB]) for b in range(B)]
        st1, mv1 = sb("st1", [P, SUB, 6]), sb("mv1", [P, SUB, 2])
        ve1, rs1 = sb("ve1", [P, SUB]), sb("rs1", [P, SUB])
        x1 = [sb(f"x1_{n}", [P, SUB, C]) for n in range(2)]

        x2 = sb("x2", [P, SUB, C])
        hrow = sb("hrow", [P, SUB * C])
        h_rows = hrow[:, :].rearrange("p (s c) -> p s c", s=SUB)
        on = hrow[:, :].rearrange("p (g d) -> p g d", d=HD)
        ht = sb("ht", [P, 1024])
        ht16 = ht[:, :].bitcast(F16).rearrange("p (l b t) -> p l b t", l=2, b=CB)
        ot32 = ht[:, :].rearrange("p (b t) -> p b t", b=CB)
        c32, c16 = sb("c32", [P, T]), sb("c16", [P, T], F16)
        t32 = sb("t32", [P, 2, T])
        qo16 = sb("qo16", [P, 2, CB, T], F16)
        k16 = sb("k16", [P, 2, CB, T], F16)
        va32 = ht[:, :].rearrange("p (b t) -> p b t", b=CB)
        vp = sb("vp", [P, G, HD + 1])
        qs, ks = sb("qs", [P, H, T], F16), sb("ks", [P, H, T], F16)
        pr = sb("pr", [P, 2, 4 * P])
        mcol, m16 = sb("mcol", [P, G]), sb("m16", [P, 2, G], F16)
        rden = sb("rden", [P, G])
        st2, mv2 = sb("st2", [P, SUB, 6]), sb("mv2", [P, SUB, 2])
        var2, rs2 = sb("var2", [P, 2, SUB]), sb("rs2", [P, 2, SUB])
        ve3, rs3 = sb("ve3", [P, SUB]), sb("rs3", [P, SUB])
        msq = sb("msq", [P, SUB])
        gl, gmx, gsum = sb("gl", [P, SUB, E]), sb("gmx", [P, SUB]), sb("gsum", [P, SUB])
        gates = sb("gates", [P, SUB, E])

        h2t = sb("h2t", [P, 2, CB, T], F16)
        acc = sb("acc", [P, SUB, C])

        stage = [b[:, :, :].rearrange("p h t -> p (h t)").bitcast(F32).rearrange("p (b c) -> p b c", b=CB)
                 for b in (qs, ks)]
        d32 = hrow[:, 0:512].rearrange("p (b c) -> p b c", b=CB)
        g32 = hrow[:, 512:512 + CB * E].rearrange("p (b c) -> p b c", b=CB)
        u32 = x2[:, :, :].rearrange("p s c -> p (s c)")

        const_in, smalls_in = sem("const_in"), sem("smalls_in")
        max_in = [sem("max_in0"), sem("max_in1")]
        split_in = [sem("split_in0"), sem("split_in1")]
        masks_in = sem("masks_in")
        set_dve, set_act, set_pool, set_pe = sem("set_dve"), sem("set_act"), sem("set_pool"), sem("set_pe")

        x_in = Steps(sem("x_in"), 16, x=1)
        res_in = Steps(sem("res_in"), 16, x=1)
        stack_in = Steps(sem("stack_in"), 16, qk=16)
        m_in = Steps(sem("m_in"), 16, m=2)
        stored = Steps(sem("stored"), 16, out=1)
        mix_pe = Steps(sem("mix_pe"), T=2, K=2, V=2, O=2)
        mix_act = Steps(sem("mix_act"), x_hi=2, k=2, v=2, r_0=1, e1_0=2, e2_0=1, th_0=1, o_hi_0=1,
                        r_1=1, e1_1=2, e2_1=1, th_1=1, o_hi_1=1)
        wkv_steps = ("carry", 1), ("pp", 2), ("z", 2), ("zc", 1), ("b", 2), ("rec", 2), ("ev", 1), ("a", 2), ("keep", 1), ("bv", 1), \
            ("num", 1), ("frac", 1), ("y", 1), ("gated", 1), ("o_lo", 1)
        wkv_pool = ("d1", 1), ("d2", 1), ("den", 1)
        pre_dve = Steps(sem("pre_dve"), stats=2, idle=1, aggr=2, norm=2)
        pre_pool = Steps(sem("pre_pool"), eps=1, rstd=1)
        mix_dve = Steps(sem("mix_dve"), x_lo=2,
                        **{f"{s}_{h}": c for h in (0, 1) for s, c in wkv_steps}, x1=2)
        mix_pool = Steps(sem("mix_pool"), **{f"{s}_{h}": c for h in (0, 1) for s, c in wkv_pool})
        att_pe = Steps(sem("att_pe"), **{f"{n}{k}": 1 for n, k in ATT_USES})
        att_act = Steps(sem("att_act"), h_hi=2, c=2, q=8, k=8, ex=8, ot_hi=2, sq=2,
                        h2_hi=2)
        att_dve = Steps(sem("att_dve"), stats=2, idle=1, aggr=2, var=2, h=2, h_lo=2, xn=2, c_lo=1, v=4, stack=8,
                        vt=1, smax=8, m_hi=1, m_lo=1, norm=16, ot=1, ot_lo=2, x2=2, h2=2, h2_lo=2)
        gate_dve = Steps(sem("gate_dve"), gl=1, gmax=1, gsub=1, gsum=1, grec=1, gmul=1, gates=1)
        gate_act = Steps(sem("gate_act"), ge=1)
        att_pool = Steps(sem("att_pool"), rstd=1, xb=2, q_lo=4, k_lo=4, rms=2)
        acc_pool = Steps(sem("acc_pool"), acc=2)
        moe_pe = Steps(sem("moe_pe"), u=2 * E)
        moe_dve = Steps(sem("moe_dve"), u=2 * E)

        def mix_reader(use, k):
            return {"T": (mix_dve, "x_lo", k), "K": (mix_act, "k", k), "V": (mix_act, "v", k),
                    "O": (mix_dve, "x1", k)}[use]

        def att_reader(use, k):
            return {"T": (att_dve, "h_lo", k), "D": (att_act, "c", 0), "Q": (att_act, "q", 4 * k + 2),
                    "K": (att_act, "k", 4 * k + 2), "V": (att_dve, "v", 2 * k + 1),
                    "M": (att_dve, "smax", k), "S": (att_act, "ex", k), "PV": (att_dve, "norm", 2 * k + 1),
                    "O": (att_dve, "x2", k), "T2": (att_dve, "h2_lo", k),
                    "G": (gate_dve, "gl", 0)}[use]

        def pipeline(eng, steps):
            def iteration(i, par, chunk):
                flat = isinstance(i, int)
                tiles = {}
                if not flat or i + 1 < NT:
                    tiles["pre"] = Tile(i + 1, 1 - par, chunk + par)
                if not flat or i < NT:
                    tiles["mix"] = Tile(i, par, chunk)
                if not flat or 1 <= i <= NT:
                    tiles["att"] = Tile(i - 1, 1 - par, None)
                if not flat or 2 <= i:
                    tiles["moe"] = Tile(i - 2, par, chunk - 1)
                for name, k in ORDER:
                    stage_name = name.split("_")[0]
                    if name in steps and stage_name in tiles:
                        steps[name](tiles[stage_name], k)

            for name, k in ORDER:
                if name in steps and name.startswith("pre"):
                    steps[name](Tile(0, 0, 0), k)
            for i in range(4):
                iteration(i, i % 2, i // 2)
            with eng.Fori(0, (NT - 6) // 2) as pair:
                for par in range(2):
                    iteration(pair * 2 + (4 + par), par, pair + 2)
            for i in range(NT - 2, NT + 2):
                iteration(i, i % 2, i // 2)

        weight_dram = {"k": wk, "r": wr, "o1": wo1, "q": wq, "o2": wo2}
        weight_dram |= {f"e{e}": we[e] for e in range(E)}
        block = ctx.enter_context(nc.Block())

        def rows(dram, tile):
            view = dram[tile.par].rearrange("(n s p) c -> n p s c", s=SUB, p=P)
            if isinstance(tile.chunk, int):
                return view[tile.chunk]
            return view[bass.ds(tile.chunk, 1)].rearrange("n p s c -> (n p) s c")

        @block.sync
        def _(sp):
            sp.dma_start(ident[:, :], ident_in).then_inc(const_in, 16)
            for tile_, dram in ((wcol, decay), (ucol, first), (gam[:, 0, :], gamma1), (gam[:, 1, :], gamma2), (bqcol, bq)):
                sp.dma_start(tile_[:, :], dram.rearrange("(b p) -> p b", p=P)).then_inc(const_in, 16)
            bup_v = bup.rearrange("(b f k d) -> k f d b", f=4, k=2, d=HD)
            for f in range(4):
                sp.dma_start(bkcol[f * HD:(f + 1) * HD, :], bup_v[0, f]).then_inc(const_in, 16)
                sp.dma_start(bvcol[f * HD:(f + 1) * HD, :], bup_v[1, f]).then_inc(const_in, 16)
            for n in range(2):
                sp.dma_start(bdcol[n * LAT:(n + 1) * LAT, :], bdown.rearrange("(p a) -> p a", a=1)).then_inc(const_in, 16)
            sp.dma_start(bo_row[:, :], bo.partition_broadcast(P)).then_inc(const_in, 16)
            for s in range(SUB):
                sp.dma_start(bg_row[:, s, :], bg.partition_broadcast(P)).then_inc(const_in, 16)
            for n in range(2):
                sp.dma_start(d32[:, :, n * LAT:(n + 1) * LAT], wdown.rearrange("(b p) c -> p b c", p=P)).then_inc(smalls_in, 16)
                for k in range(2):
                    sp.dma_start(u32[n * LAT:(n + 1) * LAT, k * C:(k + 1) * C].rearrange("p (g d) -> p g d", g=H),
                                 wup.rearrange("l (g k d) -> k l g d", g=H, k=2)[k]).then_inc(smalls_in, 16)
            sp.dma_start(g32, wg.rearrange("(b p) c -> p b c", p=P)).then_inc(smalls_in, 16)
            for n, name in enumerate(BIG):
                if n >= 2:
                    sp.wait_ge(set_dve, MAX_DONE + n - 2 + 1)
                sp.dma_start(stage[n % 2], weight_dram[name].rearrange("(b p) c -> p b c", p=P)).then_inc(max_in[n % 2], 16)
            for n, name in enumerate(BIG):
                if n < 2:
                    sp.wait_ge(set_dve, MAX_DONE + len(BIG))
                else:
                    sp.wait_ge(set_dve, split_done(n - 2))
                sp.dma_start(stage[n % 2], weight_dram[name].rearrange("(b p) c -> p b c", p=P)).then_inc(split_in[n % 2], 16)
            sp.wait_ge(set_dve, split_done(len(BIG) - 1))
            sp.dma_start(ks[3 * HD:SCAN_ROWS + 2, :, :], kmask_in.rearrange("a (h t) -> a h t", h=H)).then_inc(masks_in, 16)
            sp.dma_start(qs[3 * HD:SCAN_ROWS, :, :], qmask_in.rearrange("a (h t) -> a h t", h=H)).then_inc(masks_in, 16)

            def pre_load(t, _):
                if t.back(1):
                    sp.wait_ge(*mix_dve.done(t.back(1), "z_1"))
                    sp.wait_ge(*mix_pool.done(t.back(1), "d2_1"))
                sp.dma_start(xk_rows, rows(x, t)).then_inc(x_in.sem, 16)

            def mix_k(t, _):
                if t.back(2):
                    sp.wait_ge(*acc_pool.done(t.back(2), "acc"))
                sp.dma_start(x1[t.par][:, :, :], rows(x, t)).then_inc(res_in.sem, 16)

            def att_up(t, _):
                for src, dst, name, first in ((qo16, qs, "q", (0, 1)), (k16, ks, "k", ())):
                    rest = 2 if first else 1
                    for f in range(4):
                        for n in first:
                            if f == 0 and n == 0:
                                sp.wait_ge(*att_act.done(t, name))
                            sp.dma_start(dst[n * HD:(n + 1) * HD, f * CB:(f + 1) * CB, :],
                                         src[f * HD:(f + 1) * HD, 0]).then_inc(stack_in.sem, 16)
                    sp.wait_ge(*att_pool.done(t, f"{name}_lo"))
                    for f in range(4):
                        sp.dma_start(dst[rest * HD:(rest + 1) * HD, f * CB:(f + 1) * CB, :],
                                     src[f * HD:(f + 1) * HD, 1]).then_inc(stack_in.sem, 16)

            def att_m(t, _):
                sp.wait_ge(*att_dve.done(t, "m_lo"))
                for l in range(2):
                    sp.dma_start(qs[SCAN_ROWS + l:SCAN_ROWS + l + 1, :, :].rearrange("a h (j g) -> a (h j) g", j=NJ), m16[:, l, :])\
                        .then_inc(m_in.sem, 16)

            def moe_store(t, _):
                sp.wait_ge(*moe_dve.done(t, "u"))
                sp.dma_start(rows(out, t), acc[:, :, :]).then_inc(stored.sem, 16)

            pipeline(sp, {"pre_load": pre_load, "mix_k": mix_k, "att_up": att_up, "att_m": att_m,
                          "moe_store": moe_store})
            sp.wait_ge(*stored.done(Tile(NT - 1, 1, 0), "out"))

        @block.gpsimd
        def _(pool):
            pool.memset(half4[:, :, :], -0.5).then_inc(set_pool, 1)
            pool.memset(eps_ln[:, :], LN_EPS).then_inc(set_pool, 1)
            pool.memset(eps_rms[:, :], RMS_EPS).then_inc(set_pool, 1)
            pool.wait_ge(set_dve, MAXES)
            pool.partition_all_reduce(bound[:, 0:NW + 3], bound[:, 0:NW + 3], P, RMAX).then_inc(set_pool, 1)

            def pre_stats(t, _):
                pool.wait_ge(*pre_dve.done(t, "aggr"))
                nc.gpsimd.tensor_tensor(ve1[:, :], mv1[:, :, 1], eps_ln[:, :], ALU.add).then_inc(pre_pool.sem, 1)
                pool.wait_ge(*pre_pool.done(t, "eps"))
                nc.gpsimd.tensor_tensor(rs1[:, :], ve1[:, :], half, ALU.pow).then_inc(pre_pool.sem, 1)

            def mix_decay(t, h):
                pool.wait_ge(*mix_dve.done(t, f"pp_{h}"))
                nc.gpsimd.tensor_tensor(e1[:, :, :], wkv[:, 0, :, 0:T], wkv[:, 0, :, 1:T + 1], ALU.subtract).then_inc(mix_pool.sem, 1)
                nc.gpsimd.tensor_tensor(e2[:, :, :], k32[:, HF * h:HF * h + HF, :], wkv[:, 0, :, 1:T + 1], ALU.subtract)\
                    .then_inc(mix_pool.sem, 1)

            def mix_sum(t, h):
                pool.wait_ge(*mix_dve.done(t, f"b_{h}"))
                pool.wait_ge(*mix_act.done(t, f"r_{h}"))
                nc.gpsimd.tensor_tensor(zz[:, :, :], wkv[:, 2, :, 0:T], zz[:, :, :], ALU.add).then_inc(mix_pool.sem, 1)

            def att_stats(t, _):
                pool.wait_ge(*att_dve.done(t, "var"))
                nc.gpsimd.tensor_tensor(rs2[:, :, :], var2[:, :, :], half4[:, :, :], ALU.pow).then_inc(att_pool.sem, 1)

            def att_rest(t, _):
                for s in range(SUB):
                    pool.wait_ge(*att_dve.done(t, "xn", s))
                    nc.gpsimd.tensor_tensor(x2[:, s, :], x2[:, s, :], bo_row[:, :], ALU.add).then_inc(att_pool.sem, 1)

            def split(t, step, dst):
                for b in range(CB):
                    pool.wait_ge(*att_act.done(t, step, 2 * b + 1))
                    nc.gpsimd.tensor_tensor(dst[:, 1, b, :], t32[:, b % 2, :], dst[:, 0, b, :], ALU.subtract).then_inc(att_pool.sem, 1)

            def att_q(t, _):
                split(t, "q", qo16)

            def att_up(t, _):
                split(t, "k", k16)

            def att_square(t, _):
                pool.wait_ge(*att_act.done(t, "sq"))
                nc.gpsimd.tensor_tensor(ve3[:, :], msq[:, :], eps_rms[:, :], ALU.add).then_inc(att_pool.sem, 1)
                pool.wait_ge(*att_pool.done(t, "rms", 0))
                nc.gpsimd.tensor_tensor(rs3[:, :], ve3[:, :], half, ALU.pow).then_inc(att_pool.sem, 1)

            def moe_acc(t, _):
                if t.back(1):
                    pool.wait_ge(*stored.done(t.back(1), "out"))
                for s in range(SUB):
                    nc.gpsimd.tensor_tensor(acc[:, s, :], x1[t.par][:, s, :], x2[:, s, :], ALU.add).then_inc(acc_pool.sem, 1)

            pipeline(pool, {"pre_stats": pre_stats, "mix_decay": mix_decay, "mix_sum": mix_sum, "att_stats": att_stats,
                            "att_rest": att_rest, "att_q": att_q, "att_up": att_up, "att_square": att_square,
                            "moe_acc": moe_acc})

        @block.scalar
        def _(act):
            act.wait_ge(const_in, 16 * CONSTS)
            nc.scalar.activation(wcol[:, :], wcol[:, :], ACT.Exp).then_inc(set_act, 1)
            act.wait_ge(set_dve, SCALES)
            for n, name in enumerate(BIG):
                act.wait_ge(split_in[n % 2], 16 * (n // 2 + 1))
                for b in range(CB):
                    if name in TURNED:
                        use = n * CB + b
                        act.wait_ge(set_pe, use + 1)
                        src = bank[use % 2][:, :]
                    else:
                        src = stage[n % 2][:, b, :]
                    nc.scalar.activation(w16[name][:, 0, b, :], src, ACT.Copy, scale=scl[:, n, b:b + 1]).then_inc(set_act, 1)
            for name, src in (("d", d32), ("g", g32)):
                for b in range(CB):
                    nc.scalar.activation(w16[name][:, 0, b, :], src[:, b, :], ACT.Copy, scale=scl[:, IX[name], b:b + 1]).then_inc(set_act, 1)
            nc.scalar.activation(w16["u"][:, 0, :], u32, ACT.Copy, scale=scl[:, IX["u"], 0:1]).then_inc(set_act, 1)
            act.wait_ge(set_dve, SET_DVE)

            def mix_turn(t, _):
                for b in range(2):
                    act.wait_ge(*mix_pe.done(t, "T", b))
                    if b == 0 and t.back(1):
                        act.wait_ge(*mix_pe.done(t.back(1), "O"))
                    nc.scalar.activation(xo16[:, 0, 2 * b:2 * b + 2, :], mix_bank[b][:, :], ACT.Copy, scale=XS)\
                        .then_inc(mix_act.sem, 1)

            def mix_k(t, _):
                for b in range(2):
                    act.wait_ge(*mix_pe.done(t, "K", b))
                    nc.scalar.activation(k32[:, 2 * b:2 * b + 2, :], mix_bank[b][:, :], ACT.Copy, scale=colof["k"])\
                        .then_inc(mix_act.sem, 1)

            def mix_v(t, _):
                for b in range(2):
                    act.wait_ge(*mix_pe.done(t, "V", b))
                    nc.scalar.activation(v32[:, 2 * b:2 * b + 2, :], mix_bank[b][:, :], ACT.Copy, scale=colof["v"])\
                        .then_inc(mix_act.sem, 1)

            def mix_exp(t, h):
                act.wait_ge(*mix_dve.done(t, f"zc_{h}"))
                nc.scalar.activation(zz[:, :, :], zz[:, :, :], ACT.Exp).then_inc(mix_act.sem, 1)
                act.wait_ge(*mix_pool.done(t, f"d1_{h}"))
                for c in range(HF):
                    nc.scalar.activation(e1[:, c, :], e1[:, c, :], ACT.Exp, bias=wcol[:, HF * h + c:HF * h + c + 1])\
                        .then_inc(mix_act.sem, 1)
                act.wait_ge(*mix_pool.done(t, f"d2_{h}"))
                nc.scalar.activation(e2[:, :, :], e2[:, :, :], ACT.Exp).then_inc(mix_act.sem, 1)

            def mix_num(t, h):
                act.wait_ge(*mix_dve.done(t, f"a_{h}"))
                nc.scalar.activation(e1[:, :, :], v32[:, HF * h:HF * h + HF, :], ACT.Tanh, scale=0.5).then_inc(mix_act.sem, 1)

            def mix_split(t, h):
                act.wait_ge(*mix_dve.done(t, f"gated_{h}"))
                nc.scalar.activation(xo16[:, 0, HF * h:HF * h + HF, :], e2[:, :, :], ACT.Copy, scale=colof["o_hi"])\
                    .then_inc(mix_act.sem, 1)

            def att_turn(t, _):
                for b in range(2):
                    act.wait_ge(*att_pe.done(t, f"T{b}"))
                    nc.scalar.activation(ht16[:, 0, 2 * b:2 * b + 2, :], att_bank[ATT_BANK["T", b]][:, :], ACT.Copy, scale=XS)\
                        .then_inc(att_act.sem, 1)

            def att_latent(t, _):
                act.wait_ge(*att_pe.done(t, "D0"))
                nc.scalar.activation(c32[:, :], att_bank[ATT_BANK["D", 0]][:, 0:T], ACT.Identity, bias=bds[:, 0:1], scale=colof["c"])\
                    .then_inc(att_act.sem, 1)
                act.wait_ge(*att_act.done(t, "c", 0))
                nc.scalar.activation(c16[:, :], c32[:, :], ACT.Copy).then_inc(att_act.sem, 1)

            def att_q(t, _):
                heads(t, "Q", "q", qo16, colof["q"], bqs, "q_lo", None)

            def heads(t, use, step, dst, scale, bias, lo, before):
                for b in range(CB):
                    act.wait_ge(*att_pe.done(t, f"{use}{b // 2}"))
                    if b >= 2:
                        act.wait_ge(*att_pool.done(t, lo, b - 2))
                    elif before:
                        act.wait_ge(*att_pool.done(t, before, b + 2))
                    nc.scalar.activation(t32[:, b % 2, :], att_bank[ATT_BANK[use, b // 2]][:, (b % 2) * T:(b % 2) * T + T],
                                         ACT.Identity, bias=bias[:, b:b + 1], scale=scale).then_inc(att_act.sem, 1)
                    act.wait_ge(*att_act.done(t, step, 2 * b))
                    nc.scalar.activation(dst[:, 0, b, :], t32[:, b % 2, :], ACT.Copy).then_inc(att_act.sem, 1)

            def att_up(t, _):
                heads(t, "K", "k", k16, colof["kk"], bks, "k_lo", "q_lo")

            def att_scores(t, k):
                act.wait_ge(*att_pe.done(t, f"S{k}"))
                if k >= 2:
                    act.wait_ge(*att_pe.done(t, f"PV{k - 2}"))
                nc.scalar.activation(pr[:, k % 2, :], att_bank[ATT_BANK["S", k]][:, :], ACT.Exp, scale=colof["soft"])\
                    .then_inc(att_act.sem, 1)

            def att_back(t, _):
                act.wait_ge(*att_dve.done(t, "ot"))
                for h in range(2):
                    nc.scalar.activation(qo16[:, 0, HF * h:HF * h + HF, :], ot32[:, HF * h:HF * h + HF, :], ACT.Copy, scale=colof["ot_hi"])\
                        .then_inc(att_act.sem, 1)

            def att_square(t, _):
                for s in range(SUB):
                    act.wait_ge(*att_dve.done(t, "x2", s))
                    nc.scalar.activation(h_rows[:, s, :], x2[:, s, :], ACT.Square, scale=float(C) ** -0.5,
                                         accum_out=msq[:, s:s + 1]).then_inc(att_act.sem, 1)

            def att_turn2(t, _):
                if t.back(1):
                    act.wait_ge(*moe_pe.done(t.back(1), "u"))
                for b in range(2):
                    act.wait_ge(*att_pe.done(t, f"T2{b}"))
                    nc.scalar.activation(h2t[:, 0, 2 * b:2 * b + 2, :], att_bank[ATT_BANK["T2", b]][:, :], ACT.Copy, scale=XS)\
                        .then_inc(att_act.sem, 1)

            def moe_gate(t, _):
                act.wait_ge(*gate_dve.done(t, "gsub"))
                nc.scalar.activation(gl[:, :, :], gl[:, :, :], ACT.Exp).then_inc(gate_act.sem, 1)

            pipeline(act, {"mix_turn": mix_turn, "mix_k": mix_k, "mix_v": mix_v, "mix_exp": mix_exp,
                           "mix_num": mix_num, "mix_split": mix_split, "att_turn": att_turn,
                           "att_latent": att_latent, "att_q": att_q, "att_up": att_up,
                           "att_scores": att_scores, "att_back": att_back, "att_square": att_square,
                           "att_turn2": att_turn2, "moe_gate": moe_gate})

        @block.vector
        def _(dve):
            count = [0]

            def link(ins):
                count[0] += 1
                ins.then_inc(set_dve, 1)
                dve.wait_ge(set_dve, count[0])

            def mark(ins):
                count[0] += 1
                ins.then_inc(set_dve, 1)

            V = nc.vector
            mark(V.memset(mx[:, :, :], 0.0))
            mark(V.memset(ones4[:, :], 1.0))
            mark(V.memset(vp[:, :, HD], 1.0))
            mark(V.memset(carry[0][:, 0, :], NEG_INF))
            mark(V.memset(carry[1][:, 0, :], NEG_INF))
            mark(V.memset(carry[0][:, 1:3, :], 0.0))
            link(V.memset(carry[1][:, 1:3, :], 0.0))
            assert count[0] == MAX_DONE
            for n, name in enumerate(BIG):
                dve.wait_ge(max_in[n % 2], 16 * (n // 2 + 1))
                mark(V.tensor_reduce(mx[:, n, :], stage[n % 2], AX, ALU.max, apply_absolute_value=True))
            dve.wait_ge(smalls_in, 16 * 7)
            mark(V.tensor_reduce(mx[:, IX["d"], :], d32, AX, ALU.max, apply_absolute_value=True))
            mark(V.tensor_reduce(mx[:, IX["g"], :], g32, AX, ALU.max, apply_absolute_value=True))
            mark(V.tensor_reduce(mx[:, IX["u"], 0:1], u32, AX, ALU.max, apply_absolute_value=True))
            dve.wait_ge(const_in, 16 * CONSTS)
            mark(V.tensor_reduce(mx[:, NW, 0:1], bqcol[:, :], AX, ALU.max, apply_absolute_value=True))
            mark(V.tensor_reduce(mx[:, NW + 1, 0:1], bdcol[:, :], AX, ALU.max, apply_absolute_value=True))
            mark(V.tensor_reduce(mx[:, NW + 2, 0:1], bkcol[:, :], AX, ALU.max, apply_absolute_value=True))
            link(V.tensor_reduce(mx[:, NW + 2, 1:2], bvcol[:, :], AX, ALU.max, apply_absolute_value=True))
            gamma_of = {"q": 0, "d": 0, "g": 1} | {f"e{e}": 1 for e in range(E)}
            for name, which in gamma_of.items():
                mark(V.tensor_tensor(mx[:, IX[name], :], mx[:, IX[name], :], gam[:, which, :], ALU.mult))
            dve.wait_ge(set_dve, count[0])
            mark(V.tensor_reduce(bound[:, 0:NW + 3], mx[:, :, :], AX, ALU.max, apply_absolute_value=True))
            assert count[0] == MAXES
            dve.wait_ge(set_pool, 4)
            bb = {"o": NW + 3, "c": NW + 4, "q": NW + 5, "kv": NW + 6}

            def bcol(n):
                return bound[:, n:n + 1]

            link(V.tensor_scalar(bcol(bb["o"]), bcol(IX["r"]), float(C), None, ALU.mult))
            link(V.scalar_tensor_tensor(out=bcol(bb["c"]), in0=bcol(IX["d"]), scalar=float(C), in1=bcol(NW + 1), op0=ALU.mult, op1=ALU.add))
            link(V.scalar_tensor_tensor(out=bcol(bb["q"]), in0=bcol(IX["q"]), scalar=float(C), in1=bcol(NW), op0=ALU.mult, op1=ALU.add))
            link(V.tensor_tensor(bcol(bb["kv"]), bcol(bb["c"]), bcol(IX["u"]), ALU.mult))
            link(V.scalar_tensor_tensor(out=bcol(bb["kv"]), in0=bcol(bb["kv"]), scalar=float(LAT), in1=bcol(NW + 2), op0=ALU.mult, op1=ALU.add))
            link(V.tensor_scalar(bound[:, bb["q"]:bb["kv"] + 1], bound[:, bb["q"]:bb["kv"] + 1], 16.0, None, ALU.max))
            mark(V.tensor_scalar(pw2[:, 0:NW], bound[:, 0:NW], 1e-30, None, ALU.max))
            link(V.tensor_scalar(pw2[:, NW:NW + 4], bound[:, NW + 3:NW + 7], 1e-30, None, ALU.max))
            link(V.tensor_scalar(pw2[:, :].bitcast(I32), pw2[:, :].bitcast(I32), 0x7F800000, None, ALU.bitwise_and))
            link(V.reciprocal(inv[:, :], pw2[:, :]))
            O_, C_, Q_, K_ = NW, NW + 1, NW + 2, NW + 3

            def p(n):
                n = IX[n] if isinstance(n, str) else n
                return pw2[:, n:n + 1]

            def i_(n):
                return inv[:, n:n + 1]

            for n in range(NW):
                mark(V.tensor_scalar(scl[:, n, :], ones4[:, :], i_(n), 2.0 ** 14, ALU.mult, ALU.mult))
            dve.wait_ge(set_dve, count[0])
            for name, which in gamma_of.items():
                mark(V.tensor_tensor(scl[:, IX[name], :], scl[:, IX[name], :], gam[:, which, :], ALU.mult))

            def product(dst, a, b, factor):
                mark(V.tensor_scalar(dst, a, b, factor, ALU.mult, ALU.mult))

            def times(dst, a, factor):
                mark(V.tensor_scalar(dst, a, factor, None, ALU.mult))

            times(colof["k"], p("k"), 2.0 ** -25)
            times(colof["v"], p("r"), 2.0 ** -25)
            product(colof["o"], p(O_), p("o1"), 2.0 ** -28)
            times(colof["o_hi"], i_(O_), 2.0 ** 13)
            product(colof["c"], i_(C_), p("d"), 2.0 ** -11)
            product(colof["q"], i_(Q_), p("q"), 2.0 ** -14)
            product(colof["t0"], p(C_), p("u"), 2.0 ** -17)
            product(colof["vv"], p(C_), p("u"), 2.0 ** -28)
            product(colof["soft"], p(Q_), p(K_), 2.0 ** -22 * float(HD) ** -0.5)
            times(colof["ot_hi"], i_(K_), 2.0 ** 14)
            product(colof["x2"], p(K_), p("o2"), 2.0 ** -28)
            times(colof["g"], p("g"), 2.0 ** -25)
            for s in range(SUB):
                times(ee[:, s, :], pw2[:, IX["e0"]:IX["e0"] + E], 2.0 ** -25)
            times(colof["t1"], i_(Q_), 2.0 ** 11)
            times(colof["t2"], i_(K_), 2.0 ** 11)
            times(colof["t3"], i_(C_), 2.0 ** 14)
            dve.wait_ge(set_dve, count[0])
            mark(V.tensor_tensor(colof["kk"], colof["t0"], i_(K_), ALU.mult))
            mark(V.tensor_scalar(bqs[:, :], bqcol[:, :], colof["t1"], None, ALU.mult))
            mark(V.tensor_scalar(bks[:, :], bkcol[:, :], colof["t2"], None, ALU.mult))
            mark(V.tensor_scalar(bds[:, :], bdcol[:, :], colof["t3"], None, ALU.mult))
            dve.wait_ge(set_act, 1)
            link(V.tensor_scalar(wcol[:, :], wcol[:, :], -1.0, None, ALU.mult))
            assert count[0] == SCALES, count[0]
            for n, name in enumerate(BIG):
                for b in range(CB):
                    src = bank[(n * CB + b) % 2][:, :] if name in TURNED else stage[n % 2][:, b, :]
                    dve.wait_ge(set_act, 1 + n * CB + b + 1)
                    mark(V.scalar_tensor_tensor(out=w16[name][:, 1, b, :], in0=src, scalar=scl[:, n, b:b + 1],
                                                in1=w16[name][:, 0, b, :], op0=ALU.mult, op1=ALU.subtract))
                assert count[0] == split_done(n)
            done = 1 + len(BIG) * CB
            for name, src in (("d", d32), ("g", g32)):
                for b in range(CB):
                    done += 1
                    dve.wait_ge(set_act, done)
                    mark(V.scalar_tensor_tensor(out=w16[name][:, 1, b, :], in0=src[:, b, :], scalar=scl[:, IX[name], b:b + 1],
                                                in1=w16[name][:, 0, b, :], op0=ALU.mult, op1=ALU.subtract))
            dve.wait_ge(set_act, done + 1)
            link(V.scalar_tensor_tensor(out=w16["u"][:, 1, :], in0=u32, scalar=scl[:, IX["u"], 0:1],
                                        in1=w16["u"][:, 0, :], op0=ALU.mult, op1=ALU.subtract))
            assert count[0] == SET_DVE, count[0]

            def lo(out_, in_, scale, hi):
                return V.scalar_tensor_tensor(out=out_, in0=in_, scalar=scale, in1=hi, op0=ALU.mult, op1=ALU.subtract)

            def pre_stats(t, _):
                dve.wait_ge(*x_in.done(t, "x"))
                for s in range(SUB):
                    V.bn_stats(st1[:, s, :], xk_rows[:, s, :]).then_inc(pre_dve.sem, 1)
                dve.wait_ge(*pre_dve.done(t, "stats"))
                V.memset(idle[:, :], 0.0).then_inc(pre_dve.sem, 1)
                for s in range(SUB):
                    V.bn_aggr(mv1[:, s, :], st1[:, s, :]).then_inc(pre_dve.sem, 1)

            def pre_norm(t, _):
                dve.wait_ge(*pre_pool.done(t, "rstd"))
                for s in range(SUB):
                    V.tensor_scalar(xk_rows[:, s, :], xk_rows[:, s, :], mv1[:, s, 0:1], rs1[:, s:s + 1],
                                    ALU.subtract, ALU.mult).then_inc(pre_dve.sem, 1)

            def mix_turn(t, _):
                for b in range(2):
                    dve.wait_ge(*mix_act.done(t, "x_hi", b))
                    lo(xo16[:, 1, 2 * b:2 * b + 2, :], mix_bank[b][:, :], XS, xo16[:, 0, 2 * b:2 * b + 2, :]).then_inc(mix_dve.sem, 1)

            def mix_decay(t, h):
                V.tensor_copy(wkv[:, :, :, 0], carry[t.par][:, :, HF * h:HF * h + HF]).then_inc(mix_dve.sem, 1)
                dve.wait_ge(*mix_act.done(t, "k", h))
                dve.wait_ge(*mix_dve.done(t, f"carry_{h}"))
                for c in range(HF):
                    V.tensor_tensor_scan(wkv[:, 0, c, 1:T + 1], wcol[:, HF * h + c:HF * h + c + 1].to_broadcast([P, T]),
                                         k32[:, HF * h + c, :], wkv[:, 0, c, 0:1], ALU.add, ALU.max).then_inc(mix_dve.sem, 1)
                dve.wait_ge(*mix_dve.done(t, f"pp_{h}"))
                for c in range(HF):
                    V.scalar_tensor_tensor(out=zz[:, c, :], in0=k32[:, HF * h + c, :], scalar=ucol[:, HF * h + c:HF * h + c + 1],
                                           in1=wkv[:, 0, c, 0:T], op0=ALU.add, op1=ALU.subtract).then_inc(mix_dve.sem, 1)
                dve.wait_ge(*mix_dve.done(t, f"z_{h}"))
                V.tensor_scalar(zz[:, :, :], zz[:, :, :], ZMAX, None, ALU.min).then_inc(mix_dve.sem, 1)

            def scan(h, n, src):
                for c in range(HF):
                    V.tensor_tensor_scan(wkv[:, n, c, 1:T + 1], e1[:, c, :], src[:, c, :], wkv[:, n, c, 0:1],
                                         ALU.mult, ALU.add).then_inc(mix_dve.sem, 1)

            def mix_sum(t, h):
                dve.wait_ge(*mix_act.done(t, f"e2_{h}"))
                scan(h, 2, e2)

            def mix_scan(t, h):
                dve.wait_ge(*mix_act.done(t, "v", h))
                V.tensor_tensor(ev[:, :, :], e2[:, :, :], v32[:, HF * h:HF * h + HF, :], ALU.mult).then_inc(mix_dve.sem, 1)
                dve.wait_ge(*mix_dve.done(t, f"ev_{h}"))
                scan(h, 1, ev)

            def mix_num(t, h):
                vh = v32[:, HF * h:HF * h + HF, :]
                prev_a, prev_b = wkv[:, 1, :, 0:T], wkv[:, 2, :, 0:T]
                dve.wait_ge(*mix_dve.done(t, f"a_{h}"))
                V.tensor_copy(carry[t.par][:, :, HF * h:HF * h + HF], wkv[:, :, :, T]).then_inc(mix_dve.sem, 1)
                V.tensor_tensor(e2[:, :, :], prev_b, vh, ALU.mult).then_inc(mix_dve.sem, 1)
                dve.wait_ge(*mix_dve.done(t, f"bv_{h}"))
                V.tensor_tensor(e2[:, :, :], prev_a, e2[:, :, :], ALU.subtract).then_inc(mix_dve.sem, 1)

            def mix_rec(t, n):
                h, c = n // HF, n % HF
                dve.wait_ge(*mix_pool.done(t, f"den_{h}"))
                V.reciprocal(zz[:, c, :], zz[:, c, :]).then_inc(mix_dve.sem, 1)

            def mix_gate(t, h):
                vh = v32[:, HF * h:HF * h + HF, :]
                dve.wait_ge(*mix_dve.done(t, f"num_{h}"))
                V.tensor_tensor(e2[:, :, :], e2[:, :, :], zz[:, :, :], ALU.mult).then_inc(mix_dve.sem, 1)
                dve.wait_ge(*mix_dve.done(t, f"frac_{h}"))
                V.tensor_tensor(e2[:, :, :], e2[:, :, :], vh, ALU.add).then_inc(mix_dve.sem, 1)
                dve.wait_ge(*mix_dve.done(t, f"y_{h}"))
                dve.wait_ge(*mix_act.done(t, f"th_{h}"))
                V.scalar_tensor_tensor(out=e2[:, :, :], in0=e1[:, :, :], scalar=1.0, in1=e2[:, :, :],
                                       op0=ALU.add, op1=ALU.mult).then_inc(mix_dve.sem, 1)

            def mix_split(t, h):
                dve.wait_ge(*mix_act.done(t, f"o_hi_{h}"))
                lo(xo16[:, 1, HF * h:HF * h + HF, :], e2[:, :, :], colof["o_hi"], xo16[:, 0, HF * h:HF * h + HF, :])\
                    .then_inc(mix_dve.sem, 1)

            def mix_project(t, _):
                dve.wait_ge(*res_in.done(t, "x"))
                for s in range(SUB):
                    dve.wait_ge(*mix_pe.done(t, "O", s))
                    V.scalar_tensor_tensor(out=x1[t.par][:, s, :], in0=mix_bank[s][:, :], scalar=colof["o"],
                                           in1=x1[t.par][:, s, :], op0=ALU.mult, op1=ALU.add).then_inc(mix_dve.sem, 1)

            def att_stats(t, _):
                xa = x1[t.par]
                for s in range(SUB):
                    dve.wait_ge(*mix_dve.done(t, "x1", s))
                    V.bn_stats(st2[:, s, :], xa[:, s, :]).then_inc(att_dve.sem, 1)
                dve.wait_ge(*att_dve.done(t, "stats"))
                V.memset(idle[:, :], 0.0).then_inc(att_dve.sem, 1)
                for s in range(SUB):
                    V.bn_aggr(mv2[:, s, :], st2[:, s, :]).then_inc(att_dve.sem, 1)
                dve.wait_ge(*att_dve.done(t, "aggr"))
                V.tensor_scalar(var2[:, 0, :], mv2[:, :, 1], LN_EPS, None, ALU.add).then_inc(att_dve.sem, 1)
                V.tensor_scalar(var2[:, 1, :], mv2[:, :, 1], 1.0 + RMS_EPS, LN_EPS * RMS_EPS, ALU.mult, ALU.add).then_inc(att_dve.sem, 1)

            def att_norm(t, _):
                xa = x1[t.par]
                dve.wait_ge(*att_pool.done(t, "rstd"))
                for s in range(SUB):
                    V.tensor_scalar(h_rows[:, s, :], xa[:, s, :], mv2[:, s, 0:1], rs2[:, 1, s:s + 1],
                                    ALU.subtract, ALU.mult).then_inc(att_dve.sem, 1)

            def att_rest(t, _):
                xa = x1[t.par]
                if t.back(1):
                    dve.wait_ge(*acc_pool.done(t.back(1), "acc"))
                for s in range(SUB):
                    V.tensor_scalar(x2[:, s, :], xa[:, s, :], mv2[:, s, 0:1], rs2[:, 0, s:s + 1],
                                    ALU.subtract, ALU.mult).then_inc(att_dve.sem, 1)

            def att_turn(t, _):
                for b in range(2):
                    dve.wait_ge(*att_act.done(t, "h_hi", b))
                    lo(ht16[:, 1, 2 * b:2 * b + 2, :], att_bank[ATT_BANK["T", b]][:, :], XS, ht16[:, 0, 2 * b:2 * b + 2, :])\
                        .then_inc(att_dve.sem, 1)

            def att_latent(t, _):
                dve.wait_ge(*att_act.done(t, "c"))
                V.tensor_tensor(c16[LAT:2 * LAT, :], c32[LAT:2 * LAT, :], c16[LAT:2 * LAT, :], ALU.subtract).then_inc(att_dve.sem, 1)

            def att_up(t, _):
                for b in range(CB):
                    dve.wait_ge(*att_pe.done(t, f"V{b // 2}"))
                    V.tensor_scalar(va32[:, b, :], att_bank[ATT_BANK["V", b // 2]][:, (b % 2) * T:(b % 2) * T + T],
                                    colof["vv"], bvcol[:, b:b + 1], ALU.mult, ALU.add).then_inc(att_dve.sem, 1)

            def att_stack(t, _):
                dve.wait_ge(*att_act.done(t, "k"))
                for f in range(4):
                    for n in (0, 2):
                        V.tensor_copy(ks[n * HD:(n + 1) * HD, f * CB:(f + 1) * CB, :],
                                      k16[f * HD:(f + 1) * HD, 0]).then_inc(att_dve.sem, 1)

            def att_vt(t, _):
                dve.wait_ge(*att_dve.done(t, "v"))
                V.transpose(vp[:, :, 0:HD], va32[:, :, :].rearrange("p b (j g) -> p g (b j)", g=G)).then_inc(att_dve.sem, 1)

            def att_max(t, n):
                for k in range(4 * n, 4 * n + 4):
                    dve.wait_ge(*att_pe.done(t, f"M{k}"))
                    V.tensor_reduce(mcol[:, 4 * k:4 * k + 4], att_bank[ATT_BANK["M", k]][:, :].rearrange("p (g x) -> p g x", g=4),
                                    AX, ALU.max).then_inc(att_dve.sem, 1)

            def att_m(t, _):
                dve.wait_ge(*att_dve.done(t, "smax"))
                V.tensor_scalar(m16[:, 0, :], mcol[:, :], -2.0 ** -14, None, ALU.mult).then_inc(att_dve.sem, 1)
                dve.wait_ge(*att_dve.done(t, "m_hi"))
                lo(m16[:, 1, :], mcol[:, :], -2.0 ** -14, m16[:, 0, :]).then_inc(att_dve.sem, 1)

            def att_probs(t, k):
                pv = att_bank[ATT_BANK["PV", k]][:, 0:4 * (HD + 1)].rearrange("p (g d) -> p g d", g=4)
                dve.wait_ge(*att_pe.done(t, f"PV{k}"))
                V.reciprocal(rden[:, 4 * k:4 * k + 4], pv[:, :, HD]).then_inc(att_dve.sem, 1)
                dve.wait_ge(*att_dve.done(t, "norm", 2 * k))
                V.tensor_tensor(on[:, 4 * k:4 * k + 4, :], pv[:, :, 0:HD],
                                rden[:, 4 * k:4 * k + 4].unsqueeze(2).to_broadcast([P, 4, HD]), ALU.mult).then_inc(att_dve.sem, 1)

            def att_back(t, _):
                dve.wait_ge(*att_dve.done(t, "norm"))
                V.transpose(ot32.rearrange("p b (j g) -> p g (b j)", g=G), on[:, :, :]).then_inc(att_dve.sem, 1)
                for h in range(2):
                    dve.wait_ge(*att_act.done(t, "ot_hi", h))
                    lo(qo16[:, 1, HF * h:HF * h + HF, :], ot32[:, HF * h:HF * h + HF, :], colof["ot_hi"],
                       qo16[:, 0, HF * h:HF * h + HF, :]).then_inc(att_dve.sem, 1)

            def att_project(t, _):
                for s in range(SUB):
                    dve.wait_ge(*att_pe.done(t, f"O{s}"))
                    dve.wait_ge(*att_pool.done(t, "xb", s))
                    V.scalar_tensor_tensor(out=x2[:, s, :], in0=att_bank[ATT_BANK["O", s]][:, :], scalar=colof["x2"],
                                           in1=x2[:, s, :], op0=ALU.mult, op1=ALU.add).then_inc(att_dve.sem, 1)

            def att_norm2(t, _):
                dve.wait_ge(*att_pool.done(t, "rms"))
                for s in range(SUB):
                    V.tensor_scalar(h_rows[:, s, :], x2[:, s, :], rs3[:, s:s + 1], None, ALU.mult).then_inc(att_dve.sem, 1)

            def att_turn2(t, _):
                for b in range(2):
                    dve.wait_ge(*att_act.done(t, "h2_hi", b))
                    lo(h2t[:, 1, 2 * b:2 * b + 2, :], att_bank[ATT_BANK["T2", b]][:, :], XS, h2t[:, 0, 2 * b:2 * b + 2, :])\
                        .then_inc(att_dve.sem, 1)

            def moe_gate(t, _):
                def bcast(a):
                    return a[:, :].unsqueeze(2).to_broadcast([P, SUB, E])

                dve.wait_ge(*att_pe.done(t, "G0"))
                V.scalar_tensor_tensor(out=gl[:, :, :].rearrange("p s e -> p (s e)"), in0=att_bank[ATT_BANK["G", 0]][:, 0:SUB * E],
                                       scalar=colof["g"], in1=bg_row[:, :, :].rearrange("p s e -> p (s e)"),
                                       op0=ALU.mult, op1=ALU.add).then_inc(gate_dve.sem, 1)
                dve.wait_ge(*gate_dve.done(t, "gl"))
                V.tensor_reduce(gmx[:, :], gl[:, :, :], AX, ALU.max).then_inc(gate_dve.sem, 1)
                dve.wait_ge(*gate_dve.done(t, "gmax"))
                V.tensor_tensor(gl[:, :, :], gl[:, :, :], bcast(gmx), ALU.subtract).then_inc(gate_dve.sem, 1)
                dve.wait_ge(*gate_act.done(t, "ge"))
                V.tensor_reduce(gsum[:, :], gl[:, :, :], AX, ALU.add).then_inc(gate_dve.sem, 1)
                dve.wait_ge(*gate_dve.done(t, "gsum"))
                V.reciprocal(gmx[:, :], gsum[:, :]).then_inc(gate_dve.sem, 1)
                dve.wait_ge(*gate_dve.done(t, "grec"))
                V.tensor_tensor(gl[:, :, :], gl[:, :, :], bcast(gmx), ALU.mult).then_inc(gate_dve.sem, 1)
                dve.wait_ge(*gate_dve.done(t, "gmul"))
                V.tensor_tensor(gates[:, :, :], gl[:, :, :], ee[:, :, :], ALU.mult).then_inc(gate_dve.sem, 1)

            def moe(t, u):
                e, s = u // SUB, u % SUB
                if u == 0:
                    dve.wait_ge(*acc_pool.done(t, "acc"))
                    dve.wait_ge(*gate_dve.done(t, "gates"))
                if u >= SUB:
                    dve.wait_ge(*moe_dve.done(t, "u", u - SUB))
                dve.wait_ge(*moe_pe.done(t, "u", u))
                V.scalar_tensor_tensor(out=acc[:, s, :], in0=moe_bank[u % 2][:, :], scalar=gates[:, s, e:e + 1],
                                       in1=acc[:, s, :], op0=ALU.mult, op1=ALU.add).then_inc(moe_dve.sem, 1)

            pipeline(dve, {"pre_stats": pre_stats, "pre_norm": pre_norm, "mix_turn": mix_turn, "mix_decay": mix_decay, "mix_sum": mix_sum, "mix_scan": mix_scan,
                           "mix_num": mix_num, "mix_rec": mix_rec, "mix_gate": mix_gate, "mix_split": mix_split,
                           "mix_project": mix_project, "att_stats": att_stats, "att_norm": att_norm,
                           "att_rest": att_rest, "att_turn": att_turn, "att_latent": att_latent, "att_up": att_up, "att_stack": att_stack, "att_vt": att_vt, "att_max": att_max,
                           "att_m": att_m, "att_probs": att_probs, "att_back": att_back,
                           "att_project": att_project, "att_norm2": att_norm2, "att_turn2": att_turn2,
                           "moe_gate": moe_gate, "moe": moe})

        @block.tensor
        def _(pe):
            PASSES = ((0, 0), (1, 0), (0, 1))

            def product(dst, blocks):
                last = len(blocks) * len(PASSES) - 1
                n = 0
                for left, right in blocks:
                    for a, b in PASSES:
                        ins = nc.tensor.matmul(dst, left(a), right(b), start=(n == 0), stop=(n == last))
                        n += 1
                return ins

            pe.wait_ge(const_in, 16 * CONSTS)
            for n, name in enumerate(BIG):
                if name not in TURNED:
                    continue
                pe.wait_ge(split_in[n % 2], 16 * (n // 2 + 1))
                for b in range(CB):
                    use = n * CB + b
                    if use >= 2:
                        pe.wait_ge(set_dve, SCALES + use - 1)
                    for r in range(CB):
                        ins = nc.tensor.transpose(bank[use % 2][:, r * P:(r + 1) * P], stage[n % 2][:, r, b * P:(b + 1) * P], ident[:, :])
                    ins.then_inc(set_pe, 1)
            pe.wait_ge(set_dve, SET_DVE)
            pe.wait_ge(masks_in, 32)

            def turn(rows_, banks, steps, sem_, waits):
                for b in range(2):
                    waits(b)
                    for c in range(2):
                        for s in range(SUB):
                            ins = nc.tensor.transpose(banks[b][:, c * T + s * P:c * T + (s + 1) * P],
                                                      rows_[:, s, (2 * b + c) * P:(2 * b + c + 1) * P], ident[:, :])
                    ins.then_inc(sem_, 1)

            def mix_free(t, use, k):
                before = {"T": ("O", True), "K": ("T", False), "V": ("K", False), "O": ("V", False)}[use]
                steps, step, n = mix_reader(before[0], k)
                if not before[1]:
                    pe.wait_ge(*steps.done(t, step, n))
                elif t.back(1):
                    pe.wait_ge(*steps.done(t.back(1), step, n))

            def att_free(t, use, k):
                (before, n), earlier = att_before((use, k))
                steps, step, m = att_reader(before, n)
                if not earlier:
                    pe.wait_ge(*steps.done(t, step, m))
                elif t.back(1):
                    pe.wait_ge(*steps.done(t.back(1), step, m))

            def channel(dst, name, blk, src, width=P):
                return product(dst, [(lambda a, kb=kb: w16[name][:, a, kb, blk * width:(blk + 1) * width],
                                      lambda b, kb=kb: src[:, b, kb, :]) for kb in range(CB)])

            def token(dst, name, s, src):
                return product(dst, [(lambda a, kb=kb: src[:, a, kb, s * P:(s + 1) * P],
                                      lambda b, kb=kb: w16[name][:, b, kb, :]) for kb in range(CB)])

            def mix_turn(t, _):
                pe.wait_ge(*pre_dve.done(t, "norm"))
                turn(xk_rows, mix_bank, mix_pe, mix_pe.sem, lambda b: mix_free(t, "T", b))

            def mix_in(t, use, name):
                for b in range(2):
                    mix_free(t, use, b)
                    for c in range(2):
                        ins = channel(mix_bank[b][:, c * T:(c + 1) * T], name, 2 * b + c, xo16)
                    ins.then_inc(mix_pe.sem, 1)

            def mix_k(t, _):
                pe.wait_ge(*mix_dve.done(t, "x_lo"))
                mix_in(t, "K", "k")

            def mix_v(t, _):
                mix_in(t, "V", "r")

            def mix_project(t, _):
                pe.wait_ge(*mix_dve.done(t, "o_lo_1"))
                for s in range(SUB):
                    mix_free(t, "O", s)
                    token(mix_bank[s][:, :], "o1", s, xo16).then_inc(mix_pe.sem, 1)

            def att_turn(t, _):
                pe.wait_ge(*att_dve.done(t, "h"))
                turn(h_rows, [att_bank[ATT_BANK["T", b]] for b in range(2)], att_pe, att_pe.sem, lambda b: att_free(t, "T", b))

            def att_latent(t, _):
                pe.wait_ge(*att_dve.done(t, "h_lo"))
                att_free(t, "D", 0)
                channel(att_bank[ATT_BANK["D", 0]][:, 0:T], "d", 0, ht16).then_inc(att_pe.sem, 1)

            def att_q(t, _):
                for b in range(2):
                    att_free(t, "Q", b)
                    for c in range(2):
                        ins = channel(att_bank[ATT_BANK["Q", b]][:, c * T:(c + 1) * T], "q", 2 * b + c, ht16)
                    ins.then_inc(att_pe.sem, 1)

            def att_up(t, _):
                pe.wait_ge(*att_dve.done(t, "c_lo"))
                for n, use in enumerate("KV"):
                    for b in range(2):
                        att_free(t, use, b)
                        for c in range(2):
                            blk = n * CB + 2 * b + c
                            for a in range(2):
                                ins = nc.tensor.matmul(att_bank[ATT_BANK[use, b]][:, c * T:(c + 1) * T],
                                                       w16["u"][:, a, blk * P:(blk + 1) * P], c16[:, :], start=(a == 0), stop=(a == 1))
                        ins.then_inc(att_pe.sem, 1)

            def group(stacked, n_rows, g):
                return stacked[0:n_rows, :, :].rearrange("p h (j g) -> p g (h j)", j=NJ)[:, g]

            def att_max(t, n):
                if n == 0:
                    pe.wait_ge(*stack_in.done(t, "qk"))
                    pe.wait_ge(*att_dve.done(t, "stack"))
                for k in range(4 * n, 4 * n + 4):
                    att_free(t, "M", k)
                    for n in range(4):
                        ins = nc.tensor.matmul(att_bank[ATT_BANK["M", k]][:, n * P:(n + 1) * P],
                                               group(qs, SCAN_ROWS, 4 * k + n), group(ks, SCAN_ROWS, 4 * k + n), start=True, stop=True)
                    ins.then_inc(att_pe.sem, 1)

            def att_scores(t, k):
                if k == 0:
                    pe.wait_ge(*m_in.done(t, "m"))
                att_free(t, "S", k)
                for n in range(4):
                    ins = nc.tensor.matmul(att_bank[ATT_BANK["S", k]][:, n * P:(n + 1) * P],
                                           group(ks, SCAN_ROWS + 2, 4 * k + n), group(qs, SCAN_ROWS + 2, 4 * k + n), start=True, stop=True)
                ins.then_inc(att_pe.sem, 1)

            def att_probs(t, k):
                if k == 0:
                    pe.wait_ge(*att_dve.done(t, "vt"))
                att_free(t, "PV", k)
                pe.wait_ge(*att_act.done(t, "ex", k))
                for n in range(4):
                    ins = nc.tensor.matmul(att_bank[ATT_BANK["PV", k]][:, n * (HD + 1):(n + 1) * (HD + 1)],
                                           pr[:, k % 2, n * P:(n + 1) * P], vp[:, 4 * k + n, :], start=True, stop=True)
                ins.then_inc(att_pe.sem, 1)

            def att_project(t, _):
                pe.wait_ge(*att_dve.done(t, "ot_lo"))
                for s in range(SUB):
                    att_free(t, "O", s)
                    token(att_bank[ATT_BANK["O", s]][:, :], "o2", s, qo16).then_inc(att_pe.sem, 1)

            def att_turn2(t, _):
                pe.wait_ge(*att_dve.done(t, "h2"))
                turn(h_rows, [att_bank[ATT_BANK["T2", b]] for b in range(2)], att_pe, att_pe.sem, lambda b: att_free(t, "T2", b))

            def att_gate(t, _):
                pe.wait_ge(*att_dve.done(t, "h2_lo"))
                att_free(t, "G", 0)
                for s in range(SUB):
                    ins = token(att_bank[ATT_BANK["G", 0]][:, s * E:(s + 1) * E], "g", s, h2t)
                ins.then_inc(att_pe.sem, 1)

            def moe(t, u):
                if u >= 2:
                    pe.wait_ge(*moe_dve.done(t, "u", u - 2))
                elif t.back(1):
                    pe.wait_ge(*moe_dve.done(t.back(1), "u", 2 * E - 2 + u))
                token(moe_bank[u % 2][:, :], f"e{u // SUB}", u % SUB, h2t).then_inc(moe_pe.sem, 1)

            pipeline(pe, {"mix_turn": mix_turn, "mix_k": mix_k, "mix_v": mix_v, "mix_project": mix_project,
                          "att_turn": att_turn, "att_latent": att_latent, "att_q": att_q, "att_up": att_up, "att_max": att_max, "att_scores": att_scores, "att_probs": att_probs,
                          "att_project": att_project, "att_turn2": att_turn2,
                          "att_gate": att_gate, "moe": moe})


CONSTS = 1 + 5 + 8 + 2 + 1 + SUB
MAX_DONE = 7
MAXES = MAX_DONE + len(BIG) + 7 + (3 + E) + 1
SCALES = MAXES + 10 + NW + (3 + E) + 12 + SUB + 3 + 4 + 1
SET_DVE = SCALES + len(BIG) * CB + 2 * CB + 1


def split_done(n):
    return SCALES + (n + 1) * CB


def masks():
    j = np.arange(T) // G
    same = (j[None, :] == np.arange(NJ)[:, None]).astype(np.float16)
    km = np.repeat((same * np.float16(2.0 ** 15))[:, None, :], H, axis=1).reshape(NJ, H * T)
    qm = np.repeat(((1 - same) * np.float16(-65504.0))[:, None, :], H, axis=1).reshape(NJ, H * T)
    km = np.concatenate([km, np.full((2, H * T), 2.0 ** 14, np.float16)])
    return np.ascontiguousarray(km), np.ascontiguousarray(qm)


_INS = ["attn_x", "attn_Wk", "attn_Wr", "attn_Wo", "attn_time_decay", "attn_time_first", "ffn_gamma1",
        "ffn_Wq", "ffn_bq", "ffn_Wdown", "ffn_bdown", "ffn_Wup", "ffn_bup", "ffn_Wo", "ffn_bo",
        "ffn_gamma2", "ffn_Wg", "ffn_bg", "ffn_We"]


def kernel(**inputs):
    import concourse.bacc as bacc
    from concourse.bass_utils import run_bass_kernel_spmd

    nc = bacc.Bacc("TRN2", target_bir_lowering=False, num_devices=1)
    arrays = {f"in_{n}": np.ascontiguousarray(inputs[f"L0_{n}"]) for n in _INS}
    arrays["in_ident"] = np.eye(P, dtype=np.float32)
    arrays["in_kmask"], arrays["in_qmask"] = masks()
    args = [nc.dram_tensor(n, a.shape, mybir.dt.from_np(a.dtype), kind="ExternalInput").ap() for n, a in arrays.items()]
    out = nc.dram_tensor("result", (B, L, C), F32, kind="ExternalOutput").ap()
    build(nc, *args, out)
    r = run_bass_kernel_spmd(nc, [arrays], core_ids=[0])
    return r.results[0]["result"]
```

```python
from contextlib import ExitStack

import numpy as np

import concourse.bass as bass
from concourse import mybir

P = 128
B, L, C = 2, 4096, 512
T = 256
SUB = T // P
NT = B * L // T
CB = C // P
H, HD = 16, 32
LAT = 64
E = 8
G = 32
NJ = T // G
HF = CB // 2
XS = 2048.0
NEG_INF = -1e38
ZMAX = 87.0
LN_EPS, RMS_EPS = 1e-5, 1e-6
SCAN_ROWS = 3 * HD + NJ

ALU = mybir.AluOpType
ACT = mybir.ActivationFunctionType
AX = mybir.AxisListType.X
F32, F16, I32 = mybir.dt.float32, mybir.dt.float16, mybir.dt.int32
RMAX = bass.bass_isa.ReduceOp.max


class Tile:

    def __init__(self, n, par, chunk):
        self.n, self.par, self.chunk = n, par, chunk

    def back(self, d):
        if isinstance(self.n, int) and self.n < d:
            return None
        return Tile(self.n - d, (self.par - d) % 2, None)


class Steps:

    def __init__(self, sem, unit=1, **counts):
        self.sem, self.unit, self.first, self.total = sem, unit, {}, 0
        for step, count in counts.items():
            self.first[step] = (self.total, count)
            self.total += count

    def done(self, tile, step, k=-1):
        first, count = self.first[step]
        assert k < count
        k = k % count
        return self.sem, tile.n * (self.total * self.unit) + (first + k + 1) * self.unit


BIG = ["k", "r", "o1", "q", "o2"] + [f"e{e}" for e in range(E)]
FIRST = ["k", "r", "o1", "q", "o2", "d", "g", "u"]
TURNED = ("k", "r", "o1")
IX = {name: n for n, name in enumerate(FIRST)}
BQ, BD, BU = 8, 9, 10
O_, C_, Q_, K_ = 8, 9, 10, 11
E0 = 12
IX |= {f"e{e}": E0 + e for e in range(E)}
NW = E0 + E
GAMMA_OF = {"q": 0, "d": 0, "g": 1} | {f"e{e}": 1 for e in range(E)}
SPLITS = [(name, b) for name in BIG[:5] for b in range(CB)] + [("d", b) for b in range(CB)] \
    + [("g", b) for b in range(CB)] + [("u", 0)] + [(name, b) for name in BIG[5:] for b in range(CB)]


def splits_in(i, k):
    if i == 0:
        small = {12: SPLITS[20:24], 13: SPLITS[24:28], 14: SPLITS[28:29]}
        return SPLITS[8 + k:9 + k] if k < 12 else small.get(k, [])
    return SPLITS[29 + 2 * k:31 + 2 * k]


def split_done(name, b=-1):
    return max(n for n, (x, c) in enumerate(SPLITS) if x == name and (b < 0 or c == b)) + 1


ATT_USES = ([("T", 0), ("T", 1), ("D", 0), ("Q", 0), ("Q", 1), ("K", 0), ("K", 1), ("V", 0), ("V", 1),
             ] + [("M", k) for k in range(8)] + [("S", 0)]
            + [x for k in range(7) for x in (("S", k + 1), ("PV", k))] + [("PV", 7)]
            + [("O", 0), ("O", 1), ("T2", 0), ("T2", 1), ("G", 0)])
ATT_RING = 4
ATT_BANK = {use: n % ATT_RING for n, use in enumerate(ATT_USES)}


def att_before(use):
    n = ATT_USES.index(use)
    for m in range(n - 1, -1, -1):
        if ATT_BANK[ATT_USES[m]] == ATT_BANK[use]:
            return ATT_USES[m], False
    for m in range(len(ATT_USES) - 1, -1, -1):
        if ATT_BANK[ATT_USES[m]] == ATT_BANK[use]:
            return ATT_USES[m], True


ORDER = [
    ("moe_acc", 0), ("att_stats", 0), ("moe_gate", 0), ("mix_turn", 0), ("att_norm", 0), ("moe", 0),
    ("moe", 1), ("att_turn", 0), ("att_rest", 0), ("mix_k", 0), ("att_latent", 0), ("att_q", 0),
    ("att_up", 0), ("mix_v", 0), ("mix_decay", 0), ("att_stack", 0), ("moe", 2), ("mix_exp", 0),
    ("mix_sum", 0), ("att_vt", 0), ("moe", 3), ("mix_rec", 0), ("mix_rec", 1), ("mix_scan", 0), ("moe", 4),
    ("att_max", 0), ("att_max", 1), ("moe", 5), ("att_max", 2), ("att_max", 3), ("att_m", 0), ("mix_num", 0),
    ("moe", 6), ("mix_gate", 0), ("moe", 7), ("mix_split", 0), ("mix_decay", 1), ("att_scores", 0),
    ("att_scores", 1), ("moe", 8), ("mix_exp", 1), ("att_probs", 0), ("att_scores", 2), ("att_probs", 1),
    ("mix_sum", 1), ("mix_rec", 2), ("pre_load", 0), ("att_scores", 3), ("moe", 9), ("att_probs", 2),
    ("att_scores", 4), ("att_probs", 3), ("att_scores", 5), ("moe", 10), ("att_probs", 4), ("mix_rec", 3),
    ("att_scores", 6), ("mix_scan", 1), ("att_probs", 5), ("att_scores", 7), ("moe", 11), ("att_probs", 6),
    ("att_probs", 7), ("att_back", 0), ("moe", 12), ("moe", 13), ("mix_num", 1), ("mix_gate", 1),
    ("att_project", 0), ("att_square", 0), ("att_norm2", 0), ("pre_stats", 0), ("mix_split", 1), ("moe", 14),
    ("moe", 15), ("att_turn2", 0), ("moe_store", 0), ("pre_norm", 0), ("mix_project", 0), ("att_gate", 0),
]


def build(nc, x, wk, wr, wo1, decay, first, gamma1, wq, bq, wdown, bdown, wup, bup, wo2, bo, gamma2,
          wg, bg, we, ident_in, kmask_in, qmask_in, out):
    with ExitStack() as ctx:
        def sb(name, shape, dt=F32):
            return ctx.enter_context(nc.sbuf_tensor(name, shape, dt))

        def sem(name):
            return ctx.enter_context(nc.semaphore(name))

        ctx.enter_context(nc.allow_non_contiguous_dma(reason="short columns of constants"))
        bank = [ctx.enter_context(nc.psum_tensor(f"bank{n}", [P, 512], F32)) for n in range(8)]
        moe_bank, mix_bank, att_bank = bank[0:2], bank[2:4], bank[4:8]

        w16 = {name: sb(f"w_{name}", [P, 2, CB, C], F16) for name in BIG}
        w16["d"] = sb("w_d", [P, 2, CB, 2 * LAT], F16)
        w16["g"] = sb("w_g", [P, 2, CB, E], F16)
        w16["u"] = sb("w_u", [P, 2, 2 * C], F16)

        ident = sb("ident", [P, P])
        wcol, ucol = sb("wcol", [P, CB]), sb("ucol", [P, CB])
        gam = sb("gam", [P, 2, CB])
        bqcol, bkcol, bvcol, bdcol = sb("bqcol", [P, CB]), sb("bkcol", [P, CB]), sb("bvcol", [P, CB]), sb("bdcol", [P, 1])
        bqs, bks, bds = sb("bqs", [P, CB]), sb("bks", [P, CB]), sb("bds", [P, 1])
        bo_row, bg_row = sb("bo_row", [P, C]), sb("bg_row", [P, SUB, E])
        mx = sb("mx", [P, NW, CB])
        bound, pw2, inv = sb("bound", [P, NW + 4]), sb("pw2", [P, NW]), sb("inv", [P, NW])
        scl = sb("scl", [P, NW, CB])
        col = sb("col", [P, 24])
        ee = sb("ee", [P, SUB, E])
        half4 = sb("half4", [P, 2, SUB])
        half = half4[:, 0, :]
        eps_ln, eps_rms, idle = sb("eps_ln", [P, SUB]), sb("eps_rms", [P, SUB]), sb("idle", [P, 1])
        ones4 = sb("ones4", [P, CB])
        names = ["k", "v", "o", "o_hi", "c", "q", "kk", "vv", "soft", "ot_hi", "x2", "g", "t0", "t1", "t2", "t3", "t4"]
        colof = {name: col[:, n:n + 1] for n, name in enumerate(names)}

        xk = sb("xk", [P, 1024])
        xk_rows = xk[:, :].rearrange("p (s c) -> p s c", s=SUB)
        k32 = xk[:, :].rearrange("p (b t) -> p b t", b=CB)
        v32 = sb("v32", [P, CB, T])
        xo16 = sb("xo16", [P, 2, CB, T], F16)
        wkv = sb("wkv", [P, 3, HF, T + 1])
        e1, e2, ev, zz = (sb(n, [P, HF, T]) for n in ("e1", "e2", "ev", "zz"))
        carry = [sb(f"carry{b}", [P, 3, CB]) for b in range(B)]
        st1, mv1 = sb("st1", [P, SUB, 6]), sb("mv1", [P, SUB, 2])
        ve1, rs1 = sb("ve1", [P, SUB]), sb("rs1", [P, SUB])
        x1 = [sb(f"x1_{n}", [P, SUB, C]) for n in range(2)]

        x2 = sb("x2", [P, SUB, C])
        hrow = sb("hrow", [P, SUB * C])
        h_rows = hrow[:, :].rearrange("p (s c) -> p s c", s=SUB)
        on = hrow[:, :].rearrange("p (g d) -> p g d", d=HD)
        ht = sb("ht", [P, 1024])
        ht16 = ht[:, :].bitcast(F16).rearrange("p (l b t) -> p l b t", l=2, b=CB)
        ot32 = ht[:, :].rearrange("p (b t) -> p b t", b=CB)
        c32, c16 = sb("c32", [P, T]), sb("c16", [P, T], F16)
        t32 = sb("t32", [P, 2, T])
        qo16 = sb("qo16", [P, 2, CB, T], F16)
        k16 = sb("k16", [P, 2, CB, T], F16)
        va32 = ht[:, :].rearrange("p (b t) -> p b t", b=CB)
        vp = sb("vp", [P, G, HD + 1])
        qs, ks = sb("qs", [P, H, T], F16), sb("ks", [P, H, T], F16)
        pr = sb("pr", [P, 2, 4 * P])
        mcol, m16 = sb("mcol", [P, G]), sb("m16", [P, 2, G], F16)
        rden = sb("rden", [P, G])
        st2, mv2 = sb("st2", [P, SUB, 6]), sb("mv2", [P, SUB, 2])
        var2, rs2 = sb("var2", [P, 2, SUB]), sb("rs2", [P, 2, SUB])
        ve3, rs3 = sb("ve3", [P, SUB]), sb("rs3", [P, SUB])
        msq = sb("msq", [P, SUB])
        gl, gmx, gsum = sb("gl", [P, SUB, E]), sb("gmx", [P, SUB]), sb("gsum", [P, SUB])
        gates = sb("gates", [P, SUB, E])

        h2t = sb("h2t", [P, 2, CB, T], F16)
        acc = sb("acc", [P, SUB, C])

        def as_f32(flat):
            return flat.bitcast(F32).rearrange("p (b c) -> p b c", c=C)

        home = {"k": [as_f32(qs[:, :, :].rearrange("p h t -> p (h t)"))], "r": [as_f32(ks[:, :, :].rearrange("p h t -> p (h t)"))]}
        for name, after in zip(BIG[2:], BIG[3:]):
            home[name] = [as_f32(w16[after][:, :, :, :].rearrange("p l b c -> p (l b c)"))]
        home[BIG[-1]] = [as_f32(h2t[:, :, :, :].rearrange("p l b t -> p (l b t)")), acc[:, :, :]]
        d32 = hrow[:, 0:512].rearrange("p (b c) -> p b c", b=CB)
        g32 = hrow[:, 512:512 + CB * E].rearrange("p (b c) -> p b c", b=CB)
        u32 = x2[:, :, :].rearrange("p s c -> p (s c)")

        def f32_block(name, b):
            if name in ("d", "g"):
                return (d32 if name == "d" else g32)[:, b, :]
            if name == "u":
                return u32
            parts = home[name]
            size = CB // len(parts)
            return parts[b // size][:, b % size, :]

        def w16_block(name, half_, b):
            return w16["u"][:, half_, :] if name == "u" else w16[name][:, half_, b, :]

        def turned(n):
            return bank[n % 2][:, :]

        const_in, smalls_in = sem("const_in"), sem("smalls_in")
        weight_in = {name: sem(f"weight_in_{name}") for name in BIG}
        masks_in = sem("masks_in")
        set_dve, set_act, set_pool = sem("set_dve"), sem("set_act"), sem("set_pool")
        hi_done, lo_done, turn_done = sem("hi_done"), sem("lo_done"), sem("turn_done")

        x_in = Steps(sem("x_in"), 16, x=1)
        res_in = Steps(sem("res_in"), 16, x=1)
        stack_in = Steps(sem("stack_in"), 16, qk=16)
        m_in = Steps(sem("m_in"), 16, m=2)
        stored = Steps(sem("stored"), 16, out=1)
        mix_pe = Steps(sem("mix_pe"), T=2, K=2, V=2, O=2)
        mix_act = Steps(sem("mix_act"), x_hi=2, k=2, v=2, r_0=1, e1_0=2, e2_0=1, th_0=1, o_hi_0=1,
                        r_1=1, e1_1=2, e2_1=1, th_1=1, o_hi_1=1)
        wkv_steps = ("carry", 1), ("pp", 2), ("z", 2), ("zc", 1), ("b", 2), ("rec", 2), ("ev", 1), ("a", 2), ("keep", 1), ("bv", 1), \
            ("num", 1), ("frac", 1), ("y", 1), ("gated", 1), ("o_lo", 1)
        wkv_pool = ("d1", 1), ("d2", 1), ("den", 1)
        pre_dve = Steps(sem("pre_dve"), stats=2, idle=1, aggr=2, norm=2)
        pre_pool = Steps(sem("pre_pool"), eps=1, rstd=1)
        mix_dve = Steps(sem("mix_dve"), x_lo=2,
                        **{f"{s}_{h}": c for h in (0, 1) for s, c in wkv_steps}, x1=2)
        mix_pool = Steps(sem("mix_pool"), **{f"{s}_{h}": c for h in (0, 1) for s, c in wkv_pool})
        att_pe = Steps(sem("att_pe"), **{f"{n}{k}": 1 for n, k in ATT_USES})
        att_act = Steps(sem("att_act"), h_hi=2, c=2, q=8, k=8, ex=8, ot_hi=2, sq=2,
                        h2_hi=2)
        att_dve = Steps(sem("att_dve"), stats=2, idle=1, aggr=2, var=2, h=2, h_lo=2, xn=2, c_lo=1, v=4, stack=8,
                        vt=1, smax=8, m_hi=1, m_lo=1, norm=16, ot=1, ot_lo=2, x2=2, h2=2, h2_lo=2)
        gate_dve = Steps(sem("gate_dve"), gl=1, gmax=1, gsub=1, gsum=1, grec=1, gmul=1, gates=1)
        gate_act = Steps(sem("gate_act"), ge=1)
        att_pool = Steps(sem("att_pool"), rstd=1, xb=2, q_lo=4, k_lo=4, rms=2)
        acc_pool = Steps(sem("acc_pool"), acc=2)
        moe_pe = Steps(sem("moe_pe"), u=2 * E)
        moe_dve = Steps(sem("moe_dve"), u=2 * E)

        def mix_reader(use, k):
            return {"T": (mix_dve, "x_lo", k), "K": (mix_act, "k", k), "V": (mix_act, "v", k),
                    "O": (mix_dve, "x1", k)}[use]

        def att_reader(use, k):
            return {"T": (att_dve, "h_lo", k), "D": (att_act, "c", 0), "Q": (att_act, "q", 4 * k + 2),
                    "K": (att_act, "k", 4 * k + 2), "V": (att_dve, "v", 2 * k + 1),
                    "M": (att_dve, "smax", k), "S": (att_act, "ex", k), "PV": (att_dve, "norm", 2 * k + 1),
                    "O": (att_dve, "x2", k), "T2": (att_dve, "h2_lo", k),
                    "G": (gate_dve, "gl", 0)}[use]

        def pipeline(eng, steps, split=None, between=None):
            def iteration(i, par, chunk):
                flat = isinstance(i, int)
                tiles = {}
                if not flat or i + 1 < NT:
                    tiles["pre"] = Tile(i + 1, 1 - par, chunk + par)
                if not flat or i < NT:
                    tiles["mix"] = Tile(i, par, chunk)
                if not flat or 1 <= i <= NT:
                    tiles["att"] = Tile(i - 1, 1 - par, None)
                if not flat or 2 <= i:
                    tiles["moe"] = Tile(i - 2, par, chunk - 1)
                for name, k in ORDER:
                    stage_name = name.split("_")[0]
                    if split and name == "moe" and flat and i < 2:
                        split(i, k)
                    if name in steps and stage_name in tiles:
                        steps[name](tiles[stage_name], k)

            for name, k in ORDER:
                if name in steps and name.startswith("pre"):
                    steps[name](Tile(0, 0, 0), k)
            if between:
                between()
            for i in range(4):
                iteration(i, i % 2, i // 2)
            with eng.Fori(0, (NT - 6) // 2) as pair:
                for par in range(2):
                    iteration(pair * 2 + (4 + par), par, pair + 2)
            for i in range(NT - 2, NT + 2):
                iteration(i, i % 2, i // 2)

        weight_dram = {"k": wk, "r": wr, "o1": wo1, "q": wq, "o2": wo2}
        weight_dram |= {f"e{e}": we[e] for e in range(E)}
        block = ctx.enter_context(nc.Block())

        def rows(dram, tile):
            view = dram[tile.par].rearrange("(n s p) c -> n p s c", s=SUB, p=P)
            if isinstance(tile.chunk, int):
                return view[tile.chunk]
            return view[bass.ds(tile.chunk, 1)].rearrange("n p s c -> (n p) s c")

        @block.sync
        def _(sp):
            def load_weight(name):
                view = weight_dram[name].rearrange("(b p) c -> p b c", p=P)
                b = 0
                for part in home[name]:
                    sp.dma_start(part, view[:, b:b + part.shape[1], :]).then_inc(weight_in[name], 16)
                    b += part.shape[1]

            for name in FIRST[:5]:
                load_weight(name)
            sp.dma_start(ident[:, :], ident_in).then_inc(const_in, 16)
            for tile_, dram in ((wcol, decay), (ucol, first), (gam[:, 0, :], gamma1), (gam[:, 1, :], gamma2), (bqcol, bq)):
                sp.dma_start(tile_[:, :], dram.rearrange("(b p) -> p b", p=P)).then_inc(const_in, 16)
            bup_v = bup.rearrange("(b f k d) -> k f d b", f=4, k=2, d=HD)
            for f in range(4):
                sp.dma_start(bkcol[f * HD:(f + 1) * HD, :], bup_v[0, f]).then_inc(const_in, 16)
                sp.dma_start(bvcol[f * HD:(f + 1) * HD, :], bup_v[1, f]).then_inc(const_in, 16)
            for n in range(2):
                sp.dma_start(bdcol[n * LAT:(n + 1) * LAT, :], bdown.rearrange("(p a) -> p a", a=1)).then_inc(const_in, 16)
            sp.dma_start(bo_row[:, :], bo.partition_broadcast(P)).then_inc(const_in, 16)
            for s in range(SUB):
                sp.dma_start(bg_row[:, s, :], bg.partition_broadcast(P)).then_inc(const_in, 16)
            for n in range(2):
                sp.dma_start(d32[:, :, n * LAT:(n + 1) * LAT], wdown.rearrange("(b p) c -> p b c", p=P)).then_inc(smalls_in, 16)
                for k in range(2):
                    sp.dma_start(u32[n * LAT:(n + 1) * LAT, k * C:(k + 1) * C].rearrange("p (g d) -> p g d", g=H),
                                 wup.rearrange("l (g k d) -> k l g d", g=H, k=2)[k]).then_inc(smalls_in, 16)
            sp.dma_start(g32, wg.rearrange("(b p) c -> p b c", p=P)).then_inc(smalls_in, 16)
            def rest():
                for e in range(E):
                    load_weight(f"e{e}")
                sp.wait_ge(lo_done, split_done("r"))
                sp.dma_start(ks[3 * HD:SCAN_ROWS + 2, :, :], kmask_in.rearrange("a (h t) -> a h t", h=H)).then_inc(masks_in, 16)
                sp.dma_start(qs[3 * HD:SCAN_ROWS, :, :], qmask_in.rearrange("a (h t) -> a h t", h=H)).then_inc(masks_in, 16)

            def pre_load(t, _):
                if t.back(1):
                    sp.wait_ge(*mix_dve.done(t.back(1), "z_1"))
                    sp.wait_ge(*mix_pool.done(t.back(1), "d2_1"))
                sp.dma_start(xk_rows, rows(x, t)).then_inc(x_in.sem, 16)

            def mix_k(t, _):
                if t.back(2):
                    sp.wait_ge(*acc_pool.done(t.back(2), "acc"))
                sp.dma_start(x1[t.par][:, :, :], rows(x, t)).then_inc(res_in.sem, 16)

            def att_up(t, _):
                for src, dst, name, first in ((qo16, qs, "q", (0, 1)), (k16, ks, "k", ())):
                    rest = 2 if first else 1
                    for f in range(4):
                        for n in first:
                            if f == 0 and n == 0:
                                sp.wait_ge(*att_act.done(t, name))
                            sp.dma_start(dst[n * HD:(n + 1) * HD, f * CB:(f + 1) * CB, :],
                                         src[f * HD:(f + 1) * HD, 0]).then_inc(stack_in.sem, 16)
                    sp.wait_ge(*att_pool.done(t, f"{name}_lo"))
                    for f in range(4):
                        sp.dma_start(dst[rest * HD:(rest + 1) * HD, f * CB:(f + 1) * CB, :],
                                     src[f * HD:(f + 1) * HD, 1]).then_inc(stack_in.sem, 16)

            def att_m(t, _):
                for l, step in enumerate(("m_hi", "m_lo")):
                    sp.wait_ge(*att_dve.done(t, step))
                    sp.dma_start(qs[SCAN_ROWS + l:SCAN_ROWS + l + 1, :, :].rearrange("a h (j g) -> a (h j) g", j=NJ), m16[:, l, :])\
                        .then_inc(m_in.sem, 16)

            def moe_store(t, _):
                sp.wait_ge(*moe_dve.done(t, "u"))
                sp.dma_start(rows(out, t), acc[:, :, :]).then_inc(stored.sem, 16)

            pipeline(sp, {"pre_load": pre_load, "mix_k": mix_k, "att_up": att_up, "att_m": att_m,
                          "moe_store": moe_store}, between=rest)
            sp.wait_ge(*stored.done(Tile(NT - 1, 1, 0), "out"))

        @block.gpsimd
        def _(pool):
            pool.memset(half4[:, :, :], -0.5).then_inc(set_pool, 1)
            pool.memset(eps_ln[:, :], LN_EPS).then_inc(set_pool, 1)
            pool.memset(eps_rms[:, :], RMS_EPS).then_inc(set_pool, 1)
            pool.wait_ge(set_dve, MAXES)
            pool.partition_all_reduce(bound[:, 0:E0], bound[:, 0:E0], P, RMAX).then_inc(set_pool, 1)

            def split(i, k):
                if (i, k) == (0, 15):
                    pool.wait_ge(set_dve, EXPERT_MAXES)
                    pool.partition_all_reduce(bound[:, E0:NW], bound[:, E0:NW], P, RMAX).then_inc(set_pool, 1)

            def pre_stats(t, _):
                pool.wait_ge(*pre_dve.done(t, "aggr"))
                nc.gpsimd.tensor_tensor(ve1[:, :], mv1[:, :, 1], eps_ln[:, :], ALU.add).then_inc(pre_pool.sem, 1)
                pool.wait_ge(*pre_pool.done(t, "eps"))
                nc.gpsimd.tensor_tensor(rs1[:, :], ve1[:, :], half, ALU.pow).then_inc(pre_pool.sem, 1)

            def mix_decay(t, h):
                pool.wait_ge(*mix_dve.done(t, f"pp_{h}"))
                nc.gpsimd.tensor_tensor(e1[:, :, :], wkv[:, 0, :, 0:T], wkv[:, 0, :, 1:T + 1], ALU.subtract).then_inc(mix_pool.sem, 1)
                nc.gpsimd.tensor_tensor(e2[:, :, :], k32[:, HF * h:HF * h + HF, :], wkv[:, 0, :, 1:T + 1], ALU.subtract)\
                    .then_inc(mix_pool.sem, 1)

            def mix_sum(t, h):
                pool.wait_ge(*mix_dve.done(t, f"b_{h}"))
                pool.wait_ge(*mix_act.done(t, f"r_{h}"))
                nc.gpsimd.tensor_tensor(zz[:, :, :], wkv[:, 2, :, 0:T], zz[:, :, :], ALU.add).then_inc(mix_pool.sem, 1)

            def att_stats(t, _):
                pool.wait_ge(*att_dve.done(t, "var"))
                nc.gpsimd.tensor_tensor(rs2[:, :, :], var2[:, :, :], half4[:, :, :], ALU.pow).then_inc(att_pool.sem, 1)

            def att_rest(t, _):
                for s in range(SUB):
                    pool.wait_ge(*att_dve.done(t, "xn", s))
                    nc.gpsimd.tensor_tensor(x2[:, s, :], x2[:, s, :], bo_row[:, :], ALU.add).then_inc(att_pool.sem, 1)

            def lo_half(t, step, dst):
                for b in range(CB):
                    pool.wait_ge(*att_act.done(t, step, 2 * b + 1))
                    nc.gpsimd.tensor_tensor(dst[:, 1, b, :], t32[:, b % 2, :], dst[:, 0, b, :], ALU.subtract).then_inc(att_pool.sem, 1)

            def att_q(t, _):
                lo_half(t, "q", qo16)

            def att_up(t, _):
                lo_half(t, "k", k16)

            def att_square(t, _):
                pool.wait_ge(*att_act.done(t, "sq"))
                nc.gpsimd.tensor_tensor(ve3[:, :], msq[:, :], eps_rms[:, :], ALU.add).then_inc(att_pool.sem, 1)
                pool.wait_ge(*att_pool.done(t, "rms", 0))
                nc.gpsimd.tensor_tensor(rs3[:, :], ve3[:, :], half, ALU.pow).then_inc(att_pool.sem, 1)

            def moe_acc(t, _):
                if t.back(1):
                    pool.wait_ge(*stored.done(t.back(1), "out"))
                else:
                    pool.wait_ge(lo_done, len(SPLITS))
                for s in range(SUB):
                    nc.gpsimd.tensor_tensor(acc[:, s, :], x1[t.par][:, s, :], x2[:, s, :], ALU.add).then_inc(acc_pool.sem, 1)

            pipeline(pool, {"pre_stats": pre_stats, "mix_decay": mix_decay, "mix_sum": mix_sum, "att_stats": att_stats,
                            "att_rest": att_rest, "att_q": att_q, "att_up": att_up, "att_square": att_square,
                            "moe_acc": moe_acc}, split)

        @block.scalar
        def _(act):
            act.wait_ge(const_in, 16 * CONSTS)
            nc.scalar.activation(wcol[:, :], wcol[:, :], ACT.Exp).then_inc(set_act, 1)
            def split_block(n):
                name, b = SPLITS[n]
                if name in BIG:
                    act.wait_ge(weight_in[name], 16 * len(home[name]))
                    before = BIG.index(name) - 1
                    if before >= 2 and b == 0:
                        act.wait_ge(lo_done, split_done(BIG[before]))
                if name in TURNED:
                    act.wait_ge(turn_done, n + 1)
                nc.scalar.activation(w16_block(name, 0, b), turned(n) if name in TURNED else f32_block(name, b), ACT.Copy,
                                     scale=scl[:, IX[name], b:b + 1]).then_inc(hi_done, 1)

            def split(i, k):
                for name, b in splits_in(i, k):
                    if (name, b) == ("e0", 0):
                        act.wait_ge(set_dve, SET_DVE)
                    split_block(SPLITS.index((name, b)))

            act.wait_ge(set_dve, SCALES)
            for n in range(2 * CB):
                split_block(n)

            def mix_turn(t, _):
                for b in range(2):
                    act.wait_ge(*mix_pe.done(t, "T", b))
                    if b == 0 and t.back(1):
                        act.wait_ge(*mix_pe.done(t.back(1), "O"))
                    nc.scalar.activation(xo16[:, 0, 2 * b:2 * b + 2, :], mix_bank[b][:, :], ACT.Copy, scale=XS)\
                        .then_inc(mix_act.sem, 1)

            def mix_k(t, _):
                for b in range(2):
                    act.wait_ge(*mix_pe.done(t, "K", b))
                    nc.scalar.activation(k32[:, 2 * b:2 * b + 2, :], mix_bank[b][:, :], ACT.Copy, scale=colof["k"])\
                        .then_inc(mix_act.sem, 1)

            def mix_v(t, _):
                for b in range(2):
                    act.wait_ge(*mix_pe.done(t, "V", b))
                    nc.scalar.activation(v32[:, 2 * b:2 * b + 2, :], mix_bank[b][:, :], ACT.Copy, scale=colof["v"])\
                        .then_inc(mix_act.sem, 1)

            def mix_exp(t, h):
                act.wait_ge(*mix_dve.done(t, f"zc_{h}"))
                nc.scalar.activation(zz[:, :, :], zz[:, :, :], ACT.Exp).then_inc(mix_act.sem, 1)
                act.wait_ge(*mix_pool.done(t, f"d1_{h}"))
                for c in range(HF):
                    nc.scalar.activation(e1[:, c, :], e1[:, c, :], ACT.Exp, bias=wcol[:, HF * h + c:HF * h + c + 1])\
                        .then_inc(mix_act.sem, 1)
                act.wait_ge(*mix_pool.done(t, f"d2_{h}"))
                nc.scalar.activation(e2[:, :, :], e2[:, :, :], ACT.Exp).then_inc(mix_act.sem, 1)

            def mix_num(t, h):
                act.wait_ge(*mix_dve.done(t, f"a_{h}"))
                nc.scalar.activation(e1[:, :, :], v32[:, HF * h:HF * h + HF, :], ACT.Tanh, scale=0.5).then_inc(mix_act.sem, 1)

            def mix_split(t, h):
                act.wait_ge(*mix_dve.done(t, f"gated_{h}"))
                nc.scalar.activation(xo16[:, 0, HF * h:HF * h + HF, :], e2[:, :, :], ACT.Copy, scale=colof["o_hi"])\
                    .then_inc(mix_act.sem, 1)

            def att_turn(t, _):
                for b in range(2):
                    act.wait_ge(*att_pe.done(t, f"T{b}"))
                    nc.scalar.activation(ht16[:, 0, 2 * b:2 * b + 2, :], att_bank[ATT_BANK["T", b]][:, :], ACT.Copy, scale=XS)\
                        .then_inc(att_act.sem, 1)

            def att_latent(t, _):
                act.wait_ge(*att_pe.done(t, "D0"))
                nc.scalar.activation(c32[:, :], att_bank[ATT_BANK["D", 0]][:, 0:T], ACT.Identity, bias=bds[:, 0:1], scale=colof["c"])\
                    .then_inc(att_act.sem, 1)
                act.wait_ge(*att_act.done(t, "c", 0))
                nc.scalar.activation(c16[:, :], c32[:, :], ACT.Copy).then_inc(att_act.sem, 1)

            def att_q(t, _):
                heads(t, "Q", "q", qo16, colof["q"], bqs, "q_lo", None)

            def heads(t, use, step, dst, scale, bias, lo, before):
                for b in range(CB):
                    act.wait_ge(*att_pe.done(t, f"{use}{b // 2}"))
                    if b >= 2:
                        act.wait_ge(*att_pool.done(t, lo, b - 2))
                    elif before:
                        act.wait_ge(*att_pool.done(t, before, b + 2))
                    nc.scalar.activation(t32[:, b % 2, :], att_bank[ATT_BANK[use, b // 2]][:, (b % 2) * T:(b % 2) * T + T],
                                         ACT.Identity, bias=bias[:, b:b + 1], scale=scale).then_inc(att_act.sem, 1)
                    act.wait_ge(*att_act.done(t, step, 2 * b))
                    nc.scalar.activation(dst[:, 0, b, :], t32[:, b % 2, :], ACT.Copy).then_inc(att_act.sem, 1)

            def att_up(t, _):
                heads(t, "K", "k", k16, colof["kk"], bks, "k_lo", "q_lo")

            def att_scores(t, k):
                act.wait_ge(*att_pe.done(t, f"S{k}"))
                if k >= 2:
                    act.wait_ge(*att_pe.done(t, f"PV{k - 2}"))
                nc.scalar.activation(pr[:, k % 2, :], att_bank[ATT_BANK["S", k]][:, :], ACT.Exp, scale=colof["soft"])\
                    .then_inc(att_act.sem, 1)

            def att_back(t, _):
                act.wait_ge(*att_dve.done(t, "ot"))
                for h in range(2):
                    nc.scalar.activation(qo16[:, 0, HF * h:HF * h + HF, :], ot32[:, HF * h:HF * h + HF, :], ACT.Copy, scale=colof["ot_hi"])\
                        .then_inc(att_act.sem, 1)

            def att_square(t, _):
                for s in range(SUB):
                    act.wait_ge(*att_dve.done(t, "x2", s))
                    nc.scalar.activation(h_rows[:, s, :], x2[:, s, :], ACT.Square, scale=float(C) ** -0.5,
                                         accum_out=msq[:, s:s + 1]).then_inc(att_act.sem, 1)

            def att_turn2(t, _):
                if t.back(1):
                    act.wait_ge(*moe_pe.done(t.back(1), "u"))
                else:
                    act.wait_ge(lo_done, len(SPLITS))
                for b in range(2):
                    act.wait_ge(*att_pe.done(t, f"T2{b}"))
                    nc.scalar.activation(h2t[:, 0, 2 * b:2 * b + 2, :], att_bank[ATT_BANK["T2", b]][:, :], ACT.Copy, scale=XS)\
                        .then_inc(att_act.sem, 1)

            def moe_gate(t, _):
                act.wait_ge(*gate_dve.done(t, "gsub"))
                nc.scalar.activation(gl[:, :, :], gl[:, :, :], ACT.Exp).then_inc(gate_act.sem, 1)

            pipeline(act, {"mix_turn": mix_turn, "mix_k": mix_k, "mix_v": mix_v, "mix_exp": mix_exp,
                           "mix_num": mix_num, "mix_split": mix_split, "att_turn": att_turn,
                           "att_latent": att_latent, "att_q": att_q, "att_up": att_up,
                           "att_scores": att_scores, "att_back": att_back, "att_square": att_square,
                           "att_turn2": att_turn2, "moe_gate": moe_gate}, split)

        @block.vector
        def _(dve):
            count = [0]

            def link(ins):
                count[0] += 1
                ins.then_inc(set_dve, 1)
                dve.wait_ge(set_dve, count[0])

            def mark(ins):
                count[0] += 1
                ins.then_inc(set_dve, 1)

            V = nc.vector
            mark(V.memset(mx[:, :, :], 0.0))
            mark(V.memset(ones4[:, :], 1.0))
            mark(V.memset(vp[:, :, HD], 1.0))
            mark(V.memset(carry[0][:, 0, :], NEG_INF))
            mark(V.memset(carry[1][:, 0, :], NEG_INF))
            mark(V.memset(carry[0][:, 1:3, :], 0.0))
            link(V.memset(carry[1][:, 1:3, :], 0.0))
            assert count[0] == MAX_DONE
            def largest(name):
                dve.wait_ge(weight_in[name], 16 * len(home[name]))
                b = 0
                for part in home[name]:
                    mark(V.tensor_reduce(mx[:, IX[name], b:b + part.shape[1]], part, AX, ALU.max, apply_absolute_value=True))
                    b += part.shape[1]

            def largest_with_gamma(names):
                for name in names:
                    if name in GAMMA_OF:
                        mark(V.tensor_tensor(mx[:, IX[name], :], mx[:, IX[name], :], gam[:, GAMMA_OF[name], :], ALU.mult))

            for name in FIRST[:5]:
                largest(name)
            dve.wait_ge(smalls_in, 16 * 7)
            mark(V.tensor_reduce(mx[:, IX["d"], :], d32, AX, ALU.max, apply_absolute_value=True))
            mark(V.tensor_reduce(mx[:, IX["g"], :], g32, AX, ALU.max, apply_absolute_value=True))
            mark(V.tensor_reduce(mx[:, IX["u"], 0:1], u32, AX, ALU.max, apply_absolute_value=True))
            dve.wait_ge(const_in, 16 * CONSTS)
            mark(V.tensor_reduce(mx[:, BQ, 0:1], bqcol[:, :], AX, ALU.max, apply_absolute_value=True))
            mark(V.tensor_reduce(mx[:, BD, 0:1], bdcol[:, :], AX, ALU.max, apply_absolute_value=True))
            mark(V.tensor_reduce(mx[:, BU, 0:1], bkcol[:, :], AX, ALU.max, apply_absolute_value=True))
            link(V.tensor_reduce(mx[:, BU, 1:2], bvcol[:, :], AX, ALU.max, apply_absolute_value=True))
            largest_with_gamma(FIRST)
            dve.wait_ge(set_dve, count[0])
            mark(V.tensor_reduce(bound[:, 0:E0], mx[:, 0:E0, :], AX, ALU.max, apply_absolute_value=True))
            assert count[0] == MAXES
            dve.wait_ge(set_pool, 4)
            bb = {"o": NW, "c": NW + 1, "q": NW + 2, "kv": NW + 3}

            def bcol(n):
                return bound[:, n:n + 1]

            link(V.tensor_scalar(bcol(bb["o"]), bcol(IX["r"]), float(C), None, ALU.mult))
            link(V.scalar_tensor_tensor(out=bcol(bb["c"]), in0=bcol(IX["d"]), scalar=float(C), in1=bcol(BD), op0=ALU.mult, op1=ALU.add))
            link(V.scalar_tensor_tensor(out=bcol(bb["q"]), in0=bcol(IX["q"]), scalar=float(C), in1=bcol(BQ), op0=ALU.mult, op1=ALU.add))
            link(V.tensor_tensor(bcol(bb["kv"]), bcol(bb["c"]), bcol(IX["u"]), ALU.mult))
            link(V.scalar_tensor_tensor(out=bcol(bb["kv"]), in0=bcol(bb["kv"]), scalar=float(LAT), in1=bcol(BU), op0=ALU.mult, op1=ALU.add))
            link(V.tensor_scalar(bound[:, bb["q"]:bb["kv"] + 1], bound[:, bb["q"]:bb["kv"] + 1], 16.0, None, ALU.max))
            mark(V.tensor_scalar(pw2[:, 0:O_], bound[:, 0:O_], 1e-30, None, ALU.max))
            link(V.tensor_scalar(pw2[:, O_:E0], bound[:, NW:NW + 4], 1e-30, None, ALU.max))

            def powers(lo_, hi_):
                link(V.tensor_scalar(pw2[:, lo_:hi_].bitcast(I32), pw2[:, lo_:hi_].bitcast(I32), 0x7F800000, None, ALU.bitwise_and))
                link(V.reciprocal(inv[:, lo_:hi_], pw2[:, lo_:hi_]))

            powers(0, E0)

            def p(n):
                n = IX[n] if isinstance(n, str) else n
                return pw2[:, n:n + 1]

            def i_(n):
                return inv[:, n:n + 1]

            def scale_weights(names):
                for name in names:
                    mark(V.tensor_scalar(scl[:, IX[name], :], ones4[:, :], i_(IX[name]), 2.0 ** 14, ALU.mult, ALU.mult))
                dve.wait_ge(set_dve, count[0])
                for name in names:
                    if name in GAMMA_OF:
                        mark(V.tensor_tensor(scl[:, IX[name], :], scl[:, IX[name], :], gam[:, GAMMA_OF[name], :], ALU.mult))

            scale_weights(FIRST)

            def product(dst, a, b, factor):
                mark(V.tensor_scalar(dst, a, b, factor, ALU.mult, ALU.mult))

            def times(dst, a, factor):
                mark(V.tensor_scalar(dst, a, factor, None, ALU.mult))

            times(colof["k"], p("k"), 2.0 ** -25)
            times(colof["v"], p("r"), 2.0 ** -25)
            product(colof["o"], p(O_), p("o1"), 2.0 ** -28)
            times(colof["o_hi"], i_(O_), 2.0 ** 13)
            product(colof["c"], i_(C_), p("d"), 2.0 ** -11)
            product(colof["q"], i_(Q_), p("q"), 2.0 ** -14)
            product(colof["t0"], p(C_), p("u"), 2.0 ** -17)
            product(colof["vv"], p(C_), p("u"), 2.0 ** -28)
            product(colof["soft"], p(Q_), p(K_), 2.0 ** -22 * float(HD) ** -0.5)
            times(colof["ot_hi"], i_(K_), 2.0 ** 14)
            product(colof["x2"], p(K_), p("o2"), 2.0 ** -28)
            times(colof["g"], p("g"), 2.0 ** -25)
            times(colof["t1"], i_(Q_), 2.0 ** 11)
            times(colof["t2"], i_(K_), 2.0 ** 11)
            times(colof["t3"], i_(C_), 2.0 ** 14)
            dve.wait_ge(set_dve, count[0])
            mark(V.tensor_tensor(colof["kk"], colof["t0"], i_(K_), ALU.mult))
            mark(V.tensor_scalar(bqs[:, :], bqcol[:, :], colof["t1"], None, ALU.mult))
            mark(V.tensor_scalar(bks[:, :], bkcol[:, :], colof["t2"], None, ALU.mult))
            mark(V.tensor_scalar(bds[:, :], bdcol[:, :], colof["t3"], None, ALU.mult))
            dve.wait_ge(set_act, 1)
            link(V.tensor_scalar(wcol[:, :], wcol[:, :], -1.0, None, ALU.mult))
            assert count[0] == SCALES, count[0]
            def split_block(n):
                name, b = SPLITS[n]
                dve.wait_ge(hi_done, n + 1)
                V.scalar_tensor_tensor(out=w16_block(name, 1, b), in0=turned(n) if name in TURNED else f32_block(name, b),
                                       scalar=scl[:, IX[name], b:b + 1], in1=w16_block(name, 0, b),
                                       op0=ALU.mult, op1=ALU.subtract).then_inc(lo_done, 1)

            def split(i, k):
                for name, b in splits_in(i, k):
                    split_block(SPLITS.index((name, b)))
                if i == 0 and 4 <= k < 4 + E:
                    largest(f"e{k - 4}")
                if i == 0 and k == 4 + E:
                    dve.wait_ge(set_dve, count[0])
                    largest_with_gamma(BIG[5:])
                    dve.wait_ge(set_dve, count[0])
                    mark(V.tensor_reduce(bound[:, E0:NW], mx[:, E0:NW, :], AX, ALU.max, apply_absolute_value=True))
                    assert count[0] == EXPERT_MAXES, count[0]
                if (i, k) == (0, 15):
                    dve.wait_ge(set_pool, 5)
                    link(V.tensor_scalar(pw2[:, E0:NW], bound[:, E0:NW], 1e-30, None, ALU.max))
                    powers(E0, NW)
                    scale_weights(BIG[5:])
                    for s in range(SUB):
                        times(ee[:, s, :], pw2[:, E0:NW], 2.0 ** -25)
                    dve.wait_ge(set_dve, count[0])
                    assert count[0] == SET_DVE, count[0]

            for n in range(2 * CB):
                split_block(n)

            def lo(out_, in_, scale, hi):
                return V.scalar_tensor_tensor(out=out_, in0=in_, scalar=scale, in1=hi, op0=ALU.mult, op1=ALU.subtract)

            def pre_stats(t, _):
                dve.wait_ge(*x_in.done(t, "x"))
                for s in range(SUB):
                    V.bn_stats(st1[:, s, :], xk_rows[:, s, :]).then_inc(pre_dve.sem, 1)
                dve.wait_ge(*pre_dve.done(t, "stats"))
                V.memset(idle[:, :], 0.0).then_inc(pre_dve.sem, 1)
                for s in range(SUB):
                    V.bn_aggr(mv1[:, s, :], st1[:, s, :]).then_inc(pre_dve.sem, 1)

            def pre_norm(t, _):
                dve.wait_ge(*pre_pool.done(t, "rstd"))
                for s in range(SUB):
                    V.tensor_scalar(xk_rows[:, s, :], xk_rows[:, s, :], mv1[:, s, 0:1], rs1[:, s:s + 1],
                                    ALU.subtract, ALU.mult).then_inc(pre_dve.sem, 1)

            def mix_turn(t, _):
                for b in range(2):
                    dve.wait_ge(*mix_act.done(t, "x_hi", b))
                    lo(xo16[:, 1, 2 * b:2 * b + 2, :], mix_bank[b][:, :], XS, xo16[:, 0, 2 * b:2 * b + 2, :]).then_inc(mix_dve.sem, 1)

            def mix_decay(t, h):
                V.tensor_copy(wkv[:, :, :, 0], carry[t.par][:, :, HF * h:HF * h + HF]).then_inc(mix_dve.sem, 1)
                dve.wait_ge(*mix_act.done(t, "k", h))
                dve.wait_ge(*mix_dve.done(t, f"carry_{h}"))
                for c in range(HF):
                    V.tensor_tensor_scan(wkv[:, 0, c, 1:T + 1], wcol[:, HF * h + c:HF * h + c + 1].to_broadcast([P, T]),
                                         k32[:, HF * h + c, :], wkv[:, 0, c, 0:1], ALU.add, ALU.max).then_inc(mix_dve.sem, 1)
                dve.wait_ge(*mix_dve.done(t, f"pp_{h}"))
                for c in range(HF):
                    V.scalar_tensor_tensor(out=zz[:, c, :], in0=k32[:, HF * h + c, :], scalar=ucol[:, HF * h + c:HF * h + c + 1],
                                           in1=wkv[:, 0, c, 0:T], op0=ALU.add, op1=ALU.subtract).then_inc(mix_dve.sem, 1)
                dve.wait_ge(*mix_dve.done(t, f"z_{h}"))
                V.tensor_scalar(zz[:, :, :], zz[:, :, :], ZMAX, None, ALU.min).then_inc(mix_dve.sem, 1)

            def scan(h, n, src):
                for c in range(HF):
                    V.tensor_tensor_scan(wkv[:, n, c, 1:T + 1], e1[:, c, :], src[:, c, :], wkv[:, n, c, 0:1],
                                         ALU.mult, ALU.add).then_inc(mix_dve.sem, 1)

            def mix_sum(t, h):
                dve.wait_ge(*mix_act.done(t, f"e2_{h}"))
                scan(h, 2, e2)

            def mix_scan(t, h):
                dve.wait_ge(*mix_act.done(t, "v", h))
                V.tensor_tensor(ev[:, :, :], e2[:, :, :], v32[:, HF * h:HF * h + HF, :], ALU.mult).then_inc(mix_dve.sem, 1)
                dve.wait_ge(*mix_dve.done(t, f"ev_{h}"))
                scan(h, 1, ev)

            def mix_num(t, h):
                vh = v32[:, HF * h:HF * h + HF, :]
                prev_a, prev_b = wkv[:, 1, :, 0:T], wkv[:, 2, :, 0:T]
                dve.wait_ge(*mix_dve.done(t, f"a_{h}"))
                V.tensor_copy(carry[t.par][:, :, HF * h:HF * h + HF], wkv[:, :, :, T]).then_inc(mix_dve.sem, 1)
                V.tensor_tensor(e2[:, :, :], prev_b, vh, ALU.mult).then_inc(mix_dve.sem, 1)
                dve.wait_ge(*mix_dve.done(t, f"bv_{h}"))
                V.tensor_tensor(e2[:, :, :], prev_a, e2[:, :, :], ALU.subtract).then_inc(mix_dve.sem, 1)

            def mix_rec(t, n):
                h, c = n // HF, n % HF
                dve.wait_ge(*mix_pool.done(t, f"den_{h}"))
                V.reciprocal(zz[:, c, :], zz[:, c, :]).then_inc(mix_dve.sem, 1)

            def mix_gate(t, h):
                vh = v32[:, HF * h:HF * h + HF, :]
                dve.wait_ge(*mix_dve.done(t, f"num_{h}"))
                V.tensor_tensor(e2[:, :, :], e2[:, :, :], zz[:, :, :], ALU.mult).then_inc(mix_dve.sem, 1)
                dve.wait_ge(*mix_dve.done(t, f"frac_{h}"))
                V.tensor_tensor(e2[:, :, :], e2[:, :, :], vh, ALU.add).then_inc(mix_dve.sem, 1)
                dve.wait_ge(*mix_dve.done(t, f"y_{h}"))
                dve.wait_ge(*mix_act.done(t, f"th_{h}"))
                V.scalar_tensor_tensor(out=e2[:, :, :], in0=e1[:, :, :], scalar=1.0, in1=e2[:, :, :],
                                       op0=ALU.add, op1=ALU.mult).then_inc(mix_dve.sem, 1)

            def mix_split(t, h):
                dve.wait_ge(*mix_act.done(t, f"o_hi_{h}"))
                lo(xo16[:, 1, HF * h:HF * h + HF, :], e2[:, :, :], colof["o_hi"], xo16[:, 0, HF * h:HF * h + HF, :])\
                    .then_inc(mix_dve.sem, 1)

            def mix_project(t, _):
                dve.wait_ge(*res_in.done(t, "x"))
                for s in range(SUB):
                    dve.wait_ge(*mix_pe.done(t, "O", s))
                    V.scalar_tensor_tensor(out=x1[t.par][:, s, :], in0=mix_bank[s][:, :], scalar=colof["o"],
                                           in1=x1[t.par][:, s, :], op0=ALU.mult, op1=ALU.add).then_inc(mix_dve.sem, 1)

            def att_stats(t, _):
                xa = x1[t.par]
                for s in range(SUB):
                    dve.wait_ge(*mix_dve.done(t, "x1", s))
                    V.bn_stats(st2[:, s, :], xa[:, s, :]).then_inc(att_dve.sem, 1)
                dve.wait_ge(*att_dve.done(t, "stats"))
                V.memset(idle[:, :], 0.0).then_inc(att_dve.sem, 1)
                for s in range(SUB):
                    V.bn_aggr(mv2[:, s, :], st2[:, s, :]).then_inc(att_dve.sem, 1)
                dve.wait_ge(*att_dve.done(t, "aggr"))
                V.tensor_scalar(var2[:, 0, :], mv2[:, :, 1], LN_EPS, None, ALU.add).then_inc(att_dve.sem, 1)
                V.tensor_scalar(var2[:, 1, :], mv2[:, :, 1], 1.0 + RMS_EPS, LN_EPS * RMS_EPS, ALU.mult, ALU.add).then_inc(att_dve.sem, 1)

            def att_norm(t, _):
                xa = x1[t.par]
                dve.wait_ge(*att_pool.done(t, "rstd"))
                for s in range(SUB):
                    V.tensor_scalar(h_rows[:, s, :], xa[:, s, :], mv2[:, s, 0:1], rs2[:, 1, s:s + 1],
                                    ALU.subtract, ALU.mult).then_inc(att_dve.sem, 1)

            def att_rest(t, _):
                xa = x1[t.par]
                if t.back(1):
                    dve.wait_ge(*acc_pool.done(t.back(1), "acc"))
                for s in range(SUB):
                    V.tensor_scalar(x2[:, s, :], xa[:, s, :], mv2[:, s, 0:1], rs2[:, 0, s:s + 1],
                                    ALU.subtract, ALU.mult).then_inc(att_dve.sem, 1)

            def att_turn(t, _):
                for b in range(2):
                    dve.wait_ge(*att_act.done(t, "h_hi", b))
                    lo(ht16[:, 1, 2 * b:2 * b + 2, :], att_bank[ATT_BANK["T", b]][:, :], XS, ht16[:, 0, 2 * b:2 * b + 2, :])\
                        .then_inc(att_dve.sem, 1)

            def att_latent(t, _):
                dve.wait_ge(*att_act.done(t, "c"))
                V.tensor_tensor(c16[LAT:2 * LAT, :], c32[LAT:2 * LAT, :], c16[LAT:2 * LAT, :], ALU.subtract).then_inc(att_dve.sem, 1)

            def att_up(t, _):
                for b in range(CB):
                    dve.wait_ge(*att_pe.done(t, f"V{b // 2}"))
                    V.tensor_scalar(va32[:, b, :], att_bank[ATT_BANK["V", b // 2]][:, (b % 2) * T:(b % 2) * T + T],
                                    colof["vv"], bvcol[:, b:b + 1], ALU.mult, ALU.add).then_inc(att_dve.sem, 1)

            def att_stack(t, _):
                dve.wait_ge(*att_act.done(t, "k"))
                for f in range(4):
                    for n in (0, 2):
                        V.tensor_copy(ks[n * HD:(n + 1) * HD, f * CB:(f + 1) * CB, :],
                                      k16[f * HD:(f + 1) * HD, 0]).then_inc(att_dve.sem, 1)

            def att_vt(t, _):
                dve.wait_ge(*att_dve.done(t, "v"))
                V.transpose(vp[:, :, 0:HD], va32[:, :, :].rearrange("p b (j g) -> p g (b j)", g=G)).then_inc(att_dve.sem, 1)

            def att_max(t, n):
                for k in range(2 * n, 2 * n + 2):
                    dve.wait_ge(*att_pe.done(t, f"M{k}"))
                    V.tensor_reduce(mcol[:, 4 * k:4 * k + 4], att_bank[ATT_BANK["M", k]][:, :].rearrange("p (g x) -> p g x", g=4),
                                    AX, ALU.max).then_inc(att_dve.sem, 1)

            def att_m(t, _):
                dve.wait_ge(*att_dve.done(t, "smax"))
                V.tensor_scalar(m16[:, 0, :], mcol[:, :], -2.0 ** -14, None, ALU.mult).then_inc(att_dve.sem, 1)
                dve.wait_ge(*att_dve.done(t, "m_hi"))
                lo(m16[:, 1, :], mcol[:, :], -2.0 ** -14, m16[:, 0, :]).then_inc(att_dve.sem, 1)

            def att_probs(t, k):
                pv = att_bank[ATT_BANK["PV", k]][:, 0:4 * (HD + 1)].rearrange("p (g d) -> p g d", g=4)
                dve.wait_ge(*att_pe.done(t, f"PV{k}"))
                V.reciprocal(rden[:, 4 * k:4 * k + 4], pv[:, :, HD]).then_inc(att_dve.sem, 1)
                dve.wait_ge(*att_dve.done(t, "norm", 2 * k))
                V.tensor_tensor(on[:, 4 * k:4 * k + 4, :], pv[:, :, 0:HD],
                                rden[:, 4 * k:4 * k + 4].unsqueeze(2).to_broadcast([P, 4, HD]), ALU.mult).then_inc(att_dve.sem, 1)

            def att_back(t, _):
                dve.wait_ge(*att_dve.done(t, "norm"))
                V.transpose(ot32.rearrange("p b (j g) -> p g (b j)", g=G), on[:, :, :]).then_inc(att_dve.sem, 1)
                for h in range(2):
                    dve.wait_ge(*att_act.done(t, "ot_hi", h))
                    lo(qo16[:, 1, HF * h:HF * h + HF, :], ot32[:, HF * h:HF * h + HF, :], colof["ot_hi"],
                       qo16[:, 0, HF * h:HF * h + HF, :]).then_inc(att_dve.sem, 1)

            def att_project(t, _):
                for s in range(SUB):
                    dve.wait_ge(*att_pe.done(t, f"O{s}"))
                    dve.wait_ge(*att_pool.done(t, "xb", s))
                    V.scalar_tensor_tensor(out=x2[:, s, :], in0=att_bank[ATT_BANK["O", s]][:, :], scalar=colof["x2"],
                                           in1=x2[:, s, :], op0=ALU.mult, op1=ALU.add).then_inc(att_dve.sem, 1)

            def att_norm2(t, _):
                dve.wait_ge(*att_pool.done(t, "rms"))
                for s in range(SUB):
                    V.tensor_scalar(h_rows[:, s, :], x2[:, s, :], rs3[:, s:s + 1], None, ALU.mult).then_inc(att_dve.sem, 1)

            def att_turn2(t, _):
                for b in range(2):
                    dve.wait_ge(*att_act.done(t, "h2_hi", b))
                    lo(h2t[:, 1, 2 * b:2 * b + 2, :], att_bank[ATT_BANK["T2", b]][:, :], XS, h2t[:, 0, 2 * b:2 * b + 2, :])\
                        .then_inc(att_dve.sem, 1)

            def moe_gate(t, _):
                def bcast(a):
                    return a[:, :].unsqueeze(2).to_broadcast([P, SUB, E])

                dve.wait_ge(*att_pe.done(t, "G0"))
                V.scalar_tensor_tensor(out=gl[:, :, :].rearrange("p s e -> p (s e)"), in0=att_bank[ATT_BANK["G", 0]][:, 0:SUB * E],
                                       scalar=colof["g"], in1=bg_row[:, :, :].rearrange("p s e -> p (s e)"),
                                       op0=ALU.mult, op1=ALU.add).then_inc(gate_dve.sem, 1)
                dve.wait_ge(*gate_dve.done(t, "gl"))
                V.tensor_reduce(gmx[:, :], gl[:, :, :], AX, ALU.max).then_inc(gate_dve.sem, 1)
                dve.wait_ge(*gate_dve.done(t, "gmax"))
                V.tensor_tensor(gl[:, :, :], gl[:, :, :], bcast(gmx), ALU.subtract).then_inc(gate_dve.sem, 1)
                dve.wait_ge(*gate_act.done(t, "ge"))
                V.tensor_reduce(gsum[:, :], gl[:, :, :], AX, ALU.add).then_inc(gate_dve.sem, 1)
                dve.wait_ge(*gate_dve.done(t, "gsum"))
                V.reciprocal(gmx[:, :], gsum[:, :]).then_inc(gate_dve.sem, 1)
                dve.wait_ge(*gate_dve.done(t, "grec"))
                V.tensor_tensor(gl[:, :, :], gl[:, :, :], bcast(gmx), ALU.mult).then_inc(gate_dve.sem, 1)
                dve.wait_ge(*gate_dve.done(t, "gmul"))
                V.tensor_tensor(gates[:, :, :], gl[:, :, :], ee[:, :, :], ALU.mult).then_inc(gate_dve.sem, 1)

            def moe(t, u):
                e, s = u // SUB, u % SUB
                if u == 0:
                    dve.wait_ge(*acc_pool.done(t, "acc"))
                    dve.wait_ge(*gate_dve.done(t, "gates"))
                if u >= SUB:
                    dve.wait_ge(*moe_dve.done(t, "u", u - SUB))
                dve.wait_ge(*moe_pe.done(t, "u", u))
                V.scalar_tensor_tensor(out=acc[:, s, :], in0=moe_bank[u % 2][:, :], scalar=gates[:, s, e:e + 1],
                                       in1=acc[:, s, :], op0=ALU.mult, op1=ALU.add).then_inc(moe_dve.sem, 1)

            pipeline(dve, {"pre_stats": pre_stats, "pre_norm": pre_norm, "mix_turn": mix_turn, "mix_decay": mix_decay, "mix_sum": mix_sum, "mix_scan": mix_scan,
                           "mix_num": mix_num, "mix_rec": mix_rec, "mix_gate": mix_gate, "mix_split": mix_split,
                           "mix_project": mix_project, "att_stats": att_stats, "att_norm": att_norm,
                           "att_rest": att_rest, "att_turn": att_turn, "att_latent": att_latent, "att_up": att_up, "att_stack": att_stack, "att_vt": att_vt, "att_max": att_max,
                           "att_m": att_m, "att_probs": att_probs, "att_back": att_back,
                           "att_project": att_project, "att_norm2": att_norm2, "att_turn2": att_turn2,
                           "moe_gate": moe_gate, "moe": moe}, split)

        @block.tensor
        def _(pe):
            PASSES = ((0, 0), (1, 0), (0, 1))

            def product(dst, blocks):
                last = len(blocks) * len(PASSES) - 1
                n = 0
                for left, right in blocks:
                    for a, b in PASSES:
                        ins = nc.tensor.matmul(dst, left(a), right(b), start=(n == 0), stop=(n == last))
                        n += 1
                return ins

            def split_block(n):
                name, b = SPLITS[n]
                if b == 0:
                    pe.wait_ge(weight_in[name], 16)
                if n >= 2:
                    pe.wait_ge(lo_done, n - 1)
                for r in range(CB):
                    ins = nc.tensor.transpose(turned(n)[:, r * P:(r + 1) * P], f32_block(name, r)[:, b * P:(b + 1) * P], ident[:, :])
                ins.then_inc(turn_done, 1)

            def split(i, k):
                for name, b in splits_in(i, k):
                    if name in TURNED:
                        split_block(SPLITS.index((name, b)))

            pe.wait_ge(const_in, 16 * CONSTS)
            for n in range(2 * CB):
                split_block(n)

            def turn(rows_, banks, steps, sem_, waits):
                for b in range(2):
                    waits(b)
                    for c in range(2):
                        for s in range(SUB):
                            ins = nc.tensor.transpose(banks[b][:, c * T + s * P:c * T + (s + 1) * P],
                                                      rows_[:, s, (2 * b + c) * P:(2 * b + c + 1) * P], ident[:, :])
                    ins.then_inc(sem_, 1)

            def mix_free(t, use, k):
                before = {"T": ("O", True), "K": ("T", False), "V": ("K", False), "O": ("V", False)}[use]
                steps, step, n = mix_reader(before[0], k)
                if not before[1]:
                    pe.wait_ge(*steps.done(t, step, n))
                elif t.back(1):
                    pe.wait_ge(*steps.done(t.back(1), step, n))

            def att_free(t, use, k):
                (before, n), earlier = att_before((use, k))
                steps, step, m = att_reader(before, n)
                if not earlier:
                    pe.wait_ge(*steps.done(t, step, m))
                elif t.back(1):
                    pe.wait_ge(*steps.done(t.back(1), step, m))

            def channel(dst, name, blk, src, width=P):
                return product(dst, [(lambda a, kb=kb: w16[name][:, a, kb, blk * width:(blk + 1) * width],
                                      lambda b, kb=kb: src[:, b, kb, :]) for kb in range(CB)])

            def token(dst, name, s, src):
                return product(dst, [(lambda a, kb=kb: src[:, a, kb, s * P:(s + 1) * P],
                                      lambda b, kb=kb: w16[name][:, b, kb, :]) for kb in range(CB)])

            def mix_turn(t, _):
                pe.wait_ge(*pre_dve.done(t, "norm"))
                turn(xk_rows, mix_bank, mix_pe, mix_pe.sem, lambda b: mix_free(t, "T", b))

            def mix_in(t, use, name):
                for b in range(2):
                    mix_free(t, use, b)
                    for c in range(2):
                        ins = channel(mix_bank[b][:, c * T:(c + 1) * T], name, 2 * b + c, xo16)
                    ins.then_inc(mix_pe.sem, 1)

            def mix_k(t, _):
                pe.wait_ge(*mix_dve.done(t, "x_lo"))
                if not t.back(1):
                    pe.wait_ge(lo_done, split_done("r"))
                mix_in(t, "K", "k")

            def mix_v(t, _):
                mix_in(t, "V", "r")

            def mix_project(t, _):
                pe.wait_ge(*mix_dve.done(t, "o_lo_1"))
                if not t.back(1):
                    pe.wait_ge(lo_done, split_done("o1"))
                for s in range(SUB):
                    mix_free(t, "O", s)
                    token(mix_bank[s][:, :], "o1", s, xo16).then_inc(mix_pe.sem, 1)

            def att_turn(t, _):
                pe.wait_ge(*att_dve.done(t, "h"))
                turn(h_rows, [att_bank[ATT_BANK["T", b]] for b in range(2)], att_pe, att_pe.sem, lambda b: att_free(t, "T", b))

            def att_latent(t, _):
                pe.wait_ge(*att_dve.done(t, "h_lo"))
                if not t.back(1):
                    pe.wait_ge(lo_done, split_done("u"))
                att_free(t, "D", 0)
                channel(att_bank[ATT_BANK["D", 0]][:, 0:T], "d", 0, ht16).then_inc(att_pe.sem, 1)

            def att_q(t, _):
                for b in range(2):
                    att_free(t, "Q", b)
                    for c in range(2):
                        ins = channel(att_bank[ATT_BANK["Q", b]][:, c * T:(c + 1) * T], "q", 2 * b + c, ht16)
                    ins.then_inc(att_pe.sem, 1)

            def att_up(t, _):
                pe.wait_ge(*att_dve.done(t, "c_lo"))
                for n, use in enumerate("KV"):
                    for b in range(2):
                        att_free(t, use, b)
                        for c in range(2):
                            blk = n * CB + 2 * b + c
                            for a in range(2):
                                ins = nc.tensor.matmul(att_bank[ATT_BANK[use, b]][:, c * T:(c + 1) * T],
                                                       w16["u"][:, a, blk * P:(blk + 1) * P], c16[:, :], start=(a == 0), stop=(a == 1))
                        ins.then_inc(att_pe.sem, 1)

            def group(stacked, n_rows, g):
                return stacked[0:n_rows, :, :].rearrange("p h (j g) -> p g (h j)", j=NJ)[:, g]

            def att_max(t, n):
                if n == 0:
                    pe.wait_ge(*stack_in.done(t, "qk"))
                    pe.wait_ge(*att_dve.done(t, "stack"))
                    if not t.back(1):
                        pe.wait_ge(masks_in, 32)
                for k in range(2 * n, 2 * n + 2):
                    att_free(t, "M", k)
                    for n in range(4):
                        ins = nc.tensor.matmul(att_bank[ATT_BANK["M", k]][:, n * P:(n + 1) * P],
                                               group(qs, SCAN_ROWS, 4 * k + n), group(ks, SCAN_ROWS, 4 * k + n), start=True, stop=True)
                    ins.then_inc(att_pe.sem, 1)

            def att_scores(t, k):
                if k == 0:
                    pe.wait_ge(*m_in.done(t, "m"))
                att_free(t, "S", k)
                for n in range(4):
                    ins = nc.tensor.matmul(att_bank[ATT_BANK["S", k]][:, n * P:(n + 1) * P],
                                           group(ks, SCAN_ROWS + 2, 4 * k + n), group(qs, SCAN_ROWS + 2, 4 * k + n), start=True, stop=True)
                ins.then_inc(att_pe.sem, 1)

            def att_probs(t, k):
                if k == 0:
                    pe.wait_ge(*att_dve.done(t, "vt"))
                att_free(t, "PV", k)
                pe.wait_ge(*att_act.done(t, "ex", k))
                for n in range(4):
                    ins = nc.tensor.matmul(att_bank[ATT_BANK["PV", k]][:, n * (HD + 1):(n + 1) * (HD + 1)],
                                           pr[:, k % 2, n * P:(n + 1) * P], vp[:, 4 * k + n, :], start=True, stop=True)
                ins.then_inc(att_pe.sem, 1)

            def att_project(t, _):
                pe.wait_ge(*att_dve.done(t, "ot_lo"))
                for s in range(SUB):
                    att_free(t, "O", s)
                    token(att_bank[ATT_BANK["O", s]][:, :], "o2", s, qo16).then_inc(att_pe.sem, 1)

            def att_turn2(t, _):
                pe.wait_ge(*att_dve.done(t, "h2"))
                turn(h_rows, [att_bank[ATT_BANK["T2", b]] for b in range(2)], att_pe, att_pe.sem, lambda b: att_free(t, "T2", b))

            def att_gate(t, _):
                pe.wait_ge(*att_dve.done(t, "h2_lo"))
                att_free(t, "G", 0)
                for s in range(SUB):
                    ins = token(att_bank[ATT_BANK["G", 0]][:, s * E:(s + 1) * E], "g", s, h2t)
                ins.then_inc(att_pe.sem, 1)

            def moe(t, u):
                if u >= 2:
                    pe.wait_ge(*moe_dve.done(t, "u", u - 2))
                elif t.back(1):
                    pe.wait_ge(*moe_dve.done(t.back(1), "u", 2 * E - 2 + u))
                elif u == 0:
                    pe.wait_ge(lo_done, len(SPLITS))
                token(moe_bank[u % 2][:, :], f"e{u // SUB}", u % SUB, h2t).then_inc(moe_pe.sem, 1)

            pipeline(pe, {"mix_turn": mix_turn, "mix_k": mix_k, "mix_v": mix_v, "mix_project": mix_project,
                          "att_turn": att_turn, "att_latent": att_latent, "att_q": att_q, "att_up": att_up, "att_max": att_max, "att_scores": att_scores, "att_probs": att_probs,
                          "att_project": att_project, "att_turn2": att_turn2,
                          "att_gate": att_gate, "moe": moe}, split)


CONSTS = 1 + 5 + 8 + 2 + 1 + SUB
MAX_DONE = 7
MAXES = MAX_DONE + 5 + 7 + 3 + 1
SCALES = MAXES + 10 + 8 + 3 + 12 + 3 + 4 + 1
EXPERT_MAXES = SCALES + E + 1 + E + 1
SET_DVE = EXPERT_MAXES + 3 + 2 * E + SUB


def masks():
    j = np.arange(T) // G
    same = (j[None, :] == np.arange(NJ)[:, None]).astype(np.float16)
    km = np.repeat((same * np.float16(2.0 ** 15))[:, None, :], H, axis=1).reshape(NJ, H * T)
    qm = np.repeat(((1 - same) * np.float16(-65504.0))[:, None, :], H, axis=1).reshape(NJ, H * T)
    km = np.concatenate([km, np.full((2, H * T), 2.0 ** 14, np.float16)])
    return np.ascontiguousarray(km), np.ascontiguousarray(qm)


_INS = ["attn_x", "attn_Wk", "attn_Wr", "attn_Wo", "attn_time_decay", "attn_time_first", "ffn_gamma1",
        "ffn_Wq", "ffn_bq", "ffn_Wdown", "ffn_bdown", "ffn_Wup", "ffn_bup", "ffn_Wo", "ffn_bo",
        "ffn_gamma2", "ffn_Wg", "ffn_bg", "ffn_We"]


def kernel(**inputs):
    import concourse.bacc as bacc
    from concourse.bass_utils import run_bass_kernel_spmd

    nc = bacc.Bacc("TRN2", target_bir_lowering=False, num_devices=1)
    arrays = {f"in_{n}": np.ascontiguousarray(inputs[f"L0_{n}"]) for n in _INS}
    arrays["in_ident"] = np.eye(P, dtype=np.float32)
    arrays["in_kmask"], arrays["in_qmask"] = masks()
    args = [nc.dram_tensor(n, a.shape, mybir.dt.from_np(a.dtype), kind="ExternalInput").ap() for n, a in arrays.items()]
    out = nc.dram_tensor("result", (B, L, C), F32, kind="ExternalOutput").ap()
    build(nc, *args, out)
    r = run_bass_kernel_spmd(nc, [arrays], core_ids=[0])
    return r.results[0]["result"]
```
